# Optimizing a Trainium2 kernel written in Bass

```python
import numpy as np
import jax
import jax.numpy as jnp

def _softmax(x, axis=-1):
    return jax.nn.softmax(x, axis=axis)

def _gelu(x):
    return jax.nn.gelu(x, approximate=True)

def _silu(x):
    return jax.nn.silu(x)

def _sigmoid(x):
    return jax.nn.sigmoid(x)

def _layernorm(x, axis=-1, eps=1e-05):
    m = jnp.mean(x, axis=axis, keepdims=True)
    v = jnp.var(x, axis=axis, keepdims=True)
    return (x - m) / jnp.sqrt(v + eps)

def _scatter_add(tgt, idx, src, axis=0):
    return tgt.at[idx].add(src)

def _segment_sum(src, seg, n):
    return jax.ops.segment_sum(src, seg, n)
kernel_name = 'mk_decoder_preln_d2_seqx_r8_41af83'

def setup_inputs(seed: int=0):
    np.random.seed(seed)
    _w = jnp.asarray

    def _rec_inputs():
        import jax
        import jax.numpy as jnp
        _rk = jax.random.key(seed)
        x = -0.0003929 + 0.9999 * jax.random.normal(jax.random.fold_in(_rk, 1), (16, 128, 256), jnp.float32)
        _lenS = 128 - jax.random.randint(jax.random.fold_in(_rk, 7), (16,), 0, max(1, 128 // 4) + 1, jnp.int32)
        _lenS2 = 128 - jax.random.randint(jax.random.fold_in(_rk, 8), (16,), 0, max(1, 128 // 4) + 1, jnp.int32)
        _ctx_2048P = jax.random.normal(jax.random.fold_in(_rk, 11), (16, 16, 256), jnp.float32)
        _ctx_2048c = jax.random.dirichlet(jax.random.fold_in(_rk, 511), 0.3 * jnp.ones((16,), jnp.float32), (16, 128))
        _ctx_2048t = jnp.einsum('bsk,bkd->bsd', _ctx_2048c, _ctx_2048P)
        _ctx_2048t = _ctx_2048t * jax.lax.rsqrt(jnp.mean(jnp.square(_ctx_2048t)) + 1e-12) * 0.953939
        ctx_2048 = -0.000514642 + 1.00011 * (_ctx_2048t + 0.3 * jax.random.normal(jax.random.fold_in(_rk, 611), (16, 128, 256), jnp.float32))
        return (x, ctx_2048)
    x, ctx_2048 = _rec_inputs()

    def _L0_attn_setup():
        import jax, jax.numpy as jnp
        import numpy as np
        EMBED_DIM = 256
        NUM_HEADS = 32
        HEAD_DIM = EMBED_DIM // NUM_HEADS
        BATCH = 2
        SEQ_LEN = 256
        key = jax.random.key(seed)
        ks = jax.random.split(key, 5)
        scale = 1.0 / np.sqrt(EMBED_DIM)
        x = jax.random.normal(ks[0], (BATCH, SEQ_LEN, EMBED_DIM), dtype=jnp.float32)
        Wq = jax.random.normal(ks[1], (EMBED_DIM, EMBED_DIM), dtype=jnp.float32) * scale
        Wk = jax.random.normal(ks[2], (EMBED_DIM, EMBED_DIM), dtype=jnp.float32) * scale
        Wv = jax.random.normal(ks[3], (EMBED_DIM, EMBED_DIM), dtype=jnp.float32) * scale
        Wo = jax.random.normal(ks[4], (EMBED_DIM, EMBED_DIM), dtype=jnp.float32) * scale
        return {'x': x, 'Wq': Wq, 'Wk': Wk, 'Wv': Wv, 'Wo': Wo}
    _L0_attn_all = _L0_attn_setup()
    _L0_attn_in = {k: v for k, v in _L0_attn_all.items() if k in ('Wq', 'Wk', 'Wv', 'Wo')}
    del _L0_attn_all

    def _L0_xattn_setup():
        import jax, jax.numpy as jnp
        import numpy as np
        DIM = 256
        NHEADS = 32
        HEAD_DIM = DIM // NHEADS
        EPS = 1e-06

        def _rmsnorm(t):
            return t * jax.lax.rsqrt(jnp.mean(t * t, axis=-1, keepdims=True) + EPS)
        key = jax.random.key(seed)
        kx, kc, kq, kk, kv = jax.random.split(key, 5)
        x = jax.random.normal(kx, (2, 512, DIM), dtype=jnp.float32)
        context = jax.random.normal(kc, (2, 64, DIM), dtype=jnp.float32)
        std = 0.02
        Wq = jax.random.normal(kq, (DIM, DIM), dtype=jnp.float32) * std
        Wk = jax.random.normal(kk, (DIM, DIM), dtype=jnp.float32) * std
        Wv = jax.random.normal(kv, (DIM, DIM), dtype=jnp.float32) * std
        return {'x': x, 'context': context, 'Wq': Wq, 'Wk': Wk, 'Wv': Wv}
    _L0_xattn_all = _L0_xattn_setup()
    _L0_xattn_in = {k: v for k, v in _L0_xattn_all.items() if k in ('Wq', 'Wk', 'Wv')}
    del _L0_xattn_all

    def _L0_ffn_setup():
        import jax, jax.numpy as jnp
        import numpy as np
        Q_MAX = 127.0

        def _ste_round(x):
            return x + jax.lax.stop_gradient(jnp.round(x) - x)
        key = jax.random.key(seed)
        k1, k2 = jax.random.split(key)
        B, S, D_IN, D_OUT = (4, 512, 256, 256)
        x = jax.random.normal(k1, (B, S, D_IN), dtype=jnp.float32)
        weight = jax.random.normal(k2, (D_OUT, D_IN), dtype=jnp.float32) / np.sqrt(D_IN)
        return {'x': x, 'weight': weight}
    _L0_ffn_all = _L0_ffn_setup()
    _L0_ffn_in = {k: v for k, v in _L0_ffn_all.items() if k in ('weight',)}
    del _L0_ffn_all

    def _L1_attn_setup():
        import jax, jax.numpy as jnp
        import numpy as np
        EMBED = 256
        HEADS = 16
        HEAD_DIM = EMBED // HEADS
        CHUNK = 128
        BASE = 10000.0
        EPS = 1e-06

        def _alibi_log_decay(h):
            slopes = 2.0 ** (-8.0 * (jnp.arange(h, dtype=jnp.float32) + 1.0) / h)
            return -slopes

        def _lrpe_rotate(x):
            b, n, h, d = x.shape
            half = d // 2
            theta = BASE ** (-2.0 * jnp.arange(half, dtype=jnp.float32) / d)
            ang = jnp.arange(n, dtype=jnp.float32)[:, None] * theta[None, :]
            cos = jnp.cos(ang)[None, :, None, :]
            sin = jnp.sin(ang)[None, :, None, :]
            x1, x2 = (x[..., :half], x[..., half:])
            return jnp.concatenate([x1 * cos - x2 * sin, x1 * sin + x2 * cos], axis=-1)

        def _lightning_attn(q, k, v, log_lam):
            b, n, h, d = q.shape
            C = CHUNK
            nc = n // C
            qc = q.reshape(b, nc, C, h, d).transpose(1, 0, 2, 3, 4)
            kc = k.reshape(b, nc, C, h, d).transpose(1, 0, 2, 3, 4)
            vc = v.reshape(b, nc, C, h, d).transpose(1, 0, 2, 3, 4)
            i = jnp.arange(C, dtype=jnp.float32)
            diff = i[:, None] - i[None, :]
            D = jnp.where(diff[None] >= 0, jnp.exp(log_lam[:, None, None] * diff[None]), 0.0)
            decay_q = jnp.exp(log_lam[None, :] * (i[:, None] + 1.0))
            decay_k = jnp.exp(log_lam[None, :] * (C - 1.0 - i[:, None]))
            lam_C = jnp.exp(log_lam * C)

            def step(S, qkv):
                qi, ki, vi = qkv
                scores = jnp.einsum('bthd,bshd->bhts', qi, ki) * D[None]
                o_intra = jnp.einsum('bhts,bshd->bthd', scores, vi)
                o_inter = jnp.einsum('bthd,bhde->bthe', qi * decay_q[None, :, :, None], S)
                S_new = lam_C[None, :, None, None] * S + jnp.einsum('bshd,bshe->bhde', ki * decay_k[None, :, :, None], vi)
                return (S_new, o_intra + o_inter)
            S0 = jnp.zeros((b, h, d, d), q.dtype)
            _, o = jax.lax.scan(step, S0, (qc, kc, vc))
            return o.transpose(1, 0, 2, 3, 4).reshape(b, n, h, d)

        def _gated_group_rmsnorm(o, gate, weight):
            b, n, d = o.shape
            x = o * jax.nn.sigmoid(gate)
            xg = x.reshape(b, n, HEADS, HEAD_DIM)
            ms = jnp.mean(xg * xg, axis=-1, keepdims=True)
            xg = xg * jax.lax.rsqrt(ms + EPS)
            return xg.reshape(b, n, d) * weight
        key = jax.random.key(seed)
        ks = jax.random.split(key, 8)
        b, n, d = (2, 256, EMBED)
        std = 0.02
        return {'x': jax.random.normal(ks[0], (b, n, d), jnp.float32), 'Wq': jax.random.normal(ks[1], (d, d), jnp.float32) * std, 'Wk': jax.random.normal(ks[2], (d, d), jnp.float32) * std, 'Wv': jax.random.normal(ks[3], (d, d), jnp.float32) * std, 'Wo': jax.random.normal(ks[4], (d, d), jnp.float32) * std, 'Wg1': jax.random.normal(ks[5], (d, HEAD_DIM), jnp.float32) * std, 'Wg2': jax.random.normal(ks[6], (HEAD_DIM, d), jnp.float32) * std, 'norm_weight': jnp.ones((d,), jnp.float32)}
    _L1_attn_all = _L1_attn_setup()
    _L1_attn_in = {k: v for k, v in _L1_attn_all.items() if k in ('Wq', 'Wk', 'Wv', 'Wo', 'Wg1', 'Wg2', 'norm_weight')}
    del _L1_attn_all

    def _L1_xattn_setup():
        import jax, jax.numpy as jnp
        import numpy as np
        key = jax.random.key(seed)
        k1, k2, k3, k4, k5 = jax.random.split(key, 5)
        B, D_MODEL, L = (2, 128, 256)
        HEAD_DIM = 8
        H = D_MODEL // HEAD_DIM
        return {'k': jax.random.normal(k1, (B, D_MODEL, L), dtype=jnp.float32), 'v': jax.random.normal(k2, (B, D_MODEL, L), dtype=jnp.float32), 'q': jax.random.normal(k3, (B, D_MODEL, L), dtype=jnp.float32), 'ssm_kernel': jax.random.normal(k4, (H, L), dtype=jnp.float32), 'D': jax.random.normal(k5, (H,), dtype=jnp.float32), 'head_dim': HEAD_DIM}
    _L1_xattn_all = _L1_xattn_setup()
    _L1_xattn_in = {k: v for k, v in _L1_xattn_all.items() if k in ('ssm_kernel', 'D')}
    del _L1_xattn_all

    def _L1_ffn_setup():
        import jax, jax.numpy as jnp
        import numpy as np
        B, S, D = (2, 256, 256)
        H, KV, HD = (16, 4, 128)
        E, F, TOPK = (8, 512, 2)
        THETA = 1000000.0
        EPS = 1e-05

        def rmsnorm(x, w):
            var = jnp.mean(jnp.square(x), axis=-1, keepdims=True)
            return x * jax.lax.rsqrt(var + EPS) * w

        def rope_cos_sin(seq_len):
            inv_freq = 1.0 / THETA ** (jnp.arange(0, HD, 2, dtype=jnp.float32) / HD)
            ang = jnp.arange(seq_len, dtype=jnp.float32)[:, None] * inv_freq[None, :]
            return (jnp.cos(ang)[None, :, None, :], jnp.sin(ang)[None, :, None, :])

        def apply_rope(x, cos, sin):
            x1, x2 = jnp.split(x, 2, axis=-1)
            return jnp.concatenate([x1 * cos - x2 * sin, x2 * cos + x1 * sin], axis=-1)

        def attention(x, wq, wk, wv, wo):
            b, s, _ = x.shape
            q = (x @ wq).reshape(b, s, H, HD)
            k = (x @ wk).reshape(b, s, KV, HD)
            v = (x @ wv).reshape(b, s, KV, HD)
            cos, sin = rope_cos_sin(s)
            q = apply_rope(q, cos, sin)
            k = apply_rope(k, cos, sin)
            rep = H // KV
            k = jnp.repeat(k, rep, axis=2)
            v = jnp.repeat(v, rep, axis=2)
            scores = jnp.einsum('bqhd,bkhd->bhqk', q, k) / np.sqrt(HD)
            causal = jnp.tril(jnp.ones((s, s), dtype=bool))
            scores = jnp.where(causal[None, None], scores, jnp.finfo(scores.dtype).min)
            probs = jax.nn.softmax(scores, axis=-1)
            out = jnp.einsum('bhqk,bkhd->bqhd', probs, v).reshape(b, s, H * HD)
            return out @ wo

        def moe(x, gate_w, w1, w3, w2):
            b, s, d = x.shape
            xt = x.reshape(b * s, d)
            logits = xt @ gate_w
            topv, topi = jax.lax.top_k(logits, TOPK)
            probs = jax.nn.softmax(topv, axis=-1)
            w = jnp.zeros_like(logits)
            for kk in range(TOPK):
                w = w + jax.nn.one_hot(topi[:, kk], E, dtype=logits.dtype) * probs[:, kk:kk + 1]
            out = jnp.zeros_like(xt)
            for e in range(E):
                h = jax.nn.silu(xt @ w1[e]) * (xt @ w3[e])
                out = out + w[:, e:e + 1] * (h @ w2[e])
            return out.reshape(b, s, d)
        key = jax.random.key(seed)
        ks = jax.random.split(key, 10)
        init = lambda k, shape: jax.random.normal(k, shape, jnp.float32) * 0.02
        return {'hidden_states': jax.random.normal(ks[0], (B, S, D), jnp.float32), 'norm1_w': jnp.ones((D,), jnp.float32), 'norm2_w': jnp.ones((D,), jnp.float32), 'wq': init(ks[1], (D, H * HD)), 'wk': init(ks[2], (D, KV * HD)), 'wv': init(ks[3], (D, KV * HD)), 'wo': init(ks[4], (H * HD, D)), 'gate_w': init(ks[5], (D, E)), 'w1': init(ks[6], (E, D, F)), 'w3': init(ks[7], (E, D, F)), 'w2': init(ks[8], (E, F, D))}
    _L1_ffn_all = _L1_ffn_setup()
    _L1_ffn_in = {k: v for k, v in _L1_ffn_all.items() if k in ('norm1_w', 'norm2_w', 'wq', 'wk', 'wv', 'wo', 'gate_w', 'w1', 'w3', 'w2')}
    del _L1_ffn_all
    return {'x': x, 'ctx_2048': ctx_2048, 'L0_attn_Wq': _L0_attn_in['Wq'], 'L0_attn_Wk': _L0_attn_in['Wk'], 'L0_attn_Wv': _L0_attn_in['Wv'], 'L0_attn_Wo': _L0_attn_in['Wo'], 'L0_xattn_Wq': _L0_xattn_in['Wq'], 'L0_xattn_Wk': _L0_xattn_in['Wk'], 'L0_xattn_Wv': _L0_xattn_in['Wv'], 'L0_ffn_weight': _L0_ffn_in['weight'], 'L1_attn_Wq': _L1_attn_in['Wq'], 'L1_attn_Wk': _L1_attn_in['Wk'], 'L1_attn_Wv': _L1_attn_in['Wv'], 'L1_attn_Wo': _L1_attn_in['Wo'], 'L1_attn_Wg1': _L1_attn_in['Wg1'], 'L1_attn_Wg2': _L1_attn_in['Wg2'], 'L1_attn_norm_weight': _L1_attn_in['norm_weight'], 'L1_xattn_ssm_kernel': _L1_xattn_in['ssm_kernel'], 'L1_xattn_D': _L1_xattn_in['D'], 'L1_ffn_norm1_w': _L1_ffn_in['norm1_w'], 'L1_ffn_norm2_w': _L1_ffn_in['norm2_w'], 'L1_ffn_wq': _L1_ffn_in['wq'], 'L1_ffn_wk': _L1_ffn_in['wk'], 'L1_ffn_wv': _L1_ffn_in['wv'], 'L1_ffn_wo': _L1_ffn_in['wo'], 'L1_ffn_gate_w': _L1_ffn_in['gate_w'], 'L1_ffn_w1': _L1_ffn_in['w1'], 'L1_ffn_w3': _L1_ffn_in['w3'], 'L1_ffn_w2': _L1_ffn_in['w2']}

def reference(x, ctx_2048, L0_attn_Wq, L0_attn_Wk, L0_attn_Wv, L0_attn_Wo, L0_xattn_Wq, L0_xattn_Wk, L0_xattn_Wv, L0_ffn_weight, L1_attn_Wq, L1_attn_Wk, L1_attn_Wv, L1_attn_Wo, L1_attn_Wg1, L1_attn_Wg2, L1_attn_norm_weight, L1_xattn_ssm_kernel, L1_xattn_D, L1_ffn_norm1_w, L1_ffn_norm2_w, L1_ffn_wq, L1_ffn_wk, L1_ffn_wv, L1_ffn_wo, L1_ffn_gate_w, L1_ffn_w1, L1_ffn_w3, L1_ffn_w2):
    import jax
    import jax.numpy as jnp

    def _L0_attn_ref(x, Wq, Wk, Wv, Wo):
        import jax, jax.numpy as jnp
        import numpy as np
        EMBED_DIM = 256
        NUM_HEADS = 32
        HEAD_DIM = EMBED_DIM // NUM_HEADS
        BATCH = 2
        SEQ_LEN = 256
        q = jnp.einsum('bse,ef->bsf', x, Wq)
        k = jnp.einsum('bse,ef->bsf', x, Wk)
        v = jnp.einsum('bse,ef->bsf', x, Wv)
        qT = jnp.swapaxes(q, 1, 2)
        kT = jnp.swapaxes(k, 1, 2)
        vT = jnp.swapaxes(v, 1, 2)
        attn_scores = jnp.einsum('bes,bfs->bef', qT, kT) / np.sqrt(HEAD_DIM)
        attn_weights = jax.nn.softmax(attn_scores, axis=-1)
        attn_output = jnp.einsum('bef,bfs->bes', attn_weights, vT)
        attn_output = jnp.swapaxes(attn_output, 1, 2)
        return jnp.einsum('bse,ef->bsf', attn_output, Wo)

    def _L0_xattn_ref(x, context, Wq, Wk, Wv):
        import jax, jax.numpy as jnp
        import numpy as np
        DIM = 256
        NHEADS = 32
        HEAD_DIM = DIM // NHEADS
        EPS = 1e-06

        def _rmsnorm(t):
            return t * jax.lax.rsqrt(jnp.mean(t * t, axis=-1, keepdims=True) + EPS)
        b, n, _ = x.shape
        m = context.shape[1]
        q = x @ Wq.T
        k_raw = context @ Wk.T
        v_raw = context @ Wv.T
        q = q.reshape(b, n, NHEADS, HEAD_DIM).transpose(0, 2, 1, 3)
        kv = jnp.concatenate([k_raw, v_raw], axis=-1)
        kv = kv.reshape(b, m, NHEADS, HEAD_DIM, 2)
        k = kv[..., 0].transpose(0, 2, 1, 3)
        v = kv[..., 1].transpose(0, 2, 1, 3)
        q = _rmsnorm(q)
        k = _rmsnorm(k)
        scale = HEAD_DIM ** (-0.5)
        scores = jnp.einsum('bhnd,bhmd->bhnm', q, k) * scale
        attn = jax.nn.softmax(scores, axis=-1)
        out = jnp.einsum('bhnm,bhmd->bhnd', attn, v)
        return out.transpose(0, 2, 1, 3).reshape(b, n, NHEADS * HEAD_DIM)

    def _L0_ffn_ref(x, weight):
        import jax, jax.numpy as jnp
        import numpy as np
        Q_MAX = 127.0

        def _ste_round(x):
            return x + jax.lax.stop_gradient(jnp.round(x) - x)
        w_scale = jnp.maximum(jnp.mean(jnp.abs(weight)), 1e-06)
        w_norm = weight / w_scale
        w_quant = jnp.clip(_ste_round(w_norm), -1.0, 1.0)
        a_scale = jnp.clip(jnp.max(jnp.abs(x), axis=-1, keepdims=True), 1e-08, None)
        x_quant = jnp.clip(_ste_round(x * (Q_MAX / a_scale)), -Q_MAX, Q_MAX)
        y = jnp.einsum('bsi,oi->bso', x_quant, w_quant)
        y = y * (w_scale * (a_scale / Q_MAX))
        return y

    def _L1_attn_ref(x, Wq, Wk, Wv, Wo, Wg1, Wg2, norm_weight):
        import jax, jax.numpy as jnp
        import numpy as np
        EMBED = 256
        HEADS = 16
        HEAD_DIM = EMBED // HEADS
        CHUNK = 128
        BASE = 10000.0
        EPS = 1e-06

        def _alibi_log_decay(h):
            slopes = 2.0 ** (-8.0 * (jnp.arange(h, dtype=jnp.float32) + 1.0) / h)
            return -slopes

        def _lrpe_rotate(x):
            b, n, h, d = x.shape
            half = d // 2
            theta = BASE ** (-2.0 * jnp.arange(half, dtype=jnp.float32) / d)
            ang = jnp.arange(n, dtype=jnp.float32)[:, None] * theta[None, :]
            cos = jnp.cos(ang)[None, :, None, :]
            sin = jnp.sin(ang)[None, :, None, :]
            x1, x2 = (x[..., :half], x[..., half:])
            return jnp.concatenate([x1 * cos - x2 * sin, x1 * sin + x2 * cos], axis=-1)

        def _lightning_attn(q, k, v, log_lam):
            b, n, h, d = q.shape
            C = CHUNK
            nc = n // C
            qc = q.reshape(b, nc, C, h, d).transpose(1, 0, 2, 3, 4)
            kc = k.reshape(b, nc, C, h, d).transpose(1, 0, 2, 3, 4)
            vc = v.reshape(b, nc, C, h, d).transpose(1, 0, 2, 3, 4)
            i = jnp.arange(C, dtype=jnp.float32)
            diff = i[:, None] - i[None, :]
            D = jnp.where(diff[None] >= 0, jnp.exp(log_lam[:, None, None] * diff[None]), 0.0)
            decay_q = jnp.exp(log_lam[None, :] * (i[:, None] + 1.0))
            decay_k = jnp.exp(log_lam[None, :] * (C - 1.0 - i[:, None]))
            lam_C = jnp.exp(log_lam * C)

            def step(S, qkv):
                qi, ki, vi = qkv
                scores = jnp.einsum('bthd,bshd->bhts', qi, ki) * D[None]
                o_intra = jnp.einsum('bhts,bshd->bthd', scores, vi)
                o_inter = jnp.einsum('bthd,bhde->bthe', qi * decay_q[None, :, :, None], S)
                S_new = lam_C[None, :, None, None] * S + jnp.einsum('bshd,bshe->bhde', ki * decay_k[None, :, :, None], vi)
                return (S_new, o_intra + o_inter)
            S0 = jnp.zeros((b, h, d, d), q.dtype)
            _, o = jax.lax.scan(step, S0, (qc, kc, vc))
            return o.transpose(1, 0, 2, 3, 4).reshape(b, n, h, d)

        def _gated_group_rmsnorm(o, gate, weight):
            b, n, d = o.shape
            x = o * jax.nn.sigmoid(gate)
            xg = x.reshape(b, n, HEADS, HEAD_DIM)
            ms = jnp.mean(xg * xg, axis=-1, keepdims=True)
            xg = xg * jax.lax.rsqrt(ms + EPS)
            return xg.reshape(b, n, d) * weight
        b, n, d = x.shape
        q = (x @ Wq).reshape(b, n, HEADS, HEAD_DIM)
        k = (x @ Wk).reshape(b, n, HEADS, HEAD_DIM)
        v = (x @ Wv).reshape(b, n, HEADS, HEAD_DIM)
        q = jax.nn.silu(q)
        k = jax.nn.silu(k)
        q = _lrpe_rotate(q)
        k = _lrpe_rotate(k)
        log_lam = _alibi_log_decay(HEADS)
        o = _lightning_attn(q, k, v, log_lam).reshape(b, n, d)
        gate = x @ Wg1 @ Wg2
        o = _gated_group_rmsnorm(o, gate, norm_weight)
        return o @ Wo

    def _L1_xattn_ref(k, v, q, ssm_kernel, D, head_dim):
        import jax, jax.numpy as jnp
        import numpy as np
        B, HD, L = k.shape
        H = HD // head_dim
        fft_size = 2 * L
        k_ = k.reshape(B, H, head_dim, L)
        v_ = v.reshape(B, H, head_dim, L)
        q_ = q.reshape(B, H, head_dim, L)
        kv = jnp.einsum('bhil,bhjl->bijhl', k_, v_)
        kv_f = jnp.fft.rfft(kv, n=fft_size)
        kernel_f = jnp.fft.rfft(ssm_kernel, n=fft_size)
        y = jnp.fft.irfft(kv_f * kernel_f, n=fft_size)[..., :L]
        out = y + kv * D[None, None, None, :, None]
        out = jnp.einsum('bijhl,bhil->bjhl', out, q_)
        out = jnp.transpose(out, (0, 2, 1, 3)).reshape(B, H * head_dim, L)
        return out.astype(k.dtype)

    def _L1_ffn_ref(hidden_states, norm1_w, norm2_w, wq, wk, wv, wo, gate_w, w1, w3, w2):
        import jax, jax.numpy as jnp
        import numpy as np
        B, S, D = (2, 256, 256)
        H, KV, HD = (16, 4, 128)
        E, F, TOPK = (8, 512, 2)
        THETA = 1000000.0
        EPS = 1e-05

        def rmsnorm(x, w):
            var = jnp.mean(jnp.square(x), axis=-1, keepdims=True)
            return x * jax.lax.rsqrt(var + EPS) * w

        def rope_cos_sin(seq_len):
            inv_freq = 1.0 / THETA ** (jnp.arange(0, HD, 2, dtype=jnp.float32) / HD)
            ang = jnp.arange(seq_len, dtype=jnp.float32)[:, None] * inv_freq[None, :]
            return (jnp.cos(ang)[None, :, None, :], jnp.sin(ang)[None, :, None, :])

        def apply_rope(x, cos, sin):
            x1, x2 = jnp.split(x, 2, axis=-1)
            return jnp.concatenate([x1 * cos - x2 * sin, x2 * cos + x1 * sin], axis=-1)

        def attention(x, wq, wk, wv, wo):
            b, s, _ = x.shape
            q = (x @ wq).reshape(b, s, H, HD)
            k = (x @ wk).reshape(b, s, KV, HD)
            v = (x @ wv).reshape(b, s, KV, HD)
            cos, sin = rope_cos_sin(s)
            q = apply_rope(q, cos, sin)
            k = apply_rope(k, cos, sin)
            rep = H // KV
            k = jnp.repeat(k, rep, axis=2)
            v = jnp.repeat(v, rep, axis=2)
            scores = jnp.einsum('bqhd,bkhd->bhqk', q, k) / np.sqrt(HD)
            causal = jnp.tril(jnp.ones((s, s), dtype=bool))
            scores = jnp.where(causal[None, None], scores, jnp.finfo(scores.dtype).min)
            probs = jax.nn.softmax(scores, axis=-1)
            out = jnp.einsum('bhqk,bkhd->bqhd', probs, v).reshape(b, s, H * HD)
            return out @ wo

        def moe(x, gate_w, w1, w3, w2):
            b, s, d = x.shape
            xt = x.reshape(b * s, d)
            logits = xt @ gate_w
            topv, topi = jax.lax.top_k(logits, TOPK)
            probs = jax.nn.softmax(topv, axis=-1)
            w = jnp.zeros_like(logits)
            for kk in range(TOPK):
                w = w + jax.nn.one_hot(topi[:, kk], E, dtype=logits.dtype) * probs[:, kk:kk + 1]
            out = jnp.zeros_like(xt)
            for e in range(E):
                h = jax.nn.silu(xt @ w1[e]) * (xt @ w3[e])
                out = out + w[:, e:e + 1] * (h @ w2[e])
            return out.reshape(b, s, d)
        attn_out = attention(rmsnorm(hidden_states, norm1_w), wq, wk, wv, wo)
        h = hidden_states + attn_out
        out = h + moe(rmsnorm(h, norm2_w), gate_w, w1, w3, w2)
        return out
    x = x + _L0_attn_ref(_layernorm(x, axis=-1), L0_attn_Wq, L0_attn_Wk, L0_attn_Wv, L0_attn_Wo)
    x = x + _L0_xattn_ref(_layernorm(x, axis=-1), ctx_2048, L0_xattn_Wq, L0_xattn_Wk, L0_xattn_Wv)
    x = x + _L0_ffn_ref(_layernorm(x, axis=-1), L0_ffn_weight)
    x = x + _L1_attn_ref(_layernorm(x, axis=-1), L1_attn_Wq, L1_attn_Wk, L1_attn_Wv, L1_attn_Wo, L1_attn_Wg1, L1_attn_Wg2, L1_attn_norm_weight)
    x = x + _L1_xattn_ref(ctx_2048, ctx_2048, _layernorm(x, axis=-1), L1_xattn_ssm_kernel, L1_xattn_D, 8)
    x = x + _L1_ffn_ref(_layernorm(x, axis=-1), L1_ffn_norm1_w, L1_ffn_norm2_w, L1_ffn_wq, L1_ffn_wk, L1_ffn_wv, L1_ffn_wo, L1_ffn_gate_w, L1_ffn_w1, L1_ffn_w3, L1_ffn_w2)
    return x

_drawn_inputs = setup_inputs


def setup_inputs(seed=0):
    import zlib

    import numpy as np

    out = dict(_drawn_inputs(seed))
    spreads = {'L1_attn_norm_weight': (1.0, 0.2),
     'L1_ffn_norm1_w': (1.0, 0.6),
     'L1_ffn_norm2_w': (1.0, 0.6)}
    factors = {'L1_attn_Wg1': 8.0,
     'L1_attn_Wg2': 8.0,
     'L1_ffn_wq': 8.0,
     'L1_ffn_wk': 8.0,
     'L1_ffn_wv': 8.0,
     'L1_ffn_wo': 8.0,
     'L1_ffn_gate_w': 8.0,
     'L1_ffn_w1': 8.0,
     'L1_ffn_w3': 8.0,
     'L1_ffn_w2': 8.0}
    for name, (base, spread) in spreads.items():
        noise = np.random.default_rng([zlib.crc32(name.encode()), seed]).standard_normal(out[name].shape)
        drawn = base * np.exp(spread * noise) if base else spread * noise
        out[name] = jnp.asarray(drawn.astype(out[name].dtype))
    for name, factor in factors.items():
        out[name] = (out[name] * factor).astype(out[name].dtype)
    return out
```

```python
from contextlib import ExitStack

import numpy as np

import concourse.bass as bass
from concourse import mybir

F32 = mybir.dt.float32
BF16 = mybir.dt.bfloat16
I32 = mybir.dt.int32
ALU = mybir.AluOpType
ACT = mybir.ActivationFunctionType
AX = mybir.AxisListType

P = 128
B = 16
D = 256
C = D // P
LN_EPS = 1e-5


class At:

    def __init__(self, base, n, count=B):
        self.base, self.n, self.count = base, n, count
        self.par = n % 2
        self.i = n if base is None else base + n

    def back(self, k):
        return At(self.base, self.n - k, self.count)

    @property
    def on(self):
        return self.base is not None or 0 <= self.n < self.count


def wait(eng, sem, at, back=0, per=1, more=0):
    count = (at.i + (1 - back)) * per + more
    if at.base is not None or count > 0:
        eng.wait_ge(sem, count)


def wait_part(eng, sem, at, per, part):
    count = at.i * per + (part + 1)
    if at.base is not None or count > 0:
        eng.wait_ge(sem, count)


def wait_half(eng, sem, at):
    if at.base is None:
        eng.wait_ge(sem, 16 * (at.n // 2 + 1))
    else:
        eng.wait_ge(sem, at.i * 8 + (16 - 8 * at.par))


def steps(eng, emit, lead, lag, count=B, first=None):
    first = first or (lag + 3) // 2 * 2
    last = first + (count - lead - first) // 2 * 2
    for s in range(-lead, first):
        emit(At(None, s, count))
    with eng.Fori(first // 2, last // 2) as k:
        emit(At(2 * k, 0, count))
        emit(At(2 * k, 1, count))
    for s in range(last, count + lag):
        emit(At(None, s, count))


class Names:

    def __init__(self, nc, ctx, tag):
        self.nc, self.ctx, self.tag, self.sems = nc, ctx, tag, []

    def sb(self, name, shape, dt=F32):
        return self.ctx.enter_context(self.nc.sbuf_tensor(f"{self.tag}.{name}", shape, dt))

    def ps(self, name, shape, dt=F32):
        return self.ctx.enter_context(self.nc.psum_tensor(f"{self.tag}.{name}", shape, dt))

    def sem(self, name):
        self.sems.append(self.ctx.enter_context(self.nc.semaphore(f"{self.tag}.{name}")))
        return self.sems[-1]


def rsqrt_seed(nc, y, x):
    return nc.vector.tensor_scalar(y.bitcast(I32), x.bitcast(I32), -0.5, float(0x5F3759DF), ALU.mult, ALU.add)


def newton_rsqrt(nc, pool, y, x, t, n):
    for _ in range(n):
        nc.gpsimd.tensor_tensor(t, y, y, ALU.mult)
        pool.drain()
        nc.gpsimd.tensor_tensor(t, t, x, ALU.mult)
        pool.drain()
        nc.gpsimd.tensor_scalar(t, t, -0.5, 1.5, ALU.mult, ALU.add)
        pool.drain()
        last = nc.gpsimd.tensor_tensor(y, y, t, ALU.mult)
        pool.drain()
    return last


class Global:
    pass


def allocate(nc, ctx, h):
    g = Global()
    m = Names(nc, ctx, "g")
    g.x = m.sb("x", [P, B, D])
    g.ctxT = m.sb("ctxT", [P, C, B * P])
    g.ident = m.sb("ident", [P, P])
    g.ident_bf = m.sb("ident_bf", [P, P], BF16)
    g.minus_half = m.sb("minus_half", [P, 1])
    early = m.sb("early", [P, 10240])
    late = m.sb("late", [P, 8192])

    def cut(lo, c, n):
        return early[:, lo:lo + c * n].rearrange("p (c n) -> p c n", c=c), lo + c * n

    at = 0
    g.ca_wqk, at = cut(at, C, 2 * D)
    g.ca_wv, at = cut(at, C, D)
    g.ca_wo, at = cut(at, C, D)
    g.xa_wq, at = cut(at, C, D)
    g.xa_wk, at = cut(at, C, D)
    g.xa_wv, at = cut(at, C, D)
    g.ql_w, at = cut(at, C, D)
    g.la_wqk, at = cut(at, C, 2 * D)
    g.la_wv, at = cut(at, C, D)
    g.la_wo, at = cut(at, C, D)
    g.la_wg1, at = cut(at, C, 16)
    g.la_wg2, at = early[0:16, at:at + D], at + D
    g.la_norm, at = early[:, at:at + C], at + C
    g.la_decay, at = cut(at, 16, P)
    g.la_cos, at = early[:, at:at + 8], at + 8
    g.la_sin, at = cut(at, 2, 8)
    assert at <= 10240
    at = 0
    g.ga_wq, at = cut(at, C, 2048)
    g.ga_wk, at = cut(at, C, 512)
    g.ga_wv, at = cut(at, C, 512)
    g.ga_wo, at = cut(at, 16, D)
    assert at <= 10240
    g.early, g.late = early, late
    g.hid = g.ctxT[:].rearrange("p c n -> p (c n)").rearrange("p (b d) -> p b d", b=B)
    g.mo_w1 = m.sb("mo_w1", [P, 8, C, 512])[:]
    g.mo_w2 = late[:, 0:8192].rearrange("p (e f d) -> p e f d", e=8, f=4)
    g.mo_w3 = early[:, 0:8192].rearrange("p (e c f) -> p e c f", e=8, c=C)
    g.ga_norm, g.mo_norm = m.sb("ga_norm", [P, C]), m.sb("mo_norm", [P, C])
    g.ga_cosT, g.ga_sinT = m.sb("ga_cosT", [P, P]), m.sb("ga_sinT", [P, P])
    g.ga_hidden = m.sb("ga_hidden", [P, P], BF16)
    g.quad = m.sb("quad", [P, 4])
    g.pair = m.sb("pair", [P, 2])
    (g.x_loaded, g.ident_loaded, g.consts_loaded, g.ca_loaded, g.xa_loaded, g.la_loaded, g.ctx_loaded, g.ga_loaded,
     g.mo_loaded, g.fill) = map(m.sem, (
        "x_loaded", "ident_loaded", "consts_loaded", "ca_loaded", "xa_loaded", "la_loaded", "ctx_loaded", "ga_loaded",
        "mo_loaded", "fill"))
    g.x_loads, g.const_loads, g.ca_loads, g.xa_loads, g.la_loads = 1, 1, 4, 4, 10
    g.ga_loads, g.mo_loads = 9, 3
    g.m = m
    return g


def load_first(nc, g, h):
    with nc.Block() as block:
        @block.sync
        def _(sp):
            sp.dma_start(g.x[:], h["x"]).then_inc(g.x_loaded, 16)
            for name, to in (("la_wqk", g.la_wqk), ("la_wv", g.la_wv), ("la_wo", g.la_wo), ("la_wg1", g.la_wg1),
                             ("la_wg2", g.la_wg2), ("la_norm", g.la_norm), ("la_decay", g.la_decay), ("la_cos", g.la_cos),
                             ("la_sin", g.la_sin), ("pair", g.pair[:])):
                sp.dma_start(to, h[name]).then_inc(g.la_loaded, 16)
            sp.dma_start(g.ctxT[:], h["ctxR"]).then_inc(g.ctx_loaded, 16)

        @block.scalar
        def _(act):
            act.dma_start(g.ident[:], h["ident"]).then_inc(g.ident_loaded, 16)
            act.dma_start(g.ca_wqk[:, :, 0:D], h["ca_wq"]).then_inc(g.ca_loaded, 16)
            act.dma_start(g.ca_wqk[:, :, D:2 * D], h["ca_wk"]).then_inc(g.ca_loaded, 16)
            act.dma_start(g.ca_wv, h["ca_wv"]).then_inc(g.ca_loaded, 16)
            act.dma_start(g.ca_wo, h["ca_wo"]).then_inc(g.ca_loaded, 16)
            act.dma_start(g.quad[:], h["quad"]).then_inc(g.consts_loaded, 16)
            act.dma_start(g.xa_wq, h["xa_wq"]).then_inc(g.xa_loaded, 16)
            act.dma_start(g.xa_wk, h["xa_wk"]).then_inc(g.xa_loaded, 16)
            act.dma_start(g.xa_wv, h["xa_wv"]).then_inc(g.xa_loaded, 16)
            act.dma_start(g.ql_w, h["ql_w"]).then_inc(g.xa_loaded, 16)

        @block.gpsimd
        def _(pool):
            nc.gpsimd.memset(g.minus_half[:], -0.5).then_inc(g.fill, 1)
            pool.wait_ge(g.ident_loaded, 16)
            nc.gpsimd.tensor_copy(g.ident_bf[:], g.ident[:]).then_inc(g.fill, 1)


def layer_norm_stats(nc, m, x_b, par, eps_var_ready):
    dve = nc.vector
    nc.vector.bn_stats(m.stats[:, par, :], x_b)
    dve.drain()
    nc.vector.bn_aggr(m.mv[:, par, 0:2], m.stats[:, par, :])
    dve.drain()
    nc.vector.tensor_scalar(m.mv[:, par, 2:3], m.mv[:, par, 1:2], LN_EPS, None, ALU.add).then_inc(eps_var_ready, 1)


def layer_norm_apply(nc, m, out, x_b, par):
    return nc.vector.tensor_scalar(out, x_b, m.mv[:, par, 0:1], m.rstd[:, par, 0:1], ALU.subtract, ALU.mult)


def channel_attention(nc, g):
    with ExitStack() as ctx:
        m = Names(nc, ctx, "ca")
        xn = m.sb("xn", [P, 2, D])
        m.stats, m.mv, m.rstd = m.sb("stats", [P, 2, 6]), m.sb("mv", [P, 2, 3]), m.sb("rstd", [P, 2, 1])
        xnT = m.sb("xnT", [P, 2, C, P])
        qk = m.sb("qk", [P, 2, 2 * D])
        vT = m.sb("vT", [P, 2, C, P])
        w = m.sb("w", [P, 2, C, D])
        negmax, rowsum = m.sb("negmax", [P, 2, C]), m.sb("rowsum", [P, 2, C])
        wo = m.sb("wo", [P, 2, C, D])
        mix = m.sb("mix", [P, 2, C, D])
        turn = m.ps("turn", [P, 512])
        pqk = m.ps("pqk", [P, 2 * D])
        pv = m.ps("pv", [P, 512])
        psc = m.ps("psc", [P, C, D])
        pmix = m.ps("pmix", [P, C, D])
        pout = m.ps("pout", [P, 512])
        (var_ready, rstd_ready, xn_ready, turned, xnT_ready, qk_done, qk_ready, vT_done, vT_ready, scores_done,
         max_ready, w_ready, wo_ready, mix_done, mix_ready, out_done, x_added) = map(m.sem, (
            "var_ready", "rstd_ready", "xn_ready", "turned", "xnT_ready", "qk_done", "qk_ready", "vT_done",
            "vT_ready", "scores_done", "max_ready", "w_ready", "wo_ready", "mix_done", "mix_ready", "out_done",
            "x_added"))
        g.finished = m.sems
        scale = 8 ** -0.5
        block = ctx.enter_context(nc.Block())

        @block.gpsimd
        def _(pool):
            def step(s):
                b = s.back(-2)
                if b.on:
                    wait(pool, var_ready, b)
                    wait(pool, xn_ready, b, back=2)
                    nc.gpsimd.tensor_tensor(m.rstd[:, b.par, :], m.mv[:, b.par, 2:3], g.minus_half[:],
                                            ALU.pow).then_inc(rstd_ready, 1)
            steps(pool, step, 2, 2)

        @block.vector
        def _(dve):
            dve.wait_ge(g.x_loaded, 16 * g.x_loads)

            def step(s):
                b = s.back(2)
                if b.on:
                    wait(dve, out_done, b)
                    nc.vector.tensor_tensor(g.x[:, b.i, :], pout[:, 0:D], g.x[:, b.i, :], ALU.add).then_inc(x_added, 1)
                b = s.back(1)
                if b.on:
                    wait(dve, scores_done, b)
                    nc.vector.tensor_reduce(negmax[:, b.par, :], psc[:], AX.X, ALU.max)
                    dve.drain()
                    nc.vector.tensor_scalar(negmax[:, b.par, :], negmax[:, b.par, :], -scale, None,
                                            ALU.mult).then_inc(max_ready, 1)
                b = s.back(-1)
                if b.on:
                    wait(dve, rstd_ready, b)
                    wait(dve, turned, b, back=2)
                    layer_norm_apply(nc, m, xn[:, b.par, :], g.x[:, b.i, :], b.par).then_inc(xn_ready, 1)
                b = s.back(1)
                if b.on:
                    wait(dve, w_ready, b)
                    nc.vector.reciprocal(rowsum[:, b.par, :], rowsum[:, b.par, :])
                    dve.drain()
                    wait(dve, mix_done, b, back=2)
                    for c in range(C):
                        last = nc.vector.tensor_scalar(wo[:, b.par, c, :], g.ca_wo[:, c, :], rowsum[:, b.par, c:c + 1],
                                                       None, ALU.mult)
                    last.then_inc(wo_ready, 1)
                b = s.back(-2)
                if b.on:
                    wait(dve, xn_ready, b, back=2)
                    layer_norm_stats(nc, m, g.x[:, b.i, :], b.par, var_ready)
                if s.on:
                    wait(dve, vT_done, s)
                    wait(dve, out_done, s, back=2)
                    nc.vector.tensor_copy(vT[:, s.par, :, :], pv[:, 0:D]).then_inc(vT_ready, 1)
            steps(dve, step, 2, 2)

        @block.scalar
        def _(act):
            def step(s):
                if s.on:
                    wait(act, turned, s)
                    wait(act, vT_done, s, back=2)
                    nc.scalar.activation(xnT[:, s.par, :, :], turn[:, 0:D], ACT.Copy).then_inc(xnT_ready, 1)
                b = s.back(1)
                if b.on:
                    wait(act, max_ready, b)
                    wait(act, mix_done, b, back=2)
                    for c in range(C):
                        last = nc.scalar.activation(w[:, b.par, c, :], psc[:, c, :], ACT.Exp, bias=negmax[:, b.par, c:c + 1],
                                                    scale=scale, accum_out=rowsum[:, b.par, c:c + 1])
                    last.then_inc(w_ready, 1)
                if s.on:
                    wait(act, qk_done, s)
                    wait(act, scores_done, s, back=2)
                    nc.scalar.activation(qk[:, s.par, :], pqk[:], ACT.Copy).then_inc(qk_ready, 1)
                if b.on:
                    wait(act, mix_done, b)
                    wait(act, out_done, b, back=2)
                    nc.scalar.activation(mix[:, b.par, :, :], pmix[:], ACT.Copy).then_inc(mix_ready, 1)
            steps(act, step, 0, 2)

        @block.tensor
        def _(pe):
            pe.wait_ge(g.ident_loaded, 16)
            pe.wait_ge(g.ca_loaded, 16 * g.ca_loads)

            def step(s):
                if s.on:
                    wait(pe, xn_ready, s)
                    wait(pe, xnT_ready, s, back=1)
                    for c in range(C):
                        last = nc.tensor.transpose(turn[:, c * P:(c + 1) * P], xn[:, s.par, c * P:(c + 1) * P], g.ident[:])
                    last.then_inc(turned, 1)
                b = s.back(2)
                if b.on:
                    wait(pe, mix_ready, b)
                    wait(pe, vT_ready, b)
                    wait(pe, x_added, b, back=1)
                    for c in range(C):
                        last = nc.tensor.matmul(pout[:, 0:D], vT[:, b.par, c, :], mix[:, b.par, c, :],
                                                start=(c == 0), stop=(c == C - 1))
                    last.then_inc(out_done, 1)
                b = s.back(1)
                if b.on:
                    wait(pe, qk_ready, b)
                    wait(pe, w_ready, b, back=1)
                    for c in range(C):
                        last = nc.tensor.matmul(psc[:, c, :], qk[:, b.par, c * P:(c + 1) * P], qk[:, b.par, D:2 * D],
                                                start=True, stop=True)
                    last.then_inc(scores_done, 1)
                if s.on:
                    wait(pe, xnT_ready, s)
                    wait(pe, qk_ready, s, back=1)
                    for c in range(C):
                        last = nc.tensor.matmul(pqk[:], xnT[:, s.par, c, :], g.ca_wqk[:, c, :], start=(c == 0), stop=(c == C - 1))
                    last.then_inc(qk_done, 1)
                    wait(pe, vT_ready, s, back=1)
                    for f in range(C):
                        for c in range(C):
                            last = nc.tensor.matmul(pv[:, f * P:(f + 1) * P], g.ca_wv[:, c, f * P:(f + 1) * P],
                                                    xnT[:, s.par, c, :], start=(c == 0), stop=(c == C - 1))
                    last.then_inc(vT_done, 1)
                if b.on:
                    wait(pe, wo_ready, b)
                    wait(pe, mix_ready, b, back=1)
                    for f in range(C):
                        for c in range(C):
                            last = nc.tensor.matmul(pmix[:, f, :], w[:, b.par, c, f * P:(f + 1) * P], wo[:, b.par, c, :],
                                                    start=(c == 0), stop=(c == C - 1))
                    last.then_inc(mix_done, 1)
            steps(pe, step, 0, 2)


def spread(ap, axis, n):
    v = ap.unsqueeze(axis)
    shape = list(v.shape)
    shape[axis] = n
    return v.broadcast_to(shape)


MAGIC = 12582912.0
Q_MAX = 127.0


def cross_attention_and_quantised_linear(nc, g):
    H, HD = 32, 8
    with ExitStack() as ctx:
        m = Names(nc, ctx, "xa")
        xn = m.sb("xn", [P, 2, D])
        m.stats, m.mv, m.rstd = m.sb("stats", [P, 2, 6]), m.sb("mv", [P, 2, 3]), m.sb("rstd", [P, 2, 1])
        xnT = m.sb("xnT", [P, 2, C, P])
        ctxT = m.sb("ctxT", [P, 2, C, P])
        ctx_loaded = [m.sem(f"ctx_loaded{i}") for i in range(2)]
        sq = m.sb("sq", [P, 2 * D])
        msq, norm, work = m.sb("msq", [P, 2 * H]), m.sb("norm", [P, 2, 2 * H]), m.sb("work", [P, 2 * H])
        qkn = m.sb("qkn", [P, 2, 2 * D])
        kT = m.sb("kT", [P, 2, C, P])
        qT = m.sb("qT", [P, 2, C, 4, P])
        vd = [m.sb(f"vd{k}", [P, 4, 8 * 144]) for k in range(2)]
        oT = m.sb("oT", [P, 4, P])
        e = [g.late[:, n * 4096:(n + 1) * 4096].rearrange("p (h n) -> p h n", h=H) for n in range(2)]
        inv = m.sb("inv", [P, 2, H])
        o = m.sb("o", [P, 2, D])
        n = Names(nc, ctx, "ql")
        yn = n.sb("xn", [P, D])
        n.stats, n.mv, n.rstd = n.sb("stats", [P, 2, 6]), n.sb("mv", [P, 2, 3]), n.sb("rstd", [P, 2, 1])
        amax, q_scale = n.sb("amax", [P, 2, 1]), n.sb("q_scale", [P, 2, 1])
        deq = n.sb("deq", [P, 2, 1])
        rounded = n.sb("rounded", [P, D])
        xq = n.sb("xq", [P, 2, D], BF16)
        xqT = n.sb("xqT", [P, 2, C, P], BF16)
        wq = n.sb("wq", [P, C, D], BF16)
        w_sum, w_all, w_scale = n.sb("w_sum", [P, 1]), n.sb("w_all", [P, 1]), n.sb("w_scale", [P, 4])
        ones = n.sb("ones", [P, P])
        magic = n.sb("magic", [P, 1])
        w_tmp = g.late[:, 0:C * D].rearrange("p (c n) -> p c n", c=C)
        turn, turn2 = m.ps("turn", [P, 512]), m.ps("turn2", [P, 2, C, P])
        pv = turn[:, D:2 * D]
        pqk, po, pot = m.ps("pqk", [P, 2 * D]), m.ps("po", [P, 4, P]), m.ps("pot", [P, 4, P])
        ps = m.ps("ps", [P, 2, 512])
        pc = m.ps("pc", [P, 512])
        pcT = pc[:, 0:P].bitcast(BF16)
        pov = pot[:].rearrange("p g (h t d) -> p (g h) t d", h=8, t=2)
        (var_ready, rstd_ready, xn_ready, turned, xnT_ready, qk_done, sq_ready, v_done, v_ready, msq_ready, norm_ready,
         qk_ready, qk_turned, kT_ready, qT_ready, scores_done, exp_done, pv_done, oT_ready, o_turned, o_ready, x_added) = map(m.sem, (
            "var_ready", "rstd_ready", "xn_ready", "turned", "xnT_ready", "qk_done", "sq_ready", "v_done", "v_ready",
            "msq_ready", "norm_ready", "qk_ready", "qk_turned", "kT_ready", "qT_ready", "scores_done",
            "exp_done", "pv_done", "oT_ready", "o_turned", "o_ready", "x_added"))
        (q_var_ready, q_rstd_ready, rounded_ready, xq_ready, xq_turned, xqT_ready,
         y_done, y_added, w_sum_ready, wq_ready, filled) = map(n.sem, (
            "var_ready", "rstd_ready", "rounded_ready", "xq_ready", "xq_turned",
            "xqT_ready", "y_done", "y_added", "w_sum_ready", "wq_ready", "filled"))
        block = ctx.enter_context(nc.Block())

        @block.sync
        def _(sp):
            def step(s):
                if s.on:
                    wait(sp, v_done, s, back=2)
                    sp.dma_start(ctxT[:, s.par, :, :], g.h["ctxT"][:, :, bass.ts(s.i, P)]).then_inc(ctx_loaded[s.par], 16)
            steps(sp, step, 0, 0, first=2)

        @block.gpsimd
        def _(pool):
            for sem in g.finished:
                nc.gpsimd.sem_clear(sem)
            nc.gpsimd.memset(ones[:], 1.0).then_inc(filled, 1)
            nc.gpsimd.memset(magic[:], MAGIC).then_inc(filled, 1)
            for k in range(2):
                nc.gpsimd.memset(vd[k][:], 0.0)
                pool.drain()
                nc.gpsimd.memset(vd[k][:].rearrange("p g (h c) -> p g h c", c=144)[:, :, :, 8:16], 1.0).then_inc(filled, 1)
            pool.wait_ge(filled, 4)

            def step(s):
                c = s.back(3)
                if c.on:
                    wait(pool, q_var_ready, c)
                    nc.gpsimd.tensor_tensor(n.rstd[:, c.par, :], n.mv[:, c.par, 2:3], g.minus_half[:],
                                            ALU.pow).then_inc(q_rstd_ready, 1)
                if s.on:
                    wait(pool, msq_ready, s)
                    newton_rsqrt(nc, pool, norm[:, s.par, :], msq[:], work[:], 3).then_inc(norm_ready, 1)
                b = s.back(-2)
                if b.on:
                    wait(pool, var_ready, b)
                    wait(pool, xn_ready, b, back=2)
                    nc.gpsimd.tensor_tensor(m.rstd[:, b.par, :], m.mv[:, b.par, 2:3], g.minus_half[:],
                                            ALU.pow).then_inc(rstd_ready, 1)
                if c.on:
                    wait(pool, rounded_ready, c)
                    wait(pool, xq_turned, c, back=2)
                    nc.gpsimd.tensor_tensor(xq[:, c.par, :], rounded[:], magic[:].broadcast_to([P, D]), ALU.subtract).then_inc(xq_ready, 1)
                b = s.back(2)
                if b.on:
                    wait(pool, o_ready, b)
                    nc.gpsimd.tensor_tensor(g.x[:, b.i, :], g.x[:, b.i, :], o[:, b.par, :], ALU.add).then_inc(x_added, 1)
            steps(pool, step, 2, 4)

        @block.vector
        def _(dve):
            dve.wait_ge(g.consts_loaded, 16 * g.const_loads)
            dve.wait_ge(g.xa_loaded, 16 * g.xa_loads)
            nc.vector.tensor_reduce(w_sum[:], g.ql_w, AX.XY, ALU.add, apply_absolute_value=True).then_inc(w_sum_ready, 1)
            dve.wait_ge(w_sum_ready, 2)
            nc.vector.tensor_scalar(w_scale[:, 0:1], pc[:, 0:1], 1.0 / (D * D), 1e-6, ALU.mult, ALU.max)
            dve.drain()
            nc.vector.reciprocal(w_scale[:, 1:2], w_scale[:, 0:1])
            dve.drain()
            nc.vector.tensor_scalar(w_tmp, g.ql_w, w_scale[:, 1:2], MAGIC, ALU.mult, ALU.add)
            dve.drain()
            nc.vector.tensor_scalar(w_tmp, w_tmp, MAGIC + 1.0, MAGIC - 1.0, ALU.min, ALU.max)
            dve.drain()
            nc.vector.tensor_scalar(wq[:], w_tmp, -MAGIC, None, ALU.add).then_inc(wq_ready, 1)
            nc.vector.tensor_scalar(w_scale[:, 2:3], w_scale[:, 0:1], 1.0 / Q_MAX, None, ALU.mult)

            def step(s):
                c = s.back(4)
                if c.on:
                    wait(dve, y_done, c)
                    nc.vector.scalar_tensor_tensor(out=g.x[:, c.i, :], in0=pc[:, D:2 * D], scalar=deq[:, c.par, :],
                                                   in1=g.x[:, c.i, :], op0=ALU.mult, op1=ALU.add).then_inc(y_added, 1)
                c = s.back(3)
                if c.on:
                    wait(dve, x_added, c)
                    layer_norm_stats(nc, n, g.x[:, c.i, :], c.par, q_var_ready)
                b = s.back(1)
                if b.on:
                    wait(dve, qk_turned, b)
                    wait(dve, scores_done, b, back=2, per=8)
                    for k in range(C):
                        last = nc.vector.tensor_tensor(qT[:, b.par, k, :, :], spread(turn2[:, 0, k, :], 1, 4),
                                                       spread(g.quad[:], 2, P), ALU.mult)
                    last.then_inc(qT_ready, 1)
                b = s.back(-1)
                if b.on:
                    wait(dve, rstd_ready, b)
                    wait(dve, turned, b, back=2)
                    layer_norm_apply(nc, m, xn[:, b.par, :], g.x[:, b.i, :], b.par).then_inc(xn_ready, 1)
                if c.on:
                    wait(dve, q_rstd_ready, c)
                    layer_norm_apply(nc, n, yn[:], g.x[:, c.i, :], c.par)
                    dve.drain()
                    nc.vector.tensor_reduce(amax[:, c.par, :], yn[:], AX.X, ALU.max, apply_absolute_value=True)
                    dve.drain()
                    nc.vector.tensor_scalar(amax[:, c.par, :], amax[:, c.par, :], 1e-8, None, ALU.max)
                    dve.drain()
                    nc.vector.tensor_scalar(deq[:, c.par, :], amax[:, c.par, :], w_scale[:, 2:3], None, ALU.mult)
                    nc.vector.reciprocal(q_scale[:, c.par, :], amax[:, c.par, :])
                    dve.drain()
                    nc.vector.tensor_scalar(q_scale[:, c.par, :], q_scale[:, c.par, :], Q_MAX, None, ALU.mult)
                    dve.drain()
                if s.on:
                    wait(dve, sq_ready, s)
                    wait(dve, norm_ready, s, back=1)
                    nc.vector.tensor_reduce(msq[:], sq[:].rearrange("p (h d) -> p h d", d=HD), AX.X, ALU.add)
                    dve.drain()
                    nc.vector.tensor_scalar(msq[:], msq[:], 1.0 / HD, 1e-6, ALU.mult, ALU.add)
                    dve.drain()
                    wait(dve, qk_ready, s, back=2)
                    rsqrt_seed(nc, norm[:, s.par, :], msq[:]).then_inc(msq_ready, 1)
                b = s.back(-2)
                if b.on:
                    wait(dve, xn_ready, b, back=2)
                    layer_norm_stats(nc, m, g.x[:, b.i, :], b.par, var_ready)
                if c.on:
                    nc.vector.tensor_scalar(yn[:], yn[:], q_scale[:, c.par, :], MAGIC, ALU.mult, ALU.add)
                    dve.drain()
                    wait(dve, xq_ready, c, back=1)
                    nc.vector.tensor_scalar(rounded[:], yn[:], MAGIC + Q_MAX, MAGIC - Q_MAX, ALU.min,
                                            ALU.max).then_inc(rounded_ready, 1)
                if s.on:
                    wait(dve, norm_ready, s)
                    wait(dve, qk_turned, s, back=2)
                    nc.vector.tensor_tensor(qkn[:, s.par, :].rearrange("p (h d) -> p h d", d=HD),
                                            pqk[:].rearrange("p (h d) -> p h d", d=HD),
                                            spread(norm[:, s.par, :], 2, HD), ALU.mult).then_inc(qk_ready, 1)
                b = s.back(2)
                if b.on:
                    wait(dve, o_turned, b)
                    nc.vector.reciprocal(inv[:, b.par, :], pov[:, :, 1, 0])
                    dve.drain()
                    wait(dve, x_added, b, back=2)
                    nc.vector.tensor_tensor(o[:, b.par, :].rearrange("p (h d) -> p h d", h=H), pov[:, :, 0, :],
                                            spread(inv[:, b.par, :], 2, HD), ALU.mult).then_inc(o_ready, 1)
            steps(dve, step, 2, 4)

        @block.scalar
        def _(act):
            act.wait_ge(filled, 4)

            def step(s):
                c = s.back(4)
                if c.on:
                    wait(act, xq_turned, c)
                    wait(act, y_done, c, back=2)
                    nc.scalar.activation(xqT[:, c.par, :, :], pcT, ACT.Copy).then_inc(xqT_ready, 1)
                if s.on:
                    wait(act, turned, s)
                    wait(act, qk_done, s, back=2)
                    nc.scalar.activation(xnT[:, s.par, :, :], turn[:, 0:D], ACT.Copy).then_inc(xnT_ready, 1)
                b = s.back(1)
                if b.on:
                    wait(act, qk_turned, b)
                    wait(act, qT_ready, b)
                    wait(act, scores_done, b, back=2, per=8)
                    nc.scalar.activation(kT[:, b.par, :, :], turn2[:, 1, :, :], ACT.Copy).then_inc(kT_ready, 1)
                if s.on:
                    wait(act, qk_done, s)
                    wait(act, msq_ready, s, back=1)
                    nc.scalar.activation(sq[:], pqk[:], ACT.Square).then_inc(sq_ready, 1)
                if b.on:
                    wait(act, pv_done, b, back=2)
                    for r in range(8):
                        wait(act, scores_done, b, back=1, per=8, more=r + 1)
                        nc.scalar.activation(e[b.par][:, 4 * r:4 * r + 4, :], ps[:, r % 2, :], ACT.Exp,
                                             scale=HD ** -0.5).then_inc(exp_done, 1)
                a = s.back(2)
                if a.on:
                    wait(act, pv_done, a)
                    wait(act, o_turned, a, back=1)
                    nc.scalar.activation(oT[:], po[:], ACT.Copy).then_inc(oT_ready, 1)
                if s.on:
                    wait(act, v_done, s)
                    wait(act, pv_done, s, back=2)
                    nc.scalar.activation(vd[s.par][:].rearrange("p g (h c) -> p g h c", c=144)[:, :, :, 0:HD],
                                         pv.rearrange("p (g h d) -> p g h d", g=4, h=8), ACT.Copy).then_inc(v_ready, 1)
            steps(act, step, 0, 4)

        @block.tensor
        def _(pe):
            pe.wait_ge(g.xa_loaded, 16 * g.xa_loads)
            pe.wait_ge(w_sum_ready, 1)
            pe.wait_ge(filled, 1)
            nc.tensor.matmul(pc[:, 0:1], ones[:], w_sum[:], start=True, stop=True).then_inc(w_sum_ready, 1)
            pe.wait_ge(wq_ready, 1)

            def step(s):
                c = s.back(4)
                if c.on:
                    wait(pe, xq_ready, c)
                    wait(pe, y_added, c, back=1)
                    for k in range(C):
                        last = nc.tensor.transpose(pcT[:, k * P:(k + 1) * P], xq[:, c.par, k * P:(k + 1) * P], g.ident_bf[:])
                    last.then_inc(xq_turned, 1)
                b = s.back(1)
                if b.on:
                    wait(pe, qk_ready, b)
                    wait(pe, kT_ready, b, back=1)
                    wait(pe, qT_ready, b, back=1)
                    for t in range(2):
                        for k in range(C):
                            last = nc.tensor.transpose(turn2[:, t, k, :], qkn[:, b.par, t * D + k * P:t * D + (k + 1) * P], g.ident[:])
                    last.then_inc(qk_turned, 1)
                if s.on:
                    wait(pe, xn_ready, s)
                    wait(pe, v_ready, s, back=1)
                    for k in range(C):
                        last = nc.tensor.transpose(turn[:, k * P:(k + 1) * P], xn[:, s.par, k * P:(k + 1) * P], g.ident[:])
                    last.then_inc(turned, 1)
                if c.on:
                    wait(pe, xqT_ready, c)
                    for k in range(C):
                        last = nc.tensor.matmul(pc[:, D:2 * D], xqT[:, c.par, k, :], wq[:, k, :], start=(k == 0), stop=(k == C - 1))
                    last.then_inc(y_done, 1)
                if s.on:
                    wait(pe, xnT_ready, s)
                    wait_half(pe, ctx_loaded[s.par], s)
                    wait(pe, qk_ready, s, back=1)
                    for to, lhs, w in ((pqk[:, 0:D], lambda k: xnT[:, s.par, k, :], g.xa_wq),
                                       (pqk[:, D:2 * D], lambda k: ctxT[:, s.par, k, :], g.xa_wk)):
                        for k in range(C):
                            last = nc.tensor.matmul(to, lhs(k), w[:, k, :], start=(k == 0), stop=(k == C - 1))
                    last.then_inc(qk_done, 1)
                a = s.back(2)
                if b.on:
                    wait(pe, kT_ready, b)
                    wait(pe, qT_ready, b)
                if a.on:
                    wait(pe, exp_done, a, per=8)
                    wait(pe, oT_ready, a, back=1)
                for r in range(8):
                    if b.on:
                        k, rows = r // 4, slice(32 * (r % 4), 32 * (r % 4) + 32)
                        wait(pe, exp_done, b, back=1, per=8, more=r - 1)
                        nc.tensor.matmul(ps[:, r % 2, :], kT[rows, b.par, k, :], qT[rows, b.par, k, :, :],
                                         start=True, stop=True).then_inc(scores_done, 1)
                    if a.on:
                        for t in range(4 * r, 4 * r + 4):
                            gr, hh = t // 8, t % 8
                            last = nc.tensor.matmul(po[:, gr, :], vd[a.par][:, gr, hh * P:(hh + 1) * P], e[a.par][:, t, :],
                                                    start=(hh == 0), stop=(hh == 7))
                if a.on:
                    last.then_inc(pv_done, 1)
                if s.on:
                    for k in range(C):
                        last = nc.tensor.matmul(pv, ctxT[:, s.par, k, :], g.xa_wv[:, k, :], start=(k == 0), stop=(k == C - 1))
                    last.then_inc(v_done, 1)
                if a.on:
                    wait(pe, oT_ready, a)
                    wait(pe, o_ready, a, back=1)
                    for k in range(4):
                        last = nc.tensor.transpose(pot[:, k, :], oT[:, k, :], g.ident[:])
                    last.then_inc(o_turned, 1)
            steps(pe, step, 0, 4)


def linear_attention(nc, g):
    H, HD = 16, 16
    with ExitStack() as ctx:
        m = Names(nc, ctx, "la")
        xn = m.sb("xn", [P, 2, D])
        m.stats, m.mv, m.rstd = m.sb("stats", [P, 2, 6]), m.sb("mv", [P, 2, 3]), m.sb("rstd", [P, 2, 1])
        xnT = m.sb("xnT", [P, 2, C, P])
        qk = m.sb("qk", [P, 2 * D])
        by_cos, by_sin = m.sb("by_cos", [P, 2 * D]), m.sb("by_sin", [P, 2 * D])
        qkr = m.sb("qkr", [P, 2, 2 * D])
        kT = m.sb("kT", [P, 2, C, P])
        qT = m.sb("qT", [P, 2, C, 2, P])
        vd = [m.sb(f"vd{k}", [P, 2, 8 * 144]) for k in range(2)]
        g1T = m.sb("g1T", [16, P])
        gate = m.sb("gate", [P, 2, D])
        a_mat = [g.late[:, k * 2048:(k + 1) * 2048].rearrange("p (h t) -> p h t", h=H) for k in range(2)]
        oT = m.sb("oT", [P, C, P])
        u, usq = m.sb("u", [P, D]), m.sb("usq", [P, D])
        msq, norm, work = m.sb("msq", [P, H]), m.sb("norm", [P, H]), m.sb("work", [P, H])
        un, unT = m.sb("un", [P, D]), m.sb("unT", [P, C, P])
        turn, turn2 = m.ps("turn", [P, 512]), m.ps("turn2", [P, 2, C, P])
        pqk, pvx, po, pot = m.ps("pqk", [P, 2 * D]), m.ps("pvx", [P, 512]), m.ps("po", [P, 512]), m.ps("pot", [P, 512])
        pv, pout = pvx[:, 0:D], pvx[:, D:2 * D]
        pon, pun = pot[:, 0:D], pot[:, D:2 * D]
        ps = m.ps("ps", [P, 2, 512])
        (var_ready, rstd_ready, xn_ready, turned, xnT_ready, qk_done, silu_ready, v_done, v_ready, g1_done, g1_ready,
         gate_done, gate_ready, rot_ready, qk_ready, qk_turned, kT_ready, qT_ready, scores_done, a_ready, av_done,
         oT_ready, o_turned, u_ready, usq_ready, msq_ready, norm_ready, un_ready, un_turned, unT_ready, out_done,
         x_added, filled) = map(m.sem, (
            "var_ready", "rstd_ready", "xn_ready", "turned", "xnT_ready", "qk_done", "silu_ready", "v_done", "v_ready",
            "g1_done", "g1_ready", "gate_done", "gate_ready", "rot_ready", "qk_ready", "qk_turned", "kT_ready",
            "qT_ready", "scores_done", "a_ready", "av_done", "oT_ready", "o_turned", "u_ready", "usq_ready",
            "msq_ready", "norm_ready", "un_ready", "un_turned", "unT_ready", "out_done", "x_added", "filled"))
        block = ctx.enter_context(nc.Block())

        @block.gpsimd
        def _(pool):
            for k in range(2):
                nc.gpsimd.memset(vd[k][:], 0.0).then_inc(filled, 1)

            def step(s):
                a = s.back(2)
                if a.on:
                    wait(pool, u_ready, a)
                    nc.gpsimd.tensor_tensor(usq[:], u[:], u[:], ALU.mult).then_inc(usq_ready, 1)
                    wait(pool, msq_ready, a)
                    newton_rsqrt(nc, pool, norm[:], msq[:], work[:], 3).then_inc(norm_ready, 1)
                if s.on:
                    wait(pool, rot_ready, s)
                    wait(pool, qk_turned, s, back=2)
                    nc.gpsimd.tensor_tensor(qkr[:, s.par, :], by_cos[:], by_sin[:], ALU.add).then_inc(qk_ready, 1)
                b = s.back(-2)
                if b.on:
                    wait(pool, var_ready, b)
                    wait(pool, xn_ready, b, back=2)
                    nc.gpsimd.tensor_tensor(m.rstd[:, b.par, :], m.mv[:, b.par, 2:3], g.minus_half[:],
                                            ALU.pow).then_inc(rstd_ready, 1)
            steps(pool, step, 2, 2)

        @block.vector
        def _(dve):
            dve.wait_ge(g.la_loaded, 16 * g.la_loads)
            for c in range(C):
                last = nc.vector.tensor_scalar(g.la_wo[:, c, :], g.la_wo[:, c, :], g.la_norm[:, c:c + 1], None, ALU.mult)
            last.then_inc(filled, 1)

            def decay(b, r):
                wait(dve, scores_done, b, back=1, per=4, more=r + 1)
                heads = lambda w: w.rearrange("p (k h) t -> p k h t", k=C)[:, :, 2 * r:2 * r + 2, :]
                nc.vector.tensor_tensor(heads(a_mat[b.par]), ps[:, r % 2, :].rearrange("p (k h t) -> p k h t", k=C, h=2),
                                        heads(g.la_decay), ALU.mult).then_inc(a_ready, 1)

            def step(s):
                a, b = s.back(2), s.back(1)
                if a.on:
                    wait(dve, o_turned, a)
                    wait(dve, un_ready, a, back=1)
                    nc.vector.tensor_tensor(u[:], pon, gate[:, a.par, :], ALU.mult).then_inc(u_ready, 1)
                if b.on:
                    wait(dve, qk_turned, b)
                    wait(dve, scores_done, b, back=2, per=4)
                    nc.vector.tensor_tensor(qT[:, b.par, :, :, :], spread(turn2[:, 0, :, :], 2, 2),
                                            spread(spread(g.pair[:], 1, C), 3, P), ALU.mult).then_inc(qT_ready, 1)
                if a.on:
                    wait(dve, usq_ready, a)
                    nc.vector.tensor_reduce(msq[:], usq[:].rearrange("p (h d) -> p h d", d=HD), AX.X, ALU.add)
                    dve.drain()
                    nc.vector.tensor_scalar(msq[:], msq[:], 1.0 / HD, 1e-6, ALU.mult, ALU.add)
                    dve.drain()
                    rsqrt_seed(nc, norm[:], msq[:]).then_inc(msq_ready, 1)
                n = s.back(-1)
                if n.on:
                    wait(dve, rstd_ready, n)
                    wait(dve, turned, n, back=2)
                    layer_norm_apply(nc, m, xn[:, n.par, :], g.x[:, n.i, :], n.par).then_inc(xn_ready, 1)
                if s.on:
                    wait(dve, silu_ready, s)
                    wait(dve, qk_ready, s, back=1)
                    halves = qk[:].rearrange("p (h t d) -> p h t d", t=2, d=8)
                    nc.vector.tensor_tensor(by_cos[:].rearrange("p (h t d) -> p h t d", t=2, d=8), halves,
                                            spread(spread(g.la_cos, 1, 2), 1, 2 * H), ALU.mult)
                    nc.vector.tensor_tensor(by_sin[:].rearrange("p (h t d) -> p h t d", t=2, d=8), halves[:, :, ::-1, :],
                                            spread(g.la_sin, 1, 2 * H), ALU.mult).then_inc(rot_ready, 1)
                if b.on:
                    wait(dve, av_done, b, back=2)
                    decay(b, 0)
                if a.on:
                    wait(dve, norm_ready, a)
                    wait(dve, un_turned, a, back=1)
                    nc.vector.tensor_tensor(un[:].rearrange("p (h d) -> p h d", d=HD), u[:].rearrange("p (h d) -> p h d", d=HD),
                                            spread(norm[:], 2, HD), ALU.mult).then_inc(un_ready, 1)
                if b.on:
                    for r in range(1, 4):
                        decay(b, r)
                n = s.back(-2)
                if n.on:
                    wait(dve, xn_ready, n, back=2)
                    layer_norm_stats(nc, m, g.x[:, n.i, :], n.par, var_ready)
                if a.on:
                    wait(dve, out_done, a)
                    nc.vector.tensor_tensor(g.x[:, a.i, :], pout, g.x[:, a.i, :], ALU.add).then_inc(x_added, 1)
            steps(dve, step, 2, 2)

        @block.scalar
        def _(act):
            act.wait_ge(filled, 3)

            def step(s):
                a, b = s.back(2), s.back(1)
                if b.on:
                    wait(act, qk_turned, b)
                    wait(act, qT_ready, b)
                    wait(act, scores_done, b, back=2, per=4)
                    nc.scalar.activation(kT[:, b.par, :, :], turn2[:, 1, :, :], ACT.Copy).then_inc(kT_ready, 1)
                if s.on:
                    wait(act, turned, s)
                    wait(act, v_done, s, back=2)
                    nc.scalar.activation(xnT[:, s.par, :, :], turn[:, 0:D], ACT.Copy).then_inc(xnT_ready, 1)
                    wait(act, qk_done, s)
                    wait(act, rot_ready, s, back=1)
                    nc.scalar.activation(qk[:], pqk[:], ACT.Silu).then_inc(silu_ready, 1)
                    wait(act, g1_done, s)
                    wait(act, gate_done, s, back=1)
                    nc.scalar.activation(g1T[:], turn[0:16, D:D + P], ACT.Copy).then_inc(g1_ready, 1)
                    wait(act, v_done, s)
                    wait(act, av_done, s, back=2)
                    nc.scalar.activation(vd[s.par][:].rearrange("p g (h c) -> p g h c", c=144)[:, :, :, 0:HD],
                                         pv.rearrange("p (g h d) -> p g h d", g=2, h=8), ACT.Copy).then_inc(v_ready, 1)
                    wait(act, gate_done, s)
                    wait(act, u_ready, s, back=2)
                    nc.scalar.activation(gate[:, s.par, :], turn[:, 0:D], ACT.Sigmoid).then_inc(gate_ready, 1)
                if a.on:
                    wait(act, un_turned, a)
                    wait(act, out_done, a, back=1)
                    nc.scalar.activation(unT[:], pun, ACT.Copy).then_inc(unT_ready, 1)
                if b.on:
                    wait(act, av_done, b)
                    wait(act, o_turned, b, back=1)
                    nc.scalar.activation(oT[:], po[:, 0:D], ACT.Copy).then_inc(oT_ready, 1)
            steps(act, step, 0, 2)

        @block.tensor
        def _(pe):
            pe.wait_ge(g.la_loaded, 16 * g.la_loads)
            pe.wait_ge(filled, 3)

            def step(s):
                a, b = s.back(2), s.back(1)
                if b.on:
                    wait(pe, qk_ready, b)
                    wait(pe, kT_ready, b, back=1)
                    for t in range(2):
                        for k in range(C):
                            last = nc.tensor.transpose(turn2[:, t, k, :], qkr[:, b.par, t * D + k * P:t * D + (k + 1) * P], g.ident[:])
                    last.then_inc(qk_turned, 1)
                if s.on:
                    wait(pe, xn_ready, s)
                    wait(pe, gate_ready, s, back=1)
                    for k in range(C):
                        last = nc.tensor.transpose(turn[:, k * P:(k + 1) * P], xn[:, s.par, k * P:(k + 1) * P], g.ident[:])
                    last.then_inc(turned, 1)
                    wait(pe, xnT_ready, s)
                    wait(pe, silu_ready, s, back=1)
                    for k in range(C):
                        last = nc.tensor.matmul(pqk[:], xnT[:, s.par, k, :], g.la_wqk[:, k, :], start=(k == 0), stop=(k == C - 1))
                    last.then_inc(qk_done, 1)
                    for k in range(C):
                        last = nc.tensor.matmul(turn[0:16, D:D + P], g.la_wg1[:, k, :], xnT[:, s.par, k, :],
                                                start=(k == 0), stop=(k == C - 1))
                    last.then_inc(g1_done, 1)
                    wait(pe, x_added, s, back=3)
                    for k in range(C):
                        last = nc.tensor.matmul(pv, xnT[:, s.par, k, :], g.la_wv[:, k, :], start=(k == 0), stop=(k == C - 1))
                    last.then_inc(v_done, 1)
                    wait(pe, g1_ready, s)
                    nc.tensor.matmul(turn[:, 0:D], g1T[:], g.la_wg2, start=True, stop=True).then_inc(gate_done, 1)
                if b.on:
                    wait(pe, kT_ready, b)
                    wait(pe, qT_ready, b)
                    for r in range(4):
                        wait(pe, a_ready, b, back=1, per=4, more=r - 1)
                        rows = slice(32 * r, 32 * r + 32)
                        for k in range(C):
                            last = nc.tensor.matmul(ps[:, r % 2, k * D:(k + 1) * D], kT[rows, b.par, k, :], qT[rows, b.par, k, :, :],
                                                    start=True, stop=True)
                        last.then_inc(scores_done, 1)
                if a.on:
                    wait(pe, un_ready, a)
                    wait(pe, unT_ready, a, back=1)
                    for k in range(C):
                        last = nc.tensor.transpose(pun[:, k * P:(k + 1) * P], un[:, k * P:(k + 1) * P], g.ident[:])
                    last.then_inc(un_turned, 1)
                if b.on:
                    wait(pe, v_ready, b)
                    wait(pe, a_ready, b, per=4)
                    wait(pe, oT_ready, b, back=1)
                    for h in range(H):
                        gr, hh = h // 8, h % 8
                        last = nc.tensor.matmul(po[:, gr * P:(gr + 1) * P], vd[b.par][:, gr, hh * P:(hh + 1) * P], a_mat[b.par][:, h, :],
                                                start=(hh == 0), stop=(hh == 7))
                    last.then_inc(av_done, 1)
                if a.on:
                    wait(pe, unT_ready, a)
                    if s.on:
                        wait(pe, v_ready, s)
                    for k in range(C):
                        last = nc.tensor.matmul(pout, unT[:, k, :], g.la_wo[:, k, :], start=(k == 0), stop=(k == C - 1))
                    last.then_inc(out_done, 1)
                if b.on:
                    wait(pe, oT_ready, b)
                    wait(pe, u_ready, b, back=1)
                    for k in range(C):
                        last = nc.tensor.transpose(pon[:, k * P:(k + 1) * P], oT[:, k, :], g.ident[:])
                    last.then_inc(o_turned, 1)
            steps(pe, step, 0, 2)


def gated_convolution(nc, g):
    H, HD = 16, 8
    HB = B // 2
    ROW = P - 1 + 2 * P
    with ExitStack() as ctx:
        m = Names(nc, ctx, "cv")
        xn = m.sb("xn", [P, 2, D])
        m.stats, m.mv, m.rstd = m.sb("stats", [P, 2, 6]), m.sb("mv", [P, 2, 3]), m.sb("rstd", [P, 2, 1])
        qT = g.late[:, 0:4096].rearrange("p (c b t) -> p c b t", c=C, b=B)
        oT = g.late[:, 4096:8192].rearrange("p (c b t) -> p c b t", c=C, b=B)
        row = m.sb("row", [H, ROW])
        hidden = m.sb("hidden", [P, P])
        skip = m.sb("skip", [H, 1])
        rows = nc.dram_tensor("cv_rows", [H, ROW], F32, kind="Internal").ap()
        filt = m.sb("filt", [P, 2, 2 * P])
        kv = m.sb("kv", [P, 2, C, 512])
        z = m.sb("z", [P, 2, C, 512])
        turn = m.ps("turn", [P, 2, 512])
        y = m.ps("y", [P, 4, 512])
        (var_ready, rstd_ready, xn_ready, turned, qT_ready, taps_loaded, row_ready, row_stored, kv_ready, y_done,
         z_ready, o_ready, o_turned, x_added, zero_ready) = map(m.sem, (
            "var_ready", "rstd_ready", "xn_ready", "turned", "qT_ready", "taps_loaded", "row_ready", "row_stored",
            "kv_ready", "y_done", "z_ready", "o_ready", "o_turned", "x_added", "zero_ready"))
        filt_loaded = [m.sem(f"filt_loaded{i}") for i in range(2)]
        ctxr = g.ctxT[:].rearrange("p c (b t) -> p c b t", b=B)
        block = ctx.enter_context(nc.Block())

        @block.sync
        def _(sp):
            sp.wait_ge(zero_ready, 1)
            sp.dma_start(row[:, P - 1:], g.h["cv_taps"]).then_inc(taps_loaded, 16)
            sp.dma_start(skip[:], g.h["cv_skip"]).then_inc(taps_loaded, 16)
            sp.wait_ge(row_ready, 1)
            sp.dma_start(rows, row[:]).then_inc(row_stored, 16)
            sp.wait_ge(row_stored, 16)

            def head(s):
                if s.on:
                    wait(sp, y_done, s, back=2, per=4)
                    window = bass.AP(rows.tensor, s.i * ROW, [[1, P], [1, 2 * P]])
                    sp.dma_start(filt[:, s.par, :], window).then_inc(filt_loaded[s.par], 16)
            steps(sp, head, 0, 0, first=2)

        @block.scalar
        def _(act):
            act.dma_start(g.ga_wq, g.h["ga_wq"]).then_inc(g.ga_loaded, 16)
            act.dma_start(g.ga_wk, g.h["ga_wk"]).then_inc(g.ga_loaded, 16)
            act.dma_start(g.ga_wv, g.h["ga_wv"]).then_inc(g.ga_loaded, 16)
            act.dma_start(g.ga_wo, g.h["ga_wo"]).then_inc(g.ga_loaded, 16)
            act.dma_start(g.ga_norm[:], g.h["ga_norm"]).then_inc(g.ga_loaded, 16)
            act.dma_start(g.mo_norm[:], g.h["mo_norm"]).then_inc(g.ga_loaded, 16)
            act.dma_start(g.ga_cosT[:], g.h["ga_cosT"]).then_inc(g.ga_loaded, 16)
            act.dma_start(g.ga_sinT[:], g.h["ga_sinT"]).then_inc(g.ga_loaded, 16)
            act.dma_start(hidden[:], g.h["hidden"]).then_inc(g.ga_loaded, 16)

            def turn_in(s):
                if s.on:
                    wait(act, turned, s)
                    nc.scalar.activation(qT[:, :, s.i, :], turn[:, s.par, 0:D].rearrange("p (c t) -> p c t", c=C),
                                         ACT.Copy).then_inc(qT_ready, 1)
            for b in range(B):
                turn_in(At(None, b))
            act.wait_ge(g.ga_loaded, 16 * g.ga_loads)
            nc.scalar.activation(g.ga_hidden[:], hidden[:], ACT.Copy)

        @block.gpsimd
        def _(pool):
            nc.gpsimd.memset(row[:, 0:P - 1], 0.0).then_inc(zero_ready, 1)
            pool.wait_ge(g.ctx_loaded, 16)

            def products(s):
                for half in range(2):
                    wait(pool, y_done, s, back=2, per=4, more=2 * half + 2)
                    for c in range(C):
                        v = ctxr[:, c, HB * half:HB * (half + 1), bass.ts(s.i, HD)]
                        nc.gpsimd.tensor_tensor(kv[:, half, c, :].rearrange("p (b i j) -> p b i j", b=HB, i=HD),
                                                spread(v, 3, HD), spread(v, 2, HD), ALU.mult).then_inc(kv_ready, 1)

            def norm(s):
                wait(pool, var_ready, s)
                wait(pool, xn_ready, s, back=2)
                nc.gpsimd.tensor_tensor(m.rstd[:, s.par, :], m.mv[:, s.par, 2:3], g.minus_half[:],
                                        ALU.pow).then_inc(rstd_ready, 1)
            for b in range(2):
                norm(At(None, b))
            products(At(None, 0))
            for b in range(2, B):
                norm(At(None, b))
            products(At(None, 1))
            with pool.Fori(1, H // 2) as k:
                products(At(2 * k, 0))
                products(At(2 * k, 1))

        @block.vector
        def _(dve):
            dve.wait_ge(taps_loaded, 32)
            nc.vector.tensor_tensor(row[:, P - 1:P], row[:, P - 1:P], skip[:], ALU.add).then_inc(row_ready, 1)

            for s in range(-1, B):
                n, b = At(None, s + 1), At(None, s)
                if n.on:
                    wait(dve, xn_ready, n, back=2)
                    layer_norm_stats(nc, m, g.x[:, n.i, :], n.par, var_ready)
                if b.on:
                    wait(dve, rstd_ready, b)
                    wait(dve, turned, b, back=2)
                    layer_norm_apply(nc, m, xn[:, b.par, :], g.x[:, b.i, :], b.par).then_inc(xn_ready, 1)
            dve.wait_ge(qT_ready, B)

            def gate(s):
                for half in range(2):
                    bs = slice(HB * half, HB * (half + 1))
                    for c in range(C):
                        wait(dve, y_done, s, back=1, per=4, more=2 * half + c + 1)
                        nc.vector.tensor_tensor(z[:, half, c, :].rearrange("p (b i j) -> p b i j", b=HB, i=HD),
                                                y[:, 2 * half + c, :].rearrange("p (b i j) -> p b i j", b=HB, i=HD),
                                                spread(qT[:, c, bs, bass.ts(s.i, HD)], 3, HD), ALU.mult).then_inc(z_ready, 1)
                    dve.drain()
                    for c in range(C):
                        last = nc.vector.tensor_reduce(oT[:, c, bs, bass.ts(s.i, HD)],
                                                       z[:, half, c, :].rearrange("p (b i j) -> p b j i", b=HB, i=HD),
                                                       AX.X, ALU.add)
                last.then_inc(o_ready, 1)
            with dve.Fori(0, H // 2) as k:
                gate(At(2 * k, 0))
                gate(At(2 * k, 1))
            for b in range(B):
                dve.wait_ge(o_turned, b + 1)
                nc.vector.tensor_tensor(g.x[:, b, :], turn[:, b % 2, 0:D], g.x[:, b, :], ALU.add).then_inc(x_added, 1)

        @block.tensor
        def _(pe):
            for b in range(B):
                s = At(None, b)
                wait(pe, xn_ready, s)
                wait(pe, qT_ready, s, back=2)
                for c in range(C):
                    last = nc.tensor.transpose(turn[:, s.par, c * P:(c + 1) * P], xn[:, s.par, c * P:(c + 1) * P], g.ident[:])
                last.then_inc(turned, 1)

            def convolve(s):
                wait_half(pe, filt_loaded[s.par], s)
                for half in range(2):
                    wait(pe, kv_ready, s, back=1, per=4, more=2 * half + 2)
                    wait(pe, z_ready, s, back=2, per=4, more=2 * half + 1)
                    nc.tensor.matmul(y[:, 2 * half, :], filt[:, s.par, 0:P], kv[:, half, 0, :],
                                     start=True, stop=True).then_inc(y_done, 1)
                    wait(pe, z_ready, s, back=2, per=4, more=2 * half + 2)
                    nc.tensor.matmul(y[:, 2 * half + 1, :], filt[:, s.par, P:], kv[:, half, 0, :], start=True, stop=False)
                    nc.tensor.matmul(y[:, 2 * half + 1, :], filt[:, s.par, 0:P], kv[:, half, 1, :],
                                     start=False, stop=True).then_inc(y_done, 1)
            convolve(At(None, 0))
            convolve(At(None, 1))
            with pe.Fori(1, H // 2) as k:
                convolve(At(2 * k, 0))
                convolve(At(2 * k, 1))
            pe.wait_ge(o_ready, H)
            for b in range(B):
                s = At(None, b)
                wait(pe, x_added, s, back=2)
                for c in range(C):
                    last = nc.tensor.transpose(turn[:, s.par, c * P:(c + 1) * P], oT[:, c, b, :], g.ident[:])
                last.then_inc(o_turned, 1)


def grouped_attention(nc, g):
    H, KV, HD = 16, 4, 128
    REP = H // KV
    NB = KV + 1
    scale = HD ** -0.5
    with ExitStack() as ctx:
        m = Names(nc, ctx, "ga")
        xn = m.sb("xn", [P, 2, D])
        m.stats, m.mv = m.sb("stats", [P, 2, 6]), m.sb("mv", [P, 2, 3])
        m.rstd, rms, t = m.sb("rstd", [P, 2, 1]), m.sb("rms", [P, 2, 1]), m.sb("t", [P, 1])
        xnT = m.sb("xnT", [P, C, P])
        v = m.sb("v", [P, 2, 512])
        halves = m.sb("halves", [P, 2, 512])
        by_cos, by_sin = m.sb("by_cos", [P, 2, 512]), m.sb("by_sin", [P, 2, 512])
        kqT = m.sb("kqT", [P, 2, NB, 512])
        negmax, inv = m.sb("negmax", [P, 2, REP]), m.sb("inv", [P, 2, REP])
        e = m.sb("e", [P, 2, 512])
        probs = m.sb("probs", [P, 2, 512])
        pT = m.sb("pT", [P, 2, 512])
        aT = m.sb("aT", [P, KV, 512])
        turn_out = m.ps("turn_out", [P, 512])
        turn, pout = turn_out[:, 0:D], turn_out[:, D:2 * D]
        pkq = m.ps("pkq", [P, 2, 512])
        pv = m.ps("pv", [P, 512])
        psc = m.ps("psc", [P, 2, 512])
        ppT = m.ps("ppT", [P, 512])
        paT = m.ps("paT", [P, 512])
        (var_ready, rms_ready, xn_ready, turned, xnT_ready, v_done, v_ready, kq_done, halves_ready, cos_ready,
         sin_ready, kqT_ready, scores_done, max_ready, e_ready, p_ready, p_turned, pT_ready, pv_done, aT_ready,
         out_done, h_ready) = map(m.sem, (
            "var_ready", "rms_ready", "xn_ready", "turned", "xnT_ready", "v_done", "v_ready", "kq_done", "halves_ready",
            "cos_ready", "sin_ready", "kqT_ready", "scores_done", "max_ready", "e_ready", "p_ready", "p_turned",
            "pT_ready", "pv_done", "aT_ready", "out_done", "h_ready"))
        block = ctx.enter_context(nc.Block())

        def bank(eng, sem, s, r, back=0):
            wait_part(eng, sem, s, NB, r - back)

        def group(eng, sem, s, r, back=0):
            wait_part(eng, sem, s, KV, r - back)

        @block.sync
        def _(sp):
            sp.dma_start(g.mo_w1, g.h["mo_w1"]).then_inc(g.mo_loaded, 16)
            sp.dma_start(g.mo_w2, g.h["mo_w2"]).then_inc(g.mo_loaded, 16)

        @block.gpsimd
        def _(pool):
            def rope(s, r):
                par = (s.n * NB + r) % 2
                bank(pool, halves_ready, s, r)
                nc.gpsimd.tensor_tensor(by_sin[:, par, :].rearrange("p (h t) -> p h t", h=REP),
                                        halves[:, par, :].rearrange("p (h t) -> p h t", h=REP),
                                        spread(g.ga_sinT[:], 1, REP), ALU.mult).then_inc(sin_ready, 1)
                pool.drain()
                bank(pool, cos_ready, s, r)
                if r == 0:
                    group(pool, scores_done, s, 3, back=2 * KV)
                nc.gpsimd.tensor_tensor(kqT[:, s.par, r, :], by_cos[:, par, :], by_sin[:, par, :], ALU.add).then_inc(kqT_ready, 1)

            def step(s):
                if s.on:
                    rope(s, 0)
                    rope(s, 1)
                n = s.back(-2)
                if n.on:
                    mv, rstd, rr = m.mv[:, n.par, :], m.rstd[:, n.par, :], rms[:, n.par, :]
                    wait(pool, var_ready, n)
                    wait(pool, xn_ready, n, back=2)
                    nc.gpsimd.tensor_tensor(rstd, mv[:, 2:3], g.minus_half[:], ALU.pow)
                    pool.drain()
                    nc.gpsimd.tensor_tensor(t[:], rstd, rstd, ALU.mult)
                    pool.drain()
                    nc.gpsimd.tensor_tensor(t[:], t[:], mv[:, 1:2], ALU.mult)
                    pool.drain()
                    nc.gpsimd.tensor_scalar(t[:], t[:], 1.0, 1e-5, ALU.mult, ALU.add)
                    pool.drain()
                    nc.gpsimd.tensor_tensor(t[:], t[:], g.minus_half[:], ALU.pow)
                    pool.drain()
                    nc.gpsimd.tensor_tensor(rr, t[:], rstd, ALU.mult).then_inc(rms_ready, 1)
                if s.on:
                    for r in range(2, NB):
                        rope(s, r)
            steps(pool, step, 2, 2)

        @block.vector
        def _(dve):
            def cos(s, r):
                par = (s.n * NB + r) % 2
                bank(dve, kq_done, s, r)
                bank(dve, kqT_ready, s, r, back=2)
                nc.vector.tensor_tensor(by_cos[:, par, :].rearrange("p (h t) -> p h t", h=REP),
                                        pkq[:, par, :].rearrange("p (h t) -> p h t", h=REP),
                                        spread(g.ga_cosT[:], 1, REP), ALU.mult).then_inc(cos_ready, 1)

            def maxima(b, r):
                group(dve, scores_done, b, r)
                group(dve, e_ready, b, r, back=2)
                nc.vector.tensor_reduce(negmax[:, r % 2, :], psc[:, r % 2, :].rearrange("p (h k) -> p h k", h=REP), AX.X, ALU.max)
                dve.drain()
                nc.vector.tensor_scalar(negmax[:, r % 2, :], negmax[:, r % 2, :], -scale, None, ALU.mult).then_inc(max_ready, 1)

            def normalise(b, r):
                group(dve, e_ready, b, r)
                nc.vector.reciprocal(inv[:, r % 2, :], inv[:, r % 2, :])
                dve.drain()
                group(dve, p_turned, b, r, back=2)
                nc.vector.tensor_tensor(probs[:, r % 2, :].rearrange("p (h k) -> p h k", h=REP),
                                        e[:, r % 2, :].rearrange("p (h k) -> p h k", h=REP),
                                        spread(inv[:, r % 2, :], 2, P), ALU.mult).then_inc(p_ready, 1)

            def step(s):
                a, b = s.back(2), s.back(1)
                if b.on:
                    maxima(b, 0)
                    maxima(b, 1)
                    normalise(b, 0)
                    normalise(b, 1)
                n = s.back(-2)
                if n.on:
                    wait(dve, xn_ready, n, back=2)
                    layer_norm_stats(nc, m, g.x[:, n.i, :], n.par, var_ready)
                n = s.back(-1)
                if n.on:
                    wait(dve, rms_ready, n)
                    wait(dve, turned, n, back=2)
                    nc.vector.tensor_scalar(g.hid[:, n.i, :], g.x[:, n.i, :], m.mv[:, n.par, 0:1], m.rstd[:, n.par, :],
                                            ALU.subtract, ALU.mult)
                    nc.vector.tensor_scalar(xn[:, n.par, :], g.x[:, n.i, :], m.mv[:, n.par, 0:1], rms[:, n.par, :],
                                            ALU.subtract, ALU.mult).then_inc(xn_ready, 1)
                if a.on:
                    wait(dve, out_done, a)
                    nc.vector.tensor_tensor(g.hid[:, a.i, :], pout, g.hid[:, a.i, :], ALU.add).then_inc(h_ready, 1)
                if s.on:
                    cos(s, 0)
                    cos(s, 1)
                if b.on:
                    maxima(b, 2)
                    normalise(b, 2)
                if s.on:
                    cos(s, 2)
                if b.on:
                    maxima(b, 3)
                    normalise(b, 3)
                if s.on:
                    cos(s, 3)
                    cos(s, 4)
            steps(dve, step, 2, 2)

        @block.scalar
        def _(act):
            def swap(s, r):
                par = (s.n * NB + r) % 2
                bank(act, cos_ready, s, r)
                bank(act, sin_ready, s, r, back=2)
                nc.scalar.activation(halves[0:64, par, :], pkq[64:128, par, :], ACT.Copy)
                nc.scalar.activation(halves[64:128, par, :], pkq[0:64, par, :], ACT.Copy).then_inc(halves_ready, 1)

            def exps(b, r):
                group(act, max_ready, b, r)
                group(act, p_ready, b, r, back=2)
                for j in range(REP):
                    last = nc.scalar.activation(e[:, r % 2, j * P:(j + 1) * P], psc[:, r % 2, j * P:(j + 1) * P], ACT.Exp,
                                                bias=negmax[:, r % 2, j:j + 1], scale=scale, accum_out=inv[:, r % 2, j:j + 1])
                last.then_inc(e_ready, 1)

            def copy_pT(b, r):
                group(act, p_turned, b, r)
                group(act, pv_done, b, r, back=2)
                nc.scalar.activation(pT[:, r % 2, :], ppT[:], ACT.Copy).then_inc(pT_ready, 1)

            def copy_aT(b, r):
                group(act, pv_done, b, r)
                if r == 0:
                    wait(act, out_done, b, back=1)
                nc.scalar.activation(aT[:, r, :], paT[:], ACT.Copy).then_inc(aT_ready, 1)

            def step(s):
                b = s.back(1)
                if s.on:
                    wait(act, turned, s)
                    bank(act, kq_done, s, NB - 1, back=NB)
                    for c in range(C):
                        last = nc.scalar.activation(xnT[:, c, :], turn[:, c * P:(c + 1) * P], ACT.Copy, scale=g.ga_norm[:, c:c + 1])
                    last.then_inc(xnT_ready, 1)
                if b.on:
                    exps(b, 0)
                    exps(b, 1)
                if s.on:
                    wait(act, v_done, s)
                    group(act, pv_done, s, KV - 1, back=2 * KV)
                    nc.scalar.activation(v[:, s.par, :], pv[:], ACT.Copy).then_inc(v_ready, 1)
                    swap(s, 0)
                if b.on:
                    copy_pT(b, 0)
                if s.on:
                    swap(s, 1)
                if b.on:
                    exps(b, 2)
                    copy_aT(b, 0)
                    copy_pT(b, 1)
                if s.on:
                    swap(s, 2)
                if b.on:
                    exps(b, 3)
                    copy_aT(b, 1)
                    copy_pT(b, 2)
                if s.on:
                    swap(s, 3)
                if b.on:
                    copy_aT(b, 2)
                    copy_pT(b, 3)
                if s.on:
                    swap(s, 4)
                if b.on:
                    copy_aT(b, 3)
            steps(act, step, 0, 2)

        @block.tensor
        def _(pe):
            pe.wait_ge(g.ga_loaded, 16 * g.ga_loads)

            def kq(s, r):
                par = (s.n * NB + r) % 2
                bank(pe, halves_ready, s, r, back=2)
                for j in range(REP):
                    w, at = (g.ga_wk, j) if r == 0 else (g.ga_wq, REP * (r - 1) + j)
                    for c in range(C):
                        last = nc.tensor.matmul(pkq[:, par, j * P:(j + 1) * P], w[:, c, at * P:(at + 1) * P], xnT[:, c, :],
                                                start=(c == 0), stop=(c == C - 1))
                last.then_inc(kq_done, 1)

            def scores(b, r):
                wait_part(pe, kqT_ready, b, NB, r + 1)
                group(pe, e_ready, b, r, back=2)
                nc.tensor.matmul(psc[:, r % 2, :], g.ident_bf[:], spread(g.ga_hidden[:], 1, REP), start=True, stop=False,
                                 skip_group_check=True)
                for j in range(REP):
                    last = nc.tensor.matmul(psc[:, r % 2, j * P:(j + 1) * P], kqT[:, b.par, r + 1, j * P:(j + 1) * P],
                                            kqT[:, b.par, 0, r * P:(r + 1) * P], start=False, stop=True, skip_group_check=True)
                last.then_inc(scores_done, 1)

            def turn_probs(b, r):
                group(pe, p_ready, b, r)
                group(pe, pT_ready, b, r, back=1)
                for j in range(REP):
                    last = nc.tensor.transpose(ppT[:, j * P:(j + 1) * P], probs[:, r % 2, j * P:(j + 1) * P], g.ident[:])
                last.then_inc(p_turned, 1)

            def values(b, r):
                group(pe, pT_ready, b, r)
                group(pe, aT_ready, b, r, back=1)
                nc.tensor.matmul(paT[:], v[:, b.par, r * P:(r + 1) * P], pT[:, r % 2, :], start=True, stop=True).then_inc(pv_done, 1)

            def step(s):
                a, b = s.back(2), s.back(1)
                if s.on:
                    wait(pe, xn_ready, s)
                    wait(pe, h_ready, s, back=3)
                    for c in range(C):
                        last = nc.tensor.transpose(turn[:, c * P:(c + 1) * P], xn[:, s.par, c * P:(c + 1) * P], g.ident[:])
                    last.then_inc(turned, 1)
                if b.on:
                    scores(b, 0)
                    scores(b, 1)
                if s.on:
                    wait(pe, xnT_ready, s)
                if a.on:
                    group(pe, aT_ready, a, KV - 1)
                    for h in range(H):
                        last = nc.tensor.matmul(pout, aT[:, h // REP, (h % REP) * P:(h % REP + 1) * P], g.ga_wo[:, h, :],
                                                start=(h == 0), stop=(h == H - 1))
                    last.then_inc(out_done, 1)
                if s.on:
                    wait(pe, v_ready, s, back=1)
                    for c in range(C):
                        last = nc.tensor.matmul(pv[:], xnT[:, c, :], g.ga_wv[:, c, :], start=(c == 0), stop=(c == C - 1))
                    last.then_inc(v_done, 1)
                    kq(s, 0)
                for r in range(KV):
                    if b.on:
                        turn_probs(b, r)
                        if r < 2:
                            scores(b, r + 2)
                    if s.on:
                        kq(s, r + 1)
                    if b.on:
                        if r == 0:
                            wait(pe, v_ready, b)
                        values(b, r)
            steps(pe, step, 0, 2)


E, F = 8, 512
REGION = B * P + P
TILES = 2 * B * P // P + E - 1
SPARE = E - 1
ROW = D + 2


def allocate_moe(nc, g):
    m = g.m
    g.rows = nc.dram_tensor("mo_rows", [E * REGION + SPARE * P, ROW], F32, kind="Internal").ap()
    g.acc = nc.dram_tensor("mo_acc", [B * P + P, D], F32, kind="Internal").ap()
    g.tile_expert, g.tile_row = m.sb("tile_expert", [P, TILES], I32), m.sb("tile_row", [P, TILES], I32)


def route(nc, g):
    with ExitStack() as ctx:
        m = Names(nc, ctx, "ro")
        gate = m.sb("gate", [P, C, E])
        before, before_bf, ones = m.sb("before", [P, P]), m.sb("before_bf", [P, P], BF16), m.sb("ones", [P, P], BF16)
        expert_no, region_at = m.sb("expert_no", [P, E]), m.sb("region_at", [P, E])
        token_no, tile_no = m.sb("token_no", [P, B + 1]), m.sb("tile_no", [P, TILES])
        square, ss, rms = m.sb("square", [P, 2, D]), m.sb("ss", [P, 2, 1]), m.sb("rms", [P, 2, 1])
        row = m.sb("row", [P, 2, 2 * ROW])
        xnT = m.sb("xnT", [P, 2, C, P])
        logits = m.sb("logits", [P, E])
        top = m.sb("top", [P, E])
        which, which_f = m.sb("which", [P, E], mybir.dt.uint32), m.sb("which_f", [P, 2])
        margin = m.sb("margin", [P, 2, 1])
        chosen = m.sb("chosen", [P, 2, 2, E])
        both = m.sb("both", [P, 2, E], BF16)
        earlier = m.sb("earlier", [P, E], BF16)
        place, at = m.sb("place", [P, E]), m.sb("at", [P, 2, E])
        zero = m.sb("zero", [P, 2], mybir.dt.uint32)
        slot_f, slot_d = m.sb("slot_f", [P, 2]), m.sb("slot_d", [P, 2, 2], mybir.dt.uint32)
        slot = m.sb("slot", [P, 2, 2], mybir.dt.uint32)
        pad = m.sb("pad", [P, ROW])
        pad_f, pad_slot = m.sb("pad_f", [P, E]), m.sb("pad_slot", [P, E], mybir.dt.uint32)
        tiles, ends, ends2 = m.sb("tiles", [P, E]), m.sb("ends", [P, E]), m.sb("ends2", [P, E])
        past, past_tiles = m.sb("past", [P, TILES, E]), m.sb("past_tiles", [P, TILES, E])
        expert_f, start_f = m.sb("expert_f", [P, TILES]), m.sb("start_f", [P, TILES])
        turn = m.ps("turn", [P, 512])
        plog = m.ps("plog", [P, 512])
        prank = m.ps("prank", [P, 512])
        (gates_loaded, filled, ss_ready, ms_ready, rms_ready, row_ready, turned, xnT_ready, log_done, margin_ready,
         chosen_ready, p_ready, rank_done, slot_ready, pad_ready, spare_stored, sum_ready, acc_stored) = map(m.sem, (
            "gates_loaded", "filled", "ss_ready", "ms_ready", "rms_ready", "row_ready", "turned", "xnT_ready",
            "log_done", "margin_ready", "chosen_ready", "p_ready", "rank_done", "slot_ready", "pad_ready",
            "spare_stored", "sum_ready", "acc_stored"))
        sent = [m.sem(f"sent{i}") for i in range(2)]
        pads_sent = m.sem("pads_sent")
        constants_loaded = ((gate[:], "mo_gate"), (before[:], "before"), (expert_no[:], "expert_no"),
                            (region_at[:], "region_at"), (token_no[:], "token_no"), (tile_no[:], "tile_no"))
        block = ctx.enter_context(nc.Block())

        def to_expert(pool, k, s):
            nc.gpsimd.indirect_dma_start(g.rows, bass.IndirectOffsetOnAxis(ap=slot[:, s.par, k:k + 1], axis=0),
                                         row[:, s.par, k * ROW:(k + 1) * ROW], None).then_inc(sent[s.par], 16)

        @block.sync
        def _(sp):
            for to, name in constants_loaded:
                sp.dma_start(to, g.h[name]).then_inc(gates_loaded, 16)
            sp.dma_start(g.mo_w3, g.h["mo_w3"]).then_inc(g.mo_loaded, 16)
            sp.wait_ge(pad_ready, 1)
            sp.dma_start(g.rows[E * REGION:, :].rearrange("(t p) c -> p t c", p=P), spread(pad[:], 1, SPARE)).then_inc(spare_stored, 16)
            sp.dma_start(g.acc[B * P:, :], pad[:, 0:D]).then_inc(spare_stored, 16)

            def store(s):
                if s.on:
                    wait(sp, sum_ready, s)
                    sp.dma_start(g.acc[bass.ts(s.i, P), :], g.x[:, s.i, :]).then_inc(acc_stored, 16)
            steps(sp, store, 0, 0, first=2)
            sp.wait_ge(spare_stored, 32)
            sp.wait_ge(acc_stored, 16 * B)

        @block.gpsimd
        def _(pool):
            nc.gpsimd.memset(ones[:], 1.0).then_inc(filled, 1)
            nc.gpsimd.memset(earlier[:], 0.0).then_inc(filled, 1)
            nc.gpsimd.memset(pad[:, 0:D + 1], 0.0).then_inc(filled, 1)
            nc.gpsimd.memset(zero[:], 0)
            pool.drain()

            def step(s):
                if s.on:
                    wait(pool, ms_ready, s)
                    nc.gpsimd.tensor_tensor(rms[:, s.par, :], ss[:, s.par, :], g.minus_half[:], ALU.pow).then_inc(rms_ready, 1)
                a = s.back(2)
                if a.on:
                    wait(pool, p_ready, a)
                    wait(pool, slot_ready, a)
                    nc.gpsimd.tensor_tensor(slot[:, a.par, :], slot_d[:, a.par, :], zero[:], ALU.add)
                    pool.drain()
                    to_expert(pool, 0, a)
                    to_expert(pool, 1, a)
            steps(pool, step, 0, 2)
            pool.wait_ge(pad_ready, 2)
            for e in range(E):
                nc.gpsimd.indirect_dma_start(g.rows, bass.IndirectOffsetOnAxis(ap=pad_slot[:, e:e + 1], axis=0), pad[:],
                                             None).then_inc(pads_sent, 16)
            for k in range(2):
                pool.wait_ge(sent[k], 16 * B)
            pool.wait_ge(pads_sent, 16 * E)

        @block.vector
        def _(dve):
            dve.wait_ge(filled, 3)
            dve.wait_ge(gates_loaded, 16 * len(constants_loaded))
            nc.vector.tensor_copy(pad[:, D + 1:], token_no[:, B:]).then_inc(pad_ready, 1)
            nc.vector.tensor_copy(before_bf[:], before[:]).then_inc(filled, 1)

            def step(s):
                if s.on:
                    wait(dve, ss_ready, s)
                    nc.vector.tensor_scalar(ss[:, s.par, :], ss[:, s.par, :], 1.0 / D, 1e-5, ALU.mult, ALU.add).then_inc(ms_ready, 1)
                    wait(dve, rms_ready, s)
                    if s.base is not None or s.n >= 2:
                        dve.wait_ge(sent[s.par], (s.i - s.par) * 16 if s.base is not None else (s.n - s.par) * 16)
                    for k in range(2):
                        nc.vector.tensor_scalar(row[:, s.par, k * ROW:k * ROW + D], g.hid[:, s.i, :], rms[:, s.par, :], None, ALU.mult)
                    last = nc.vector.tensor_copy(row[:, s.par, :].rearrange("p (k c) -> p k c", k=2)[:, :, D + 1],
                                                 token_no[:, bass.ds(s.i, 1)].broadcast_to([P, 2]))
                    last.then_inc(row_ready, 1)
                    nc.vector.tensor_tensor(g.x[:, s.i, :], g.x[:, s.i, :], g.hid[:, s.i, :], ALU.add).then_inc(sum_ready, 1)
                b = s.back(1)
                if b.on:
                    wait(dve, log_done, b)
                    nc.vector.tensor_copy(logits[:], plog[:, 0:E])
                    dve.drain()
                    nc.vector.max(top[:], logits[:])
                    dve.drain()
                    nc.vector.max_index(which[:], top[:], logits[:])
                    wait(dve, p_ready, b, back=2)
                    nc.vector.tensor_tensor(margin[:, b.par, :], top[:, 0:1], top[:, 1:2], ALU.subtract).then_inc(margin_ready, 1)
                    dve.drain()
                    nc.vector.tensor_copy(which_f[:], which[:, 0:2])
                    dve.drain()
                    nc.vector.tensor_tensor(chosen[:, b.par, :, :], spread(which_f[:], 2, E), spread(expert_no[:], 1, 2), ALU.is_equal)
                    dve.drain()
                    nc.vector.tensor_tensor(both[:, b.par, :], chosen[:, b.par, 0, :], chosen[:, b.par, 1, :],
                                            ALU.add).then_inc(chosen_ready, 1)
                    wait(dve, rank_done, b)
                    nc.vector.tensor_tensor(earlier[:], earlier[:], both[:, b.par, :], ALU.add)
                    nc.vector.tensor_tensor(place[:], prank[:, 0:E], region_at[:], ALU.add)
                    dve.drain()
                    nc.vector.tensor_tensor(at[:], chosen[:, b.par, :, :], spread(place[:], 1, 2), ALU.mult)
                    dve.drain()
                    nc.vector.tensor_reduce(slot_f[:], at[:], AX.X, ALU.add)
                    dve.drain()
                    if b.base is not None or b.n >= 2:
                        dve.wait_ge(sent[b.par], (b.i - b.par) * 16 if b.base is not None else (b.n - b.par) * 16)
                    nc.vector.tensor_copy(slot_d[:, b.par, :], slot_f[:]).then_inc(slot_ready, 1)
            steps(dve, step, 0, 2)

            dve.wait_ge(rank_done, B + 1)
            nc.vector.tensor_tensor(pad_f[:], prank[:, 0:E], region_at[:], ALU.add)
            nc.vector.tensor_scalar(tiles[:], prank[:, 0:E], 1.0 / P, 63.5 / P, ALU.mult, ALU.add)
            dve.drain()
            nc.vector.tensor_scalar(pad_f[:], pad_f[:], token_no[:, 0:1], None, ALU.add)
            nc.vector.tensor_scalar(tiles[:], tiles[:], MAGIC, None, ALU.add)
            dve.drain()
            nc.vector.tensor_copy(pad_slot[:], pad_f[:]).then_inc(pad_ready, 1)
            nc.vector.tensor_scalar(tiles[:], tiles[:], -MAGIC, None, ALU.add)
            dve.drain()
            src, dst = tiles, ends
            for shift in (1, 2, 4):
                nc.vector.tensor_copy(dst[:, 0:shift], src[:, 0:shift])
                nc.vector.tensor_tensor(dst[:, shift:], src[:, shift:], src[:, 0:E - shift], ALU.add)
                dve.drain()
                src, dst = dst, (ends2 if dst is ends else ends)
            nc.vector.tensor_tensor(past[:], spread(tile_no[:], 2, E), spread(src[:], 1, TILES), ALU.is_ge)
            dve.drain()
            nc.vector.tensor_tensor(past_tiles[:], past[:], spread(tiles[:], 1, TILES), ALU.mult)
            nc.vector.tensor_reduce(expert_f[:], past[:], AX.X, ALU.add)
            dve.drain()
            nc.vector.tensor_reduce(start_f[:], past_tiles[:], AX.X, ALU.add)
            dve.drain()
            nc.vector.tensor_tensor(start_f[:], tile_no[:], start_f[:], ALU.subtract)
            dve.drain()
            nc.vector.tensor_scalar(start_f[:], start_f[:], float(P), None, ALU.mult)
            dve.drain()
            nc.vector.scalar_tensor_tensor(out=start_f[:], in0=expert_f[:], scalar=float(REGION), in1=start_f[:],
                                           op0=ALU.mult, op1=ALU.add)
            nc.vector.tensor_scalar(expert_f[:], expert_f[:], float(E - 1), None, ALU.min)
            dve.drain()
            nc.vector.tensor_copy(g.tile_row[:], start_f[:])
            nc.vector.tensor_copy(g.tile_expert[:], expert_f[:])

        @block.scalar
        def _(act):
            def step(s):
                n = s.back(-1)
                if n.on:
                    wait(act, row_ready, n, back=2)
                    nc.scalar.activation(square[:, n.par, :], g.hid[:, n.i, :], ACT.Square, accum_out=ss[:, n.par, :]).then_inc(ss_ready, 1)
                if s.on:
                    wait(act, turned, s)
                    wait(act, log_done, s, back=2)
                    for c in range(C):
                        last = nc.scalar.activation(xnT[:, s.par, c, :], turn[:, c * P:(c + 1) * P], ACT.Copy, scale=g.mo_norm[:, c:c + 1])
                    last.then_inc(xnT_ready, 1)
                b = s.back(1)
                if b.on:
                    wait(act, margin_ready, b)
                    for k in range(2):
                        last = nc.scalar.activation(row[:, b.par, k * ROW + D:k * ROW + D + 1], margin[:, b.par, :], ACT.Sigmoid,
                                                    scale=1.0 - 2.0 * k)
                    last.then_inc(p_ready, 1)
            steps(act, step, 1, 2)

        @block.tensor
        def _(pe):
            pe.wait_ge(filled, 4)

            def step(s):
                if s.on:
                    wait(pe, row_ready, s)
                    wait(pe, xnT_ready, s, back=1)
                    for c in range(C):
                        last = nc.tensor.transpose(turn[:, c * P:(c + 1) * P], row[:, s.par, c * P:(c + 1) * P], g.ident[:])
                    last.then_inc(turned, 1)
                    wait(pe, xnT_ready, s)
                    wait(pe, margin_ready, s, back=1)
                    for c in range(C):
                        last = nc.tensor.matmul(plog[:, 0:E], xnT[:, s.par, c, :], gate[:, c, :], start=(c == 0), stop=(c == C - 1))
                    last.then_inc(log_done, 1)
                b = s.back(1)
                if b.on:
                    wait(pe, chosen_ready, b)
                    wait(pe, slot_ready, b, back=1)
                    nc.tensor.matmul(prank[:, 0:E], before_bf[:], both[:, b.par, :], start=True, stop=False)
                    nc.tensor.matmul(prank[:, 0:E], ones[:], earlier[:], start=False, stop=True).then_inc(rank_done, 1)
            steps(pe, step, 0, 2)
            pe.wait_ge(slot_ready, B)
            nc.tensor.matmul(prank[:, 0:E], ones[:], earlier[:], start=True, stop=True).then_inc(rank_done, 1)


def experts(nc, g):
    with ExitStack() as ctx:
        m = Names(nc, ctx, "ex")
        row = m.sb("row", [P, 2, ROW])
        weight, token_d = m.sb("weight", [P, 2, 1]), m.sb("token_d", [P, 2, 1], mybir.dt.uint32)
        token, zero = m.sb("token", [P, 2, 1], mybir.dt.uint32), m.sb("zero", [P, 1], mybir.dt.uint32)
        xnT = m.sb("xnT", [P, 2, C, P])
        silu, hidden = m.sb("silu", [P, F]), m.sb("hidden", [P, F])
        hT = m.sb("hT", [P, F])
        y = m.sb("y", [P, 2, D])
        turn, p1, p3, phT, py = m.ps("turn", [P, 512]), m.ps("p1", [P, F]), m.ps("p3", [P, F]), m.ps("phT", [P, F]), m.ps("py", [P, 512])
        (meta_ready, turned, xnT_ready, h1_done, h3_done, silu_ready, hidden_ready, h_turned, hT_ready, y_done, y_ready,
         added, out_stored) = map(m.sem, (
            "meta_ready", "turned", "xnT_ready", "h1_done", "h3_done", "silu_ready", "hidden_ready", "h_turned", "hT_ready",
            "y_done", "y_ready", "added", "out_stored"))
        row_loaded = [m.sem(f"row_loaded{i}") for i in range(2)]
        block = ctx.enter_context(nc.Block())

        @block.sync
        def _(sp):
            def load(t):
                if t.on:
                    first = sp.value_load(g.tile_row[0:1, bass.ds(t.i, 1)], min_val=0, max_val=E * REGION + (SPARE - 1) * P)
                    wait(sp, turned, t, back=2)
                    wait(sp, meta_ready, t, back=2)
                    sp.dma_start(row[:, t.par, :], g.rows[bass.ds(first, P), :]).then_inc(row_loaded[t.par], 16)
            steps(sp, load, 0, 0, count=TILES, first=2)
            sp.wait_ge(added, 16 * TILES)
            sp.dma_start(g.out.rearrange("b t d -> (b t) d"), g.acc[0:B * P, :]).then_inc(out_stored, 16)
            sp.wait_ge(out_stored, 16)

        @block.gpsimd
        def _(pool):
            nc.gpsimd.memset(zero[:], 0)
            pool.drain()

            def step(t):
                b = t.back(1)
                if b.on:
                    wait(pool, added, b, back=1, per=16)
                    wait(pool, y_ready, b)
                    nc.gpsimd.tensor_tensor(token[:, b.par, :], token_d[:, b.par, :], zero[:], ALU.add)
                    pool.drain()
                    nc.gpsimd.indirect_dma_start(g.acc, bass.IndirectOffsetOnAxis(ap=token[:, b.par, :], axis=0), y[:, b.par, :],
                                                 None, compute_op=ALU.add).then_inc(added, 16)
            steps(pool, step, 0, 1, count=TILES)

        @block.vector
        def _(dve):
            def step(t):
                if t.on:
                    wait_half(dve, row_loaded[t.par], t)
                    wait(dve, added, t, back=2, per=16)
                    nc.vector.tensor_copy(weight[:, t.par, :], row[:, t.par, D:D + 1])
                    nc.vector.tensor_copy(token_d[:, t.par, :], row[:, t.par, D + 1:]).then_inc(meta_ready, 1)
                    wait(dve, silu_ready, t)
                    wait(dve, h3_done, t)
                    wait(dve, h_turned, t, back=1)
                    nc.vector.tensor_tensor(hidden[:], silu[:], p3[:], ALU.mult).then_inc(hidden_ready, 1)
                b = t.back(1)
                if b.on:
                    wait(dve, y_done, b)
                    nc.vector.tensor_scalar(y[:, b.par, :], py[:, 0:D], weight[:, b.par, :], None, ALU.mult).then_inc(y_ready, 1)
            steps(dve, step, 0, 1, count=TILES)

        @block.scalar
        def _(act):
            def step(t):
                if t.on:
                    wait(act, h1_done, t)
                    wait(act, hidden_ready, t, back=1)
                    nc.scalar.activation(silu[:], p1[:], ACT.Silu).then_inc(silu_ready, 1)
                n = t.back(-1)
                if n.on:
                    wait(act, turned, n)
                    wait(act, h3_done, n, back=2)
                    for c in range(C):
                        last = nc.scalar.activation(xnT[:, n.par, c, :], turn[:, c * P:(c + 1) * P], ACT.Copy, scale=g.mo_norm[:, c:c + 1])
                    last.then_inc(xnT_ready, 1)
                if t.on:
                    wait(act, h_turned, t)
                    wait(act, y_done, t, back=1)
                    nc.scalar.activation(hT[:], phT[:], ACT.Copy).then_inc(hT_ready, 1)
            steps(act, step, 1, 1, count=TILES)

        @block.tensor
        def _(pe):
            pe.wait_ge(g.mo_loaded, 16 * g.mo_loads)

            def step(t):
                if t.on:
                    expert = pe.value_load(g.tile_expert[0:1, bass.ds(t.i, 1)], min_val=0, max_val=E - 1)
                    wait(pe, xnT_ready, t)
                    wait(pe, silu_ready, t, back=1)
                    for c in range(C):
                        last = nc.tensor.matmul(p1[:], xnT[:, t.par, c, :], g.mo_w1[:, bass.ds(expert, 1), c, :].rearrange("p e f -> p (e f)"), start=(c == 0), stop=(c == C - 1))
                    last.then_inc(h1_done, 1)
                    wait(pe, hidden_ready, t, back=1)
                    for c in range(C):
                        last = nc.tensor.matmul(p3[:], xnT[:, t.par, c, :], g.mo_w3[:, bass.ds(expert, 1), c, :].rearrange("p e f -> p (e f)"), start=(c == 0), stop=(c == C - 1))
                    last.then_inc(h3_done, 1)
                n = t.back(-1)
                if n.on:
                    wait_half(pe, row_loaded[n.par], n)
                    wait(pe, xnT_ready, n, back=1)
                    for c in range(C):
                        last = nc.tensor.transpose(turn[:, c * P:(c + 1) * P], row[:, n.par, c * P:(c + 1) * P], g.ident[:])
                    last.then_inc(turned, 1)
                b = t.back(1)
                if b.on:
                    expert = pe.value_load(g.tile_expert[0:1, bass.ds(b.i, 1)], min_val=0, max_val=E - 1)
                    wait(pe, hT_ready, b)
                    wait(pe, y_ready, b, back=1)
                    for f in range(4):
                        last = nc.tensor.matmul(py[:, 0:D], hT[:, f * P:(f + 1) * P], g.mo_w2[:, bass.ds(expert, 1), f, :].rearrange("p e d -> p (e d)"), start=(f == 0), stop=(f == 3))
                    last.then_inc(y_done, 1)
                if t.on:
                    wait(pe, hidden_ready, t)
                    wait(pe, hT_ready, t, back=1)
                    for f in range(4):
                        last = nc.tensor.transpose(phT[:, f * P:(f + 1) * P], hidden[:, f * P:(f + 1) * P], g.ident[:])
                    last.then_inc(h_turned, 1)
            steps(pe, step, 1, 1, count=TILES)


def constants():
    f = np.float32
    ident = np.eye(P, dtype=f)
    part = np.arange(P)
    quad = ((part[:, None] % 32) // 8 == np.arange(4)).astype(f)
    pair = ((part[:, None] % 32) // 16 == np.arange(2)).astype(f)
    pos = np.arange(P, dtype=f)

    def rope(base, d):
        half = d // 2
        if base == 10000.0:
            theta = f(base) ** (f(-2.0) * np.arange(half, dtype=f) / f(d))
        else:
            theta = f(1.0) / f(base) ** (np.arange(0, d, 2, dtype=f) / f(d))
        ang = (pos[:, None] * theta[None, :].astype(f)).astype(np.float64)
        cos, sin = np.cos(ang).astype(f), np.sin(ang).astype(f)
        return cos, np.stack([-sin, sin], axis=1)

    la_cos, la_sin = rope(10000.0, 16)
    ga_cos, ga_sin = rope(1000000.0, 128)
    lam = -(2.0 ** (-8.0 * (np.arange(16, dtype=f) + 1.0) / 16)).astype(f)
    diff = pos[None, :] - pos[:, None]
    decay = np.where(diff[:, None, :] >= 0, np.exp(np.minimum(lam[None, :, None] * diff[:, None, :], 0.0)), 0.0).astype(f)
    before = (part[:, None] < part[None, :]).astype(f)
    hidden = np.where(part[None, :] <= part[:, None], 0.0, -3e38).astype(f)
    return dict(ident=ident, quad=quad, pair=pair, la_cos=la_cos, la_sin=la_sin, la_decay=decay,
                ga_cosT=np.concatenate([ga_cos.T, ga_cos.T]), ga_sinT=ga_sin.reshape(P, P).T, before=before, hidden=hidden)


def chunked(w):
    return np.ascontiguousarray(w.reshape(-1, P, w.shape[-1]).transpose(1, 0, 2))


def layouts(i):
    k = constants()
    i = {n: np.asarray(a) for n, a in i.items()}
    kv = np.concatenate([i["L0_xattn_Wk"], i["L0_xattn_Wv"]], axis=0)
    ctx = i["ctx_2048"].reshape(B * P, D).T
    h = dict(
        x=i["x"].transpose(1, 0, 2), ctxT=chunked(ctx), ctxR=chunked(ctx)[::-1],
        ca_wq=chunked(i["L0_attn_Wq"]), ca_wk=chunked(i["L0_attn_Wk"]), ca_wv=chunked(i["L0_attn_Wv"]),
        ca_wo=chunked(i["L0_attn_Wo"]),
        xa_wq=chunked(i["L0_xattn_Wq"].T), xa_wk=chunked(kv[0::2].T), xa_wv=chunked(kv[1::2].T),
        ql_w=chunked(i["L0_ffn_weight"].T),
        la_wqk=chunked(np.concatenate([i["L1_attn_Wq"], i["L1_attn_Wk"]], axis=1)), la_wv=chunked(i["L1_attn_Wv"]),
        la_wo=chunked(i["L1_attn_Wo"]), la_wg1=chunked(i["L1_attn_Wg1"]), la_wg2=i["L1_attn_Wg2"],
        la_norm=i["L1_attn_norm_weight"].reshape(C, P).T,
        cv_taps=i["L1_xattn_ssm_kernel"], cv_skip=i["L1_xattn_D"][:, None],
        ga_norm=i["L1_ffn_norm1_w"].reshape(C, P).T, ga_wq=chunked(i["L1_ffn_wq"]), ga_wk=chunked(i["L1_ffn_wk"]),
        ga_wv=chunked(i["L1_ffn_wv"]), ga_wo=chunked(i["L1_ffn_wo"]),
        mo_norm=i["L1_ffn_norm2_w"].reshape(C, P).T, mo_gate=chunked(i["L1_ffn_gate_w"]),
        mo_w1=i["L1_ffn_w1"].reshape(8, C, P, 512).transpose(2, 0, 1, 3),
        mo_w3=i["L1_ffn_w3"].reshape(8, C, P, 512).transpose(2, 0, 1, 3),
        mo_w2=i["L1_ffn_w2"].reshape(8, 4, P, D).transpose(2, 0, 1, 3),
        expert_no=np.tile(np.arange(8, dtype=np.float32), (P, 1)),
        region_at=np.tile(np.arange(8, dtype=np.float32) * REGION, (P, 1)),
        tile_no=np.tile(np.arange(TILES, dtype=np.float32), (P, 1)),
        token_no=(np.arange(P)[:, None] + P * np.arange(B + 1)[None, :]).astype(np.float32), **k)
    return {n: np.ascontiguousarray(a) for n, a in h.items()}




def decoder(nc, h, out):
    with ExitStack() as ctx:
        g = allocate(nc, ctx, h)
        g.h, g.out = h, out
        allocate_moe(nc, g)
        load_first(nc, g, h)
        channel_attention(nc, g)
        cross_attention_and_quantised_linear(nc, g)
        linear_attention(nc, g)
        gated_convolution(nc, g)
        grouped_attention(nc, g)
        route(nc, g)
        experts(nc, g)


def kernel(**inputs):
    from concourse import bacc
    from concourse.bass_utils import run_bass_kernel_spmd as run

    nc = bacc.Bacc("TRN2", target_bir_lowering=False, num_devices=1)
    arrays = {f"in_{name}": a for name, a in layouts(inputs).items()}
    h = {name[3:]: nc.dram_tensor(name, a.shape, mybir.dt.from_np(a.dtype), kind="ExternalInput").ap() for name, a in arrays.items()}
    out = nc.dram_tensor("out_0", (B, P, D), F32, kind="ExternalOutput").ap()
    decoder(nc, h, out)
    r = run(nc, [arrays], core_ids=[0])
    return r.results[0]["out_0"]
```

```python
from contextlib import ExitStack

import numpy as np

import concourse.bass as bass
from concourse import mybir

F32 = mybir.dt.float32
BF16 = mybir.dt.bfloat16
I32 = mybir.dt.int32
ALU = mybir.AluOpType
ACT = mybir.ActivationFunctionType
AX = mybir.AxisListType

P = 128
B = 16
D = 256
C = D // P
LN_EPS = 1e-5


class At:

    def __init__(self, base, n, count=B):
        self.base, self.n, self.count = base, n, count
        self.par = n % 2
        self.i = n if base is None else base + n

    def back(self, k):
        return At(self.base, self.n - k, self.count)

    @property
    def on(self):
        return self.base is not None or 0 <= self.n < self.count


def wait(eng, sem, at, back=0, per=1, more=0):
    count = (at.i + (1 - back)) * per + more
    if at.base is not None or count > 0:
        eng.wait_ge(sem, count)


def wait_part(eng, sem, at, per, part):
    count = at.i * per + (part + 1)
    if at.base is not None or count > 0:
        eng.wait_ge(sem, count)


def wait_half(eng, sem, at):
    if at.base is None:
        eng.wait_ge(sem, 16 * (at.n // 2 + 1))
    else:
        eng.wait_ge(sem, at.i * 8 + (16 - 8 * at.par))


def steps(eng, emit, lead, lag, count=B, first=None):
    first = first or (lag + 3) // 2 * 2
    last = first + (count - lead - first) // 2 * 2
    for s in range(-lead, first):
        emit(At(None, s, count))
    with eng.Fori(first // 2, last // 2) as k:
        emit(At(2 * k, 0, count))
        emit(At(2 * k, 1, count))
    for s in range(last, count + lag):
        emit(At(None, s, count))


class Names:

    def __init__(self, nc, ctx, tag):
        self.nc, self.ctx, self.tag, self.sems = nc, ctx, tag, []

    def sb(self, name, shape, dt=F32):
        return self.ctx.enter_context(self.nc.sbuf_tensor(f"{self.tag}.{name}", shape, dt))

    def ps(self, name, shape, dt=F32):
        return self.ctx.enter_context(self.nc.psum_tensor(f"{self.tag}.{name}", shape, dt))

    def sem(self, name):
        self.sems.append(self.ctx.enter_context(self.nc.semaphore(f"{self.tag}.{name}")))
        return self.sems[-1]


def rsqrt_seed(nc, y, x):
    return nc.vector.tensor_scalar(y.bitcast(I32), x.bitcast(I32), -0.5, float(0x5F3759DF), ALU.mult, ALU.add)


def newton_rsqrt(nc, pool, y, x, t, n):
    for _ in range(n):
        nc.gpsimd.tensor_tensor(t, y, y, ALU.mult)
        pool.drain()
        nc.gpsimd.tensor_tensor(t, t, x, ALU.mult)
        pool.drain()
        nc.gpsimd.tensor_scalar(t, t, -0.5, 1.5, ALU.mult, ALU.add)
        pool.drain()
        last = nc.gpsimd.tensor_tensor(y, y, t, ALU.mult)
        pool.drain()
    return last


X_PARTS = (0, 1, 4, 16)


class Global:
    pass


def allocate(nc, ctx, h):
    g = Global()
    m = Names(nc, ctx, "g")
    g.x = m.sb("x", [P, B, D])
    g.ctxT = m.sb("ctxT", [P, C, B * P])
    g.ident = m.sb("ident", [P, P])
    g.ident_bf = m.sb("ident_bf", [P, P], BF16)
    g.minus_half = m.sb("minus_half", [P, 1])
    early = m.sb("early", [P, 12288])
    late = m.sb("late", [P, 8192])

    def cut(lo, c, n):
        return early[:, lo:lo + c * n].rearrange("p (c n) -> p c n", c=c), lo + c * n

    at = 0
    g.ca_wqk, at = cut(at, C, 2 * D)
    g.ca_wv, at = cut(at, C, D)
    g.ca_wo, at = cut(at, C, D)
    g.xa_wq, at = cut(at, C, D)
    g.xa_wk, at = cut(at, C, D)
    g.xa_wv, at = cut(at, C, D)
    g.ql_w, at = cut(at, C, D)
    g.la_wqk, at = cut(at, C, 2 * D)
    g.la_wv, at = cut(at, C, D)
    g.la_wo, at = cut(at, C, D)
    g.la_wg1, at = cut(at, C, 16)
    g.la_wg2, at = early[0:16, at:at + D], at + D
    g.la_norm, at = early[:, at:at + C], at + C
    g.la_decay, at = cut(at, 16, P)
    g.la_cos, at = early[:, at:at + 8], at + 8
    g.la_sin, at = cut(at, 2, 8)
    assert at <= 12288
    at = 2048
    g.ga_wq, at = cut(at, C, 2048)
    g.ga_wk, at = cut(at, C, 512)
    g.ga_wv, at = cut(at, C, 512)
    g.ga_wo, at = cut(at, 16, D)
    assert at <= 12288
    g.early, g.late = early, late
    g.hid = g.ctxT[:].rearrange("p c n -> p (c n)").rearrange("p (b d) -> p b d", b=B)
    g.spare = m.sb("spare", [P, 8192])
    g.cv_row = g.spare[0:16, 5120:5120 + 3 * P - 1]
    g.cv_skip = g.spare[0:16, 5119 + 3 * P:5120 + 3 * P]
    g.cv_rows = nc.dram_tensor("cv_rows", [16, 3 * P - 1], F32, kind="Internal").ap()
    g.cv_qT = late[:, 0:4096].rearrange("p (c b t) -> p c b t", c=C, b=B)
    g.xa_vd0 = g.spare[:, 0:4608].rearrange("p (g c) -> p g c", g=4)
    g.mo_w1 = g.spare[:].rearrange("p (e c f) -> p e c f", e=8, c=C)
    g.mo_w2 = late[:, 0:8192].rearrange("p (e f d) -> p e f d", e=8, f=4)
    g.mo_w3 = early[:, 0:8192].rearrange("p (e c f) -> p e c f", e=8, c=C)
    g.ga_norm, g.mo_norm = m.sb("ga_norm", [P, C]), m.sb("mo_norm", [P, C])
    g.ga_cosT, g.ga_sinT = m.sb("ga_cosT", [P, P]), m.sb("ga_sinT", [P, P])
    g.ga_hidden = m.sb("ga_hidden", [P, P])
    g.quad = m.sb("quad", [P, 4])
    g.pair = m.sb("pair", [P, 2])
    g.x_loaded = [m.sem(f"x_loaded{k}") for k in range(len(X_PARTS) - 1)]
    (g.ident_loaded, g.consts_loaded, g.ca_loaded, g.xa_loaded, g.la_loaded, g.ctx_loaded, g.ga_loaded,
     g.mo_loaded, g.fill) = map(m.sem, (
        "ident_loaded", "consts_loaded", "ca_loaded", "xa_loaded", "la_loaded", "ctx_loaded", "ga_loaded",
        "mo_loaded", "fill"))
    g.const_loads, g.ca_loads, g.xa_loads, g.la_loads = 1, 4, 4, 10
    g.ga_loads, g.mo_loads = 9, 3
    g.m = m
    return g


def load_first(nc, g, h):
    with nc.Block() as block:
        @block.sync
        def _(sp):
            for k in range(len(X_PARTS) - 1):
                part = slice(X_PARTS[k], X_PARTS[k + 1])
                sp.dma_start(g.x[:, part, :], h["x"][:, part, :]).then_inc(g.x_loaded[k], 16)

        @block.scalar
        def _(act):
            act.dma_start(g.ident[:], h["ident"]).then_inc(g.ident_loaded, 16)
            act.dma_start(g.ca_wqk[:, :, 0:D], h["ca_wq"]).then_inc(g.ca_loaded, 16)
            act.dma_start(g.ca_wqk[:, :, D:2 * D], h["ca_wk"]).then_inc(g.ca_loaded, 16)
            act.dma_start(g.ca_wv, h["ca_wv"]).then_inc(g.ca_loaded, 16)
            act.dma_start(g.ca_wo, h["ca_wo"]).then_inc(g.ca_loaded, 16)

        @block.gpsimd
        def _(pool):
            nc.gpsimd.memset(g.minus_half[:], -0.5).then_inc(g.fill, 1)
            nc.gpsimd.memset(g.xa_vd0, 0.0)
            pool.drain()
            nc.gpsimd.memset(g.xa_vd0.rearrange("p g (h c) -> p g h c", c=144)[:, :, :, 8:16], 1.0)
            pool.wait_ge(g.ident_loaded, 16)
            nc.gpsimd.tensor_copy(g.ident_bf[:], g.ident[:]).then_inc(g.fill, 1)


def layer_norm_stats(nc, m, x_b, par, eps_var_ready):
    dve = nc.vector
    nc.vector.bn_stats(m.stats[:, par, :], x_b)
    dve.drain()
    nc.vector.bn_aggr(m.mv[:, par, 0:2], m.stats[:, par, :])
    dve.drain()
    nc.vector.tensor_scalar(m.mv[:, par, 2:3], m.mv[:, par, 1:2], LN_EPS, None, ALU.add).then_inc(eps_var_ready, 1)


def layer_norm_apply(nc, m, out, x_b, par):
    return nc.vector.tensor_scalar(out, x_b, m.mv[:, par, 0:1], m.rstd[:, par, 0:1], ALU.subtract, ALU.mult)


def channel_attention(nc, g):
    with ExitStack() as ctx:
        m = Names(nc, ctx, "ca")
        xn = m.sb("xn", [P, 2, D])
        m.stats, m.mv, m.rstd = m.sb("stats", [P, 2, 6]), m.sb("mv", [P, 2, 3]), m.sb("rstd", [P, 2, 1])
        xnT = m.sb("xnT", [P, 2, C, P])
        qk = m.sb("qk", [P, 2, 2 * D])
        vT = m.sb("vT", [P, 2, C, P])
        w = m.sb("w", [P, 2, C, D])
        negmax, rowsum = m.sb("negmax", [P, 2, C]), m.sb("rowsum", [P, 2, C])
        wo = m.sb("wo", [P, 2, C, D])
        mix = m.sb("mix", [P, 2, C, D])
        turn = m.ps("turn", [P, 512])
        pqk = m.ps("pqk", [P, 2 * D])
        pv = m.ps("pv", [P, 512])
        psc = m.ps("psc", [P, C, D])
        pmix = m.ps("pmix", [P, C, D])
        pout = m.ps("pout", [P, 512])
        (var_ready, rstd_ready, xn_ready, turned, xnT_ready, qk_done, qk_ready, vT_done, vT_ready, scores_done,
         max_ready, w_ready, wo_ready, mix_done, mix_ready, out_done, x_added) = map(m.sem, (
            "var_ready", "rstd_ready", "xn_ready", "turned", "xnT_ready", "qk_done", "qk_ready", "vT_done",
            "vT_ready", "scores_done", "max_ready", "w_ready", "wo_ready", "mix_done", "mix_ready", "out_done",
            "x_added"))
        g.finished = m.sems
        scale = 8 ** -0.5
        block = ctx.enter_context(nc.Block())

        @block.sync
        def _(sp):
            h = g.h
            sp.dma_start(g.quad[:], h["quad"]).then_inc(g.consts_loaded, 16)
            sp.dma_start(g.xa_wq, h["xa_wq"]).then_inc(g.xa_loaded, 16)
            sp.dma_start(g.xa_wk, h["xa_wk"]).then_inc(g.xa_loaded, 16)
            sp.dma_start(g.xa_wv, h["xa_wv"]).then_inc(g.xa_loaded, 16)
            sp.dma_start(g.ql_w, h["ql_w"]).then_inc(g.xa_loaded, 16)
            for name, to in (("la_wqk", g.la_wqk), ("la_wv", g.la_wv), ("la_wo", g.la_wo), ("la_wg1", g.la_wg1),
                             ("la_wg2", g.la_wg2), ("la_norm", g.la_norm), ("la_decay", g.la_decay), ("la_cos", g.la_cos),
                             ("la_sin", g.la_sin), ("pair", g.pair[:])):
                sp.dma_start(to, h[name]).then_inc(g.la_loaded, 16)
            sp.dma_start(g.ctxT[:], h["ctxR"]).then_inc(g.ctx_loaded, 16)

        @block.gpsimd
        def _(pool):
            def step(s):
                b = s.back(-2)
                if b.on:
                    wait(pool, var_ready, b)
                    wait(pool, xn_ready, b, back=2)
                    nc.gpsimd.tensor_tensor(m.rstd[:, b.par, :], m.mv[:, b.par, 2:3], g.minus_half[:],
                                            ALU.pow).then_inc(rstd_ready, 1)
            steps(pool, step, 2, 2)

        @block.vector
        def _(dve):
            def step(s):
                b = s.back(2)
                if b.on:
                    wait(dve, out_done, b)
                    nc.vector.tensor_tensor(g.x[:, b.i, :], pout[:, 0:D], g.x[:, b.i, :], ALU.add).then_inc(x_added, 1)
                b = s.back(1)
                if b.on:
                    wait(dve, scores_done, b)
                    nc.vector.tensor_reduce(negmax[:, b.par, :], psc[:], AX.X, ALU.max)
                    dve.drain()
                    nc.vector.tensor_scalar(negmax[:, b.par, :], negmax[:, b.par, :], -scale, None,
                                            ALU.mult).then_inc(max_ready, 1)
                b = s.back(-1)
                if b.on:
                    wait(dve, rstd_ready, b)
                    wait(dve, turned, b, back=2)
                    layer_norm_apply(nc, m, xn[:, b.par, :], g.x[:, b.i, :], b.par).then_inc(xn_ready, 1)
                b = s.back(1)
                if b.on:
                    wait(dve, w_ready, b)
                    nc.vector.reciprocal(rowsum[:, b.par, :], rowsum[:, b.par, :])
                    dve.drain()
                    wait(dve, mix_done, b, back=2)
                    for c in range(C):
                        last = nc.vector.tensor_scalar(wo[:, b.par, c, :], g.ca_wo[:, c, :], rowsum[:, b.par, c:c + 1],
                                                       None, ALU.mult)
                    last.then_inc(wo_ready, 1)
                b = s.back(-2)
                if b.on and b.base is None and b.n in X_PARTS:
                    dve.wait_ge(g.x_loaded[X_PARTS.index(b.n)], 16)
                if b.on:
                    wait(dve, xn_ready, b, back=2)
                    layer_norm_stats(nc, m, g.x[:, b.i, :], b.par, var_ready)
                if s.on:
                    wait(dve, vT_done, s)
                    wait(dve, out_done, s, back=2)
                    nc.vector.tensor_copy(vT[:, s.par, :, :], pv[:, 0:D]).then_inc(vT_ready, 1)
            steps(dve, step, 2, 2)

        @block.scalar
        def _(act):
            def step(s):
                if s.on:
                    wait(act, turned, s)
                    wait(act, vT_done, s, back=2)
                    nc.scalar.activation(xnT[:, s.par, :, :], turn[:, 0:D], ACT.Copy).then_inc(xnT_ready, 1)
                b = s.back(1)
                if b.on:
                    wait(act, max_ready, b)
                    wait(act, mix_done, b, back=2)
                    for c in range(C):
                        last = nc.scalar.activation(w[:, b.par, c, :], psc[:, c, :], ACT.Exp, bias=negmax[:, b.par, c:c + 1],
                                                    scale=scale, accum_out=rowsum[:, b.par, c:c + 1])
                    last.then_inc(w_ready, 1)
                if s.on:
                    wait(act, qk_done, s)
                    wait(act, scores_done, s, back=2)
                    nc.scalar.activation(qk[:, s.par, :], pqk[:], ACT.Copy).then_inc(qk_ready, 1)
                if b.on:
                    wait(act, mix_done, b)
                    wait(act, out_done, b, back=2)
                    nc.scalar.activation(mix[:, b.par, :, :], pmix[:], ACT.Copy).then_inc(mix_ready, 1)
            steps(act, step, 0, 2)

        @block.tensor
        def _(pe):
            pe.wait_ge(g.ident_loaded, 16)
            pe.wait_ge(g.ca_loaded, 16 * g.ca_loads)

            def step(s):
                if s.on:
                    wait(pe, xn_ready, s)
                    wait(pe, xnT_ready, s, back=1)
                    for c in range(C):
                        last = nc.tensor.transpose(turn[:, c * P:(c + 1) * P], xn[:, s.par, c * P:(c + 1) * P], g.ident[:])
                    last.then_inc(turned, 1)
                b = s.back(1)
                if b.on:
                    wait(pe, qk_ready, b)
                    wait(pe, w_ready, b, back=1)
                    for c in range(C):
                        last = nc.tensor.matmul(psc[:, c, :], qk[:, b.par, c * P:(c + 1) * P], qk[:, b.par, D:2 * D],
                                                start=True, stop=True)
                    last.then_inc(scores_done, 1)
                b = s.back(2)
                if b.on:
                    wait(pe, mix_ready, b)
                    wait(pe, vT_ready, b)
                    wait(pe, x_added, b, back=1)
                    for c in range(C):
                        last = nc.tensor.matmul(pout[:, 0:D], vT[:, b.par, c, :], mix[:, b.par, c, :],
                                                start=(c == 0), stop=(c == C - 1))
                    last.then_inc(out_done, 1)
                if s.on:
                    wait(pe, xnT_ready, s)
                    wait(pe, qk_ready, s, back=1)
                    for c in range(C):
                        last = nc.tensor.matmul(pqk[:], xnT[:, s.par, c, :], g.ca_wqk[:, c, :], start=(c == 0), stop=(c == C - 1))
                    last.then_inc(qk_done, 1)
                    wait(pe, vT_ready, s, back=1)
                    for f in range(C):
                        for c in range(C):
                            last = nc.tensor.matmul(pv[:, f * P:(f + 1) * P], g.ca_wv[:, c, f * P:(f + 1) * P],
                                                    xnT[:, s.par, c, :], start=(c == 0), stop=(c == C - 1))
                    last.then_inc(vT_done, 1)
                b = s.back(1)
                if b.on:
                    wait(pe, wo_ready, b)
                    wait(pe, mix_ready, b, back=1)
                    for f in range(C):
                        for c in range(C):
                            last = nc.tensor.matmul(pmix[:, f, :], w[:, b.par, c, f * P:(f + 1) * P], wo[:, b.par, c, :],
                                                    start=(c == 0), stop=(c == C - 1))
                    last.then_inc(mix_done, 1)
            steps(pe, step, 0, 2)


def spread(ap, axis, n):
    v = ap.unsqueeze(axis)
    shape = list(v.shape)
    shape[axis] = n
    return v.broadcast_to(shape)


MAGIC = 12582912.0
Q_MAX = 127.0


def cross_attention_and_quantised_linear(nc, g):
    H, HD = 32, 8
    with ExitStack() as ctx:
        m = Names(nc, ctx, "xa")
        xn = m.sb("xn", [P, 2, D])
        m.stats, m.mv, m.rstd = m.sb("stats", [P, 2, 6]), m.sb("mv", [P, 2, 3]), m.sb("rstd", [P, 2, 1])
        xnT = m.sb("xnT", [P, 2, C, P])
        ctxT = m.sb("ctxT", [P, 2, C, P])
        ctx_loaded = [m.sem(f"ctx_loaded{i}") for i in range(2)]
        sq = m.sb("sq", [P, 2 * D])
        msq, norm, work = m.sb("msq", [P, 2 * H]), m.sb("norm", [P, 2, 2 * H]), m.sb("work", [P, 2 * H])
        qkn = m.sb("qkn", [P, 2, 2 * D])
        kT = m.sb("kT", [P, 2, C, P])
        qT = m.sb("qT", [P, 2, C, 4, P])
        vd = [g.xa_vd0, m.sb("vd1", [P, 4, 8 * 144])[:]]
        oT = m.sb("oT", [P, 4, P])
        e = [g.late[:, n * 4096:(n + 1) * 4096].rearrange("p (h n) -> p h n", h=H) for n in range(2)]
        inv = m.sb("inv", [P, 2, H])
        o = m.sb("o", [P, 2, D])
        n = Names(nc, ctx, "ql")
        yn = n.sb("xn", [P, D])
        n.stats, n.mv, n.rstd = n.sb("stats", [P, 2, 6]), n.sb("mv", [P, 2, 3]), n.sb("rstd", [P, 2, 1])
        amax, q_scale = n.sb("amax", [P, 2, 1]), n.sb("q_scale", [P, 2, 1])
        deq = n.sb("deq", [P, 2, 1])
        rounded = n.sb("rounded", [P, D])
        xq = n.sb("xq", [P, 2, D], BF16)
        xqT = n.sb("xqT", [P, 2, C, P], BF16)
        wq = n.sb("wq", [P, C, D], BF16)
        w_sum, w_all, w_scale = n.sb("w_sum", [P, 1]), n.sb("w_all", [P, 1]), n.sb("w_scale", [P, 4])
        ones = n.sb("ones", [P, P])
        magic = n.sb("magic", [P, 1])
        w_tmp = g.spare[:, 4608:4608 + C * D].rearrange("p (c n) -> p c n", c=C)
        turn, turn2 = m.ps("turn", [P, 512]), m.ps("turn2", [P, 2, C, P])
        pv = turn[:, D:2 * D]
        pqk, po, pot = m.ps("pqk", [P, 2 * D]), m.ps("po", [P, 4, P]), m.ps("pot", [P, 4, P])
        ps = m.ps("ps", [P, 2, 512])
        pc = m.ps("pc", [P, 512])
        pcT = pc[:, 0:P].bitcast(BF16)
        pov = pot[:].rearrange("p g (h t d) -> p (g h) t d", h=8, t=2)
        (var_ready, rstd_ready, xn_ready, turned, xnT_ready, qk_done, sq_ready, v_done, v_ready, msq_ready, norm_ready,
         qk_ready, qk_turned, kT_ready, qT_ready, scores_done, exp_done, pv_done, oT_ready, o_turned, o_ready, x_added) = map(m.sem, (
            "var_ready", "rstd_ready", "xn_ready", "turned", "xnT_ready", "qk_done", "sq_ready", "v_done", "v_ready",
            "msq_ready", "norm_ready", "qk_ready", "qk_turned", "kT_ready", "qT_ready", "scores_done",
            "exp_done", "pv_done", "oT_ready", "o_turned", "o_ready", "x_added"))
        (q_var_ready, q_rstd_ready, rounded_ready, xq_ready, xq_turned, xqT_ready,
         y_done, y_added, w_sum_ready, wq_ready, filled, vd_filled) = map(n.sem, (
            "var_ready", "rstd_ready", "rounded_ready", "xq_ready", "xq_turned",
            "xqT_ready", "y_done", "y_added", "w_sum_ready", "wq_ready", "filled", "vd_filled"))
        block = ctx.enter_context(nc.Block())

        @block.sync
        def _(sp):
            def step(s):
                if s.on:
                    wait(sp, v_done, s, back=2)
                    sp.dma_start(ctxT[:, s.par, :, :], g.h["ctxT"][:, :, bass.ts(s.i, P)]).then_inc(ctx_loaded[s.par], 16)
            steps(sp, step, 0, 0, first=2)

        @block.gpsimd
        def _(pool):
            for sem in g.finished:
                nc.gpsimd.sem_clear(sem)
            nc.gpsimd.memset(ones[:], 1.0).then_inc(filled, 1)
            nc.gpsimd.memset(magic[:], MAGIC).then_inc(filled, 1)
            pool.wait_ge(filled, 2)

            def step(s):
                c = s.back(3)
                if c.on:
                    wait(pool, q_var_ready, c)
                    nc.gpsimd.tensor_tensor(n.rstd[:, c.par, :], n.mv[:, c.par, 2:3], g.minus_half[:],
                                            ALU.pow).then_inc(q_rstd_ready, 1)
                if s.on:
                    wait(pool, msq_ready, s)
                    newton_rsqrt(nc, pool, norm[:, s.par, :], msq[:], work[:], 3).then_inc(norm_ready, 1)
                b = s.back(-2)
                if b.on:
                    wait(pool, var_ready, b)
                    wait(pool, xn_ready, b, back=2)
                    nc.gpsimd.tensor_tensor(m.rstd[:, b.par, :], m.mv[:, b.par, 2:3], g.minus_half[:],
                                            ALU.pow).then_inc(rstd_ready, 1)
                if c.on:
                    wait(pool, rounded_ready, c)
                    wait(pool, xq_turned, c, back=2)
                    nc.gpsimd.tensor_tensor(xq[:, c.par, :], rounded[:], magic[:].broadcast_to([P, D]), ALU.subtract).then_inc(xq_ready, 1)
                b = s.back(2)
                if b.on:
                    wait(pool, o_ready, b)
                    nc.gpsimd.tensor_tensor(g.x[:, b.i, :], g.x[:, b.i, :], o[:, b.par, :], ALU.add).then_inc(x_added, 1)
            steps(pool, step, 2, 4)

        @block.vector
        def _(dve):
            dve.wait_ge(g.consts_loaded, 16 * g.const_loads)

            def fill_vd1():
                nc.vector.memset(vd[1], 0.0)
                dve.drain()
                nc.vector.memset(vd[1].rearrange("p g (h c) -> p g h c", c=144)[:, :, :, 8:16], 1.0).then_inc(vd_filled, 1)

            def quantise_weight():
                dve.wait_ge(g.xa_loaded, 16 * g.xa_loads)
                nc.vector.tensor_reduce(w_sum[:], g.ql_w, AX.XY, ALU.add, apply_absolute_value=True).then_inc(w_sum_ready, 1)
                dve.wait_ge(w_sum_ready, 2)
                nc.vector.tensor_scalar(w_scale[:, 0:1], pc[:, 0:1], 1.0 / (D * D), 1e-6, ALU.mult, ALU.max)
                dve.drain()
                nc.vector.reciprocal(w_scale[:, 1:2], w_scale[:, 0:1])
                dve.drain()
                nc.vector.tensor_scalar(w_tmp, g.ql_w, w_scale[:, 1:2], MAGIC, ALU.mult, ALU.add)
                dve.drain()
                nc.vector.tensor_scalar(w_tmp, w_tmp, MAGIC + 1.0, MAGIC - 1.0, ALU.min, ALU.max)
                dve.drain()
                nc.vector.tensor_scalar(wq[:], w_tmp, -MAGIC, None, ALU.add).then_inc(wq_ready, 1)
                nc.vector.tensor_scalar(w_scale[:, 2:3], w_scale[:, 0:1], 1.0 / Q_MAX, None, ALU.mult)

            def step(s):
                if s.base is None and s.n == 0:
                    fill_vd1()
                if s.base is None and s.n == 2:
                    quantise_weight()
                b = s.back(1)
                if b.on:
                    wait(dve, qk_turned, b)
                    wait(dve, scores_done, b, back=2, per=8)
                    for k in range(C):
                        last = nc.vector.tensor_tensor(qT[:, b.par, k, :, :], spread(turn2[:, 0, k, :], 1, 4),
                                                       spread(g.quad[:], 2, P), ALU.mult)
                    last.then_inc(qT_ready, 1)
                c = s.back(4)
                if c.on:
                    wait(dve, y_done, c)
                    nc.vector.scalar_tensor_tensor(out=g.x[:, c.i, :], in0=pc[:, D:2 * D], scalar=deq[:, c.par, :],
                                                   in1=g.x[:, c.i, :], op0=ALU.mult, op1=ALU.add).then_inc(y_added, 1)
                c = s.back(3)
                if c.on:
                    wait(dve, x_added, c)
                    layer_norm_stats(nc, n, g.x[:, c.i, :], c.par, q_var_ready)
                b = s.back(-1)
                if b.on:
                    wait(dve, rstd_ready, b)
                    wait(dve, turned, b, back=2)
                    layer_norm_apply(nc, m, xn[:, b.par, :], g.x[:, b.i, :], b.par).then_inc(xn_ready, 1)
                if c.on:
                    wait(dve, q_rstd_ready, c)
                    layer_norm_apply(nc, n, yn[:], g.x[:, c.i, :], c.par)
                    dve.drain()
                    nc.vector.tensor_reduce(amax[:, c.par, :], yn[:], AX.X, ALU.max, apply_absolute_value=True)
                    dve.drain()
                    nc.vector.tensor_scalar(amax[:, c.par, :], amax[:, c.par, :], 1e-8, None, ALU.max)
                    dve.drain()
                    nc.vector.tensor_scalar(deq[:, c.par, :], amax[:, c.par, :], w_scale[:, 2:3], None, ALU.mult)
                    nc.vector.reciprocal(q_scale[:, c.par, :], amax[:, c.par, :])
                    dve.drain()
                    nc.vector.tensor_scalar(q_scale[:, c.par, :], q_scale[:, c.par, :], Q_MAX, None, ALU.mult)
                    dve.drain()
                if s.on:
                    wait(dve, sq_ready, s)
                    wait(dve, norm_ready, s, back=1)
                    nc.vector.tensor_reduce(msq[:], sq[:].rearrange("p (h d) -> p h d", d=HD), AX.X, ALU.add)
                    dve.drain()
                    nc.vector.tensor_scalar(msq[:], msq[:], 1.0 / HD, 1e-6, ALU.mult, ALU.add)
                    dve.drain()
                    wait(dve, qk_ready, s, back=2)
                    rsqrt_seed(nc, norm[:, s.par, :], msq[:]).then_inc(msq_ready, 1)
                b = s.back(-2)
                if b.on:
                    wait(dve, xn_ready, b, back=2)
                    layer_norm_stats(nc, m, g.x[:, b.i, :], b.par, var_ready)
                if c.on:
                    nc.vector.tensor_scalar(yn[:], yn[:], q_scale[:, c.par, :], MAGIC, ALU.mult, ALU.add)
                    dve.drain()
                    wait(dve, xq_ready, c, back=1)
                    nc.vector.tensor_scalar(rounded[:], yn[:], MAGIC + Q_MAX, MAGIC - Q_MAX, ALU.min,
                                            ALU.max).then_inc(rounded_ready, 1)
                if s.on:
                    wait(dve, norm_ready, s)
                    wait(dve, qk_turned, s, back=2)
                    nc.vector.tensor_tensor(qkn[:, s.par, :].rearrange("p (h d) -> p h d", d=HD),
                                            pqk[:].rearrange("p (h d) -> p h d", d=HD),
                                            spread(norm[:, s.par, :], 2, HD), ALU.mult).then_inc(qk_ready, 1)
                b = s.back(2)
                if b.on:
                    wait(dve, o_turned, b)
                    nc.vector.reciprocal(inv[:, b.par, :], pov[:, :, 1, 0])
                    dve.drain()
                    wait(dve, x_added, b, back=2)
                    nc.vector.tensor_tensor(o[:, b.par, :].rearrange("p (h d) -> p h d", h=H), pov[:, :, 0, :],
                                            spread(inv[:, b.par, :], 2, HD), ALU.mult).then_inc(o_ready, 1)
            steps(dve, step, 2, 4)

        @block.scalar
        def _(act):

            def step(s):
                c = s.back(4)
                if c.on:
                    wait(act, xq_turned, c)
                    wait(act, y_done, c, back=2)
                    nc.scalar.activation(xqT[:, c.par, :, :], pcT, ACT.Copy).then_inc(xqT_ready, 1)
                if s.on:
                    wait(act, turned, s)
                    wait(act, qk_done, s, back=2)
                    nc.scalar.activation(xnT[:, s.par, :, :], turn[:, 0:D], ACT.Copy).then_inc(xnT_ready, 1)
                b = s.back(1)
                if b.on:
                    wait(act, qk_turned, b)
                    wait(act, qT_ready, b)
                    wait(act, scores_done, b, back=2, per=8)
                    nc.scalar.activation(kT[:, b.par, :, :], turn2[:, 1, :, :], ACT.Copy).then_inc(kT_ready, 1)
                if s.on:
                    wait(act, qk_done, s)
                    wait(act, msq_ready, s, back=1)
                    nc.scalar.activation(sq[:], pqk[:], ACT.Square).then_inc(sq_ready, 1)
                if b.on:
                    wait(act, pv_done, b, back=2)
                    for r in range(8):
                        wait(act, scores_done, b, back=1, per=8, more=r + 1)
                        nc.scalar.activation(e[b.par][:, 4 * r:4 * r + 4, :], ps[:, r % 2, :], ACT.Exp,
                                             scale=HD ** -0.5).then_inc(exp_done, 1)
                a = s.back(2)
                if a.on:
                    wait(act, pv_done, a)
                    wait(act, o_turned, a, back=1)
                    nc.scalar.activation(oT[:], po[:], ACT.Copy).then_inc(oT_ready, 1)
                if s.on:
                    if s.base is None and s.n == 1:
                        act.wait_ge(vd_filled, 1)
                    wait(act, v_done, s)
                    wait(act, pv_done, s, back=2)
                    nc.scalar.activation(vd[s.par].rearrange("p g (h c) -> p g h c", c=144)[:, :, :, 0:HD],
                                         pv.rearrange("p (g h d) -> p g h d", g=4, h=8), ACT.Copy).then_inc(v_ready, 1)
            steps(act, step, 0, 4)

        @block.tensor
        def _(pe):
            pe.wait_ge(g.xa_loaded, 16 * g.xa_loads)

            def sum_weight():
                pe.wait_ge(w_sum_ready, 1)
                pe.wait_ge(filled, 1)
                nc.tensor.matmul(pc[:, 0:1], ones[:], w_sum[:], start=True, stop=True).then_inc(w_sum_ready, 1)

            def step(s):
                if s.base is None and s.n == 2:
                    sum_weight()
                c = s.back(4)
                if c.on:
                    wait(pe, xq_ready, c)
                    wait(pe, y_added, c, back=1)
                    for k in range(C):
                        last = nc.tensor.transpose(pcT[:, k * P:(k + 1) * P], xq[:, c.par, k * P:(k + 1) * P], g.ident_bf[:])
                    last.then_inc(xq_turned, 1)
                b = s.back(1)
                if b.on:
                    wait(pe, qk_ready, b)
                    wait(pe, kT_ready, b, back=1)
                    wait(pe, qT_ready, b, back=1)
                    for t in range(2):
                        for k in range(C):
                            last = nc.tensor.transpose(turn2[:, t, k, :], qkn[:, b.par, t * D + k * P:t * D + (k + 1) * P], g.ident[:])
                    last.then_inc(qk_turned, 1)
                if s.on:
                    wait(pe, xn_ready, s)
                    wait(pe, v_ready, s, back=1)
                    for k in range(C):
                        last = nc.tensor.transpose(turn[:, k * P:(k + 1) * P], xn[:, s.par, k * P:(k + 1) * P], g.ident[:])
                    last.then_inc(turned, 1)
                if c.on:
                    wait(pe, xqT_ready, c)
                    if c.base is None and c.n == 0:
                        pe.wait_ge(wq_ready, 1)
                    for k in range(C):
                        last = nc.tensor.matmul(pc[:, D:2 * D], xqT[:, c.par, k, :], wq[:, k, :], start=(k == 0), stop=(k == C - 1))
                    last.then_inc(y_done, 1)
                if s.on:
                    wait(pe, xnT_ready, s)
                    wait_half(pe, ctx_loaded[s.par], s)
                    wait(pe, qk_ready, s, back=1)
                    for to, lhs, w in ((pqk[:, 0:D], lambda k: xnT[:, s.par, k, :], g.xa_wq),
                                       (pqk[:, D:2 * D], lambda k: ctxT[:, s.par, k, :], g.xa_wk)):
                        for k in range(C):
                            last = nc.tensor.matmul(to, lhs(k), w[:, k, :], start=(k == 0), stop=(k == C - 1))
                    last.then_inc(qk_done, 1)
                a = s.back(2)
                if b.on:
                    wait(pe, kT_ready, b)
                    wait(pe, qT_ready, b)
                if a.on:
                    wait(pe, exp_done, a, per=8)
                    wait(pe, oT_ready, a, back=1)
                for r in range(8):
                    if b.on:
                        k, rows = r // 4, slice(32 * (r % 4), 32 * (r % 4) + 32)
                        wait(pe, exp_done, b, back=1, per=8, more=r - 1)
                        nc.tensor.matmul(ps[:, r % 2, :], kT[rows, b.par, k, :], qT[rows, b.par, k, :, :],
                                         start=True, stop=True).then_inc(scores_done, 1)
                    if a.on:
                        for t in range(4 * r, 4 * r + 4):
                            gr, hh = t // 8, t % 8
                            last = nc.tensor.matmul(po[:, gr, :], vd[a.par][:, gr, hh * P:(hh + 1) * P], e[a.par][:, t, :],
                                                    start=(hh == 0), stop=(hh == 7))
                if a.on:
                    last.then_inc(pv_done, 1)
                if s.on:
                    for k in range(C):
                        last = nc.tensor.matmul(pv, ctxT[:, s.par, k, :], g.xa_wv[:, k, :], start=(k == 0), stop=(k == C - 1))
                    last.then_inc(v_done, 1)
                if a.on:
                    wait(pe, oT_ready, a)
                    wait(pe, o_ready, a, back=1)
                    for k in range(4):
                        last = nc.tensor.transpose(pot[:, k, :], oT[:, k, :], g.ident[:])
                    last.then_inc(o_turned, 1)
            steps(pe, step, 0, 4)


def linear_attention(nc, g):
    H, HD = 16, 16
    with ExitStack() as ctx:
        m = Names(nc, ctx, "la")
        xn = m.sb("xn", [P, 2, D])
        m.stats, m.mv, m.rstd = m.sb("stats", [P, 2, 6]), m.sb("mv", [P, 2, 3]), m.sb("rstd", [P, 2, 1])
        xnT = m.sb("xnT", [P, 2, C, P])
        sigm = m.sb("sigm", [P, 2 * D])
        qk = m.sb("qk", [P, 2 * D])
        by_cos, by_sin = m.sb("by_cos", [P, 2 * D]), m.sb("by_sin", [P, 2 * D])
        qkr = m.sb("qkr", [P, 2, 2 * D])
        kT = m.sb("kT", [P, 2, C, P])
        qT = m.sb("qT", [P, 2, C, 2, P])
        vd = [m.sb(f"vd{k}", [P, 2, 8 * 144]) for k in range(2)]
        g1T = m.sb("g1T", [16, P])
        gate = m.sb("gate", [P, 2, D])
        a_mat = [g.late[:, 4096 + k * 2048:4096 + (k + 1) * 2048].rearrange("p (h t) -> p h t", h=H) for k in range(2)]
        oT = m.sb("oT", [P, C, P])
        u, usq = m.sb("u", [P, D]), m.sb("usq", [P, D])
        msq, norm, work = m.sb("msq", [P, H]), m.sb("norm", [P, H]), m.sb("work", [P, H])
        un, unT = m.sb("un", [P, D]), m.sb("unT", [P, C, P])
        n2 = Names(nc, ctx, "cn")
        n2.stats, n2.mv, n2.rstd = n2.sb("stats", [P, 2, 6]), n2.sb("mv", [P, 2, 3]), n2.sb("rstd", [P, 2, 1])
        xn2 = n2.sb("xn", [P, D])
        (var2_ready, rstd2_ready, xn2_ready, turned2, qT2_ready, zero_ready, taps_loaded, row_ready, row_stored) = map(n2.sem, (
            "var_ready", "rstd_ready", "xn_ready", "turned", "qT_ready", "zero_ready", "taps_loaded", "row_ready", "row_stored"))
        turn, turn2 = m.ps("turn", [P, 512]), m.ps("turn2", [P, 2, C, P])
        pqk, pvx, po, pot = m.ps("pqk", [P, 2 * D]), m.ps("pvx", [P, 512]), m.ps("po", [P, 512]), m.ps("pot", [P, 512])
        pv, pout = pvx[:, 0:D], pvx[:, D:2 * D]
        px2 = pot[:, D:2 * D]
        ps = m.ps("ps", [P, 2, 512])
        pon, pun = pot[:, 0:D], ps[:, 0, 0:D]
        (var_ready, rstd_ready, xn_ready, turned, xnT_ready, qk_done, sigm_ready, silu_ready, v_done, v_ready, g1_done, g1_ready,
         gate_done, gate_ready, rot_ready, qk_ready, qk_turned, kT_ready, qT_ready, scores_done, a_ready, av_done,
         oT_ready, o_turned, u_ready, usq_ready, msq_ready, norm_ready, un_ready, un_turned, unT_ready, out_done,
         x_added, filled) = map(m.sem, (
            "var_ready", "rstd_ready", "xn_ready", "turned", "xnT_ready", "qk_done", "sigm_ready", "silu_ready", "v_done", "v_ready",
            "g1_done", "g1_ready", "gate_done", "gate_ready", "rot_ready", "qk_ready", "qk_turned", "kT_ready",
            "qT_ready", "scores_done", "a_ready", "av_done", "oT_ready", "o_turned", "u_ready", "usq_ready",
            "msq_ready", "norm_ready", "un_ready", "un_turned", "unT_ready", "out_done", "x_added", "filled"))
        block = ctx.enter_context(nc.Block())

        @block.sync
        def _(sp):
            sp.wait_ge(zero_ready, 1)
            sp.dma_start(g.cv_row[:, P - 1:], g.h["cv_taps"]).then_inc(taps_loaded, 16)
            sp.dma_start(g.cv_skip, g.h["cv_skip"]).then_inc(taps_loaded, 16)
            sp.wait_ge(row_ready, 1)
            sp.dma_start(g.cv_rows, g.cv_row).then_inc(row_stored, 16)
            sp.wait_ge(row_stored, 16)

        @block.gpsimd
        def _(pool):
            nc.gpsimd.memset(g.cv_row[:, 0:P - 1], 0.0).then_inc(zero_ready, 1)
            for k in range(2):
                nc.gpsimd.memset(vd[k][:], 0.0).then_inc(filled, 1)

            def step(s):
                a = s.back(2)
                if a.on:
                    wait(pool, u_ready, a)
                    nc.gpsimd.tensor_tensor(usq[:], u[:], u[:], ALU.mult).then_inc(usq_ready, 1)
                c = s.back(3)
                if c.on:
                    wait(pool, var2_ready, c)
                    nc.gpsimd.tensor_tensor(n2.rstd[:, c.par, :], n2.mv[:, c.par, 2:3], g.minus_half[:],
                                            ALU.pow).then_inc(rstd2_ready, 1)
                if a.on:
                    wait(pool, msq_ready, a)
                    newton_rsqrt(nc, pool, norm[:], msq[:], work[:], 3).then_inc(norm_ready, 1)
                if s.on:
                    wait(pool, rot_ready, s)
                    wait(pool, qk_turned, s, back=2)
                    nc.gpsimd.tensor_tensor(qkr[:, s.par, :], by_cos[:], by_sin[:], ALU.add).then_inc(qk_ready, 1)
                b = s.back(-2)
                if b.on:
                    wait(pool, var_ready, b)
                    wait(pool, xn_ready, b, back=2)
                    nc.gpsimd.tensor_tensor(m.rstd[:, b.par, :], m.mv[:, b.par, 2:3], g.minus_half[:],
                                            ALU.pow).then_inc(rstd_ready, 1)
            steps(pool, step, 2, 3)

        @block.vector
        def _(dve):
            dve.wait_ge(g.la_loaded, 16 * g.la_loads)
            for c in range(C):
                last = nc.vector.tensor_scalar(g.la_wo[:, c, :], g.la_wo[:, c, :], g.la_norm[:, c:c + 1], None, ALU.mult)
            last.then_inc(filled, 1)

            def decay(b, r):
                wait(dve, scores_done, b, back=1, per=4, more=r + 1)
                heads = lambda w: w.rearrange("p (k h) t -> p k h t", k=C)[:, :, 2 * r:2 * r + 2, :]
                nc.vector.tensor_tensor(heads(a_mat[b.par]), ps[:, r % 2, :].rearrange("p (k h t) -> p k h t", k=C, h=2),
                                        heads(g.la_decay), ALU.mult).then_inc(a_ready, 1)

            def step(s):
                a, b, c = s.back(2), s.back(1), s.back(3)
                if s.base is None and s.n == 2:
                    dve.wait_ge(taps_loaded, 32)
                    nc.vector.tensor_tensor(g.cv_row[:, P - 1:P], g.cv_row[:, P - 1:P], g.cv_skip, ALU.add).then_inc(row_ready, 1)
                if b.on:
                    wait(dve, qk_turned, b)
                    wait(dve, scores_done, b, back=2, per=4)
                    nc.vector.tensor_tensor(qT[:, b.par, :, :, :], spread(turn2[:, 0, :, :], 2, 2),
                                            spread(spread(g.pair[:], 1, C), 3, P), ALU.mult).then_inc(qT_ready, 1)
                if a.on:
                    wait(dve, o_turned, a)
                    wait(dve, un_ready, a, back=1)
                    nc.vector.tensor_tensor(u[:], pon, gate[:, a.par, :], ALU.mult).then_inc(u_ready, 1)
                if c.on:
                    dve.drain()
                    layer_norm_stats(nc, n2, g.x[:, c.i, :], c.par, var2_ready)
                if a.on:
                    wait(dve, usq_ready, a)
                    nc.vector.tensor_reduce(msq[:], usq[:].rearrange("p (h d) -> p h d", d=HD), AX.X, ALU.add)
                    dve.drain()
                    nc.vector.tensor_scalar(msq[:], msq[:], 1.0 / HD, 1e-6, ALU.mult, ALU.add)
                    dve.drain()
                    rsqrt_seed(nc, norm[:], msq[:]).then_inc(msq_ready, 1)
                n = s.back(-1)
                if n.on:
                    wait(dve, rstd_ready, n)
                    wait(dve, turned, n, back=2)
                    layer_norm_apply(nc, m, xn[:, n.par, :], g.x[:, n.i, :], n.par).then_inc(xn_ready, 1)
                if c.on:
                    wait(dve, rstd2_ready, c)
                    wait(dve, turned2, c, back=1)
                    layer_norm_apply(nc, n2, xn2[:], g.x[:, c.i, :], c.par).then_inc(xn2_ready, 1)
                if b.on:
                    wait(dve, av_done, b, back=2)
                    for r in range(4):
                        decay(b, r)
                if a.on:
                    wait(dve, norm_ready, a)
                    wait(dve, un_turned, a, back=1)
                    nc.vector.tensor_tensor(un[:].rearrange("p (h d) -> p h d", d=HD), u[:].rearrange("p (h d) -> p h d", d=HD),
                                            spread(norm[:], 2, HD), ALU.mult).then_inc(un_ready, 1)
                if s.on:
                    wait(dve, sigm_ready, s)
                    nc.vector.tensor_tensor(qk[:], sigm[:], pqk[:], ALU.mult).then_inc(silu_ready, 1)
                    dve.drain()
                    wait(dve, qk_ready, s, back=1)
                    halves = qk[:].rearrange("p (h t d) -> p h t d", t=2, d=8)
                    nc.vector.tensor_tensor(by_cos[:].rearrange("p (h t d) -> p h t d", t=2, d=8), halves,
                                            spread(spread(g.la_cos, 1, 2), 1, 2 * H), ALU.mult)
                    nc.vector.tensor_tensor(by_sin[:].rearrange("p (h t d) -> p h t d", t=2, d=8), halves[:, :, ::-1, :],
                                            spread(g.la_sin, 1, 2 * H), ALU.mult).then_inc(rot_ready, 1)
                n = s.back(-2)
                if n.on:
                    wait(dve, xn_ready, n, back=2)
                    layer_norm_stats(nc, m, g.x[:, n.i, :], n.par, var_ready)
                if a.on:
                    wait(dve, out_done, a)
                    nc.vector.tensor_tensor(g.x[:, a.i, :], pout, g.x[:, a.i, :], ALU.add).then_inc(x_added, 1)
            steps(dve, step, 2, 3)

        @block.scalar
        def _(act):
            act.wait_ge(filled, 3)

            def step(s):
                a, b = s.back(2), s.back(1)
                if s.on:
                    wait(act, turned, s)
                    wait(act, v_done, s, back=2)
                    nc.scalar.activation(xnT[:, s.par, :, :], turn[:, 0:D], ACT.Copy).then_inc(xnT_ready, 1)
                if b.on:
                    wait(act, qk_turned, b)
                    wait(act, qT_ready, b)
                    wait(act, scores_done, b, back=2, per=4)
                    nc.scalar.activation(kT[:, b.par, :, :], turn2[:, 1, :, :], ACT.Copy).then_inc(kT_ready, 1)
                if s.on:
                    wait(act, qk_done, s)
                    wait(act, silu_ready, s, back=1)
                    nc.scalar.activation(sigm[:], pqk[:], ACT.Sigmoid).then_inc(sigm_ready, 1)
                    wait(act, g1_done, s)
                    wait(act, gate_done, s, back=1)
                    nc.scalar.activation(g1T[:], turn[0:16, D:D + P], ACT.Copy).then_inc(g1_ready, 1)
                    wait(act, v_done, s)
                    wait(act, av_done, s, back=2)
                    nc.scalar.activation(vd[s.par][:].rearrange("p g (h c) -> p g h c", c=144)[:, :, :, 0:HD],
                                         pv.rearrange("p (g h d) -> p g h d", g=2, h=8), ACT.Copy).then_inc(v_ready, 1)
                c = s.back(3)
                if c.on:
                    wait(act, turned2, c)
                if s.on:
                    wait(act, u_ready, s, back=2)
                    wait(act, gate_done, s)
                    nc.scalar.activation(gate[:, s.par, :], turn[:, 0:D], ACT.Sigmoid).then_inc(gate_ready, 1)
                if c.on:
                    nc.scalar.activation(g.cv_qT[:, :, c.i, :], px2.rearrange("p (c t) -> p c t", c=C), ACT.Copy).then_inc(qT2_ready, 1)
                if b.on:
                    wait(act, av_done, b)
                    wait(act, o_turned, b, back=1)
                    nc.scalar.activation(oT[:], po[:, 0:D], ACT.Copy).then_inc(oT_ready, 1)
                if a.on:
                    wait(act, un_turned, a)
                    wait(act, out_done, a, back=1)
                    nc.scalar.activation(unT[:], pun, ACT.Copy).then_inc(unT_ready, 1)
            steps(act, step, 0, 3)

        @block.tensor
        def _(pe):
            pe.wait_ge(g.la_loaded, 16 * g.la_loads)
            pe.wait_ge(filled, 3)

            def step(s):
                a, b = s.back(2), s.back(1)
                if s.on:
                    wait(pe, xn_ready, s)
                    wait(pe, gate_ready, s, back=1)
                    for k in range(C):
                        last = nc.tensor.transpose(turn[:, k * P:(k + 1) * P], xn[:, s.par, k * P:(k + 1) * P], g.ident[:])
                    last.then_inc(turned, 1)
                if b.on:
                    wait(pe, qk_ready, b)
                    wait(pe, kT_ready, b, back=1)
                    for t in range(2):
                        for k in range(C):
                            last = nc.tensor.transpose(turn2[:, t, k, :], qkr[:, b.par, t * D + k * P:t * D + (k + 1) * P], g.ident[:])
                    last.then_inc(qk_turned, 1)
                if s.on:
                    wait(pe, xnT_ready, s)
                    wait(pe, silu_ready, s, back=1)
                    for k in range(C):
                        last = nc.tensor.matmul(pqk[:], xnT[:, s.par, k, :], g.la_wqk[:, k, :], start=(k == 0), stop=(k == C - 1))
                    last.then_inc(qk_done, 1)
                    for k in range(C):
                        last = nc.tensor.matmul(turn[0:16, D:D + P], g.la_wg1[:, k, :], xnT[:, s.par, k, :],
                                                start=(k == 0), stop=(k == C - 1))
                    last.then_inc(g1_done, 1)
                if b.on:
                    wait(pe, kT_ready, b)
                    wait(pe, qT_ready, b)
                    wait(pe, unT_ready, b, back=2)
                    for r in range(4):
                        wait(pe, a_ready, b, back=1, per=4, more=r - 1)
                        rows = slice(32 * r, 32 * r + 32)
                        for k in range(C):
                            last = nc.tensor.matmul(ps[:, r % 2, k * D:(k + 1) * D], kT[rows, b.par, k, :], qT[rows, b.par, k, :, :],
                                                    start=True, stop=True)
                        last.then_inc(scores_done, 1)
                c = s.back(3)
                if c.on:
                    wait(pe, xn2_ready, c)
                    if a.on:
                        wait(pe, u_ready, a)
                    for k in range(C):
                        last = nc.tensor.transpose(px2[:, k * P:(k + 1) * P], xn2[:, k * P:(k + 1) * P], g.ident[:])
                    last.then_inc(turned2, 1)
                if s.on:
                    wait(pe, x_added, s, back=3)
                    for k in range(C):
                        last = nc.tensor.matmul(pv, xnT[:, s.par, k, :], g.la_wv[:, k, :], start=(k == 0), stop=(k == C - 1))
                    last.then_inc(v_done, 1)
                    wait(pe, g1_ready, s)
                    nc.tensor.matmul(turn[:, 0:D], g1T[:], g.la_wg2, start=True, stop=True).then_inc(gate_done, 1)
                if b.on:
                    wait(pe, v_ready, b)
                    wait(pe, a_ready, b, per=4)
                    wait(pe, oT_ready, b, back=1)
                    for h in range(H):
                        gr, hh = h // 8, h % 8
                        last = nc.tensor.matmul(po[:, gr * P:(gr + 1) * P], vd[b.par][:, gr, hh * P:(hh + 1) * P], a_mat[b.par][:, h, :],
                                                start=(hh == 0), stop=(hh == 7))
                    last.then_inc(av_done, 1)
                if a.on:
                    wait(pe, un_ready, a)
                    wait(pe, unT_ready, a, back=1)
                    for k in range(C):
                        last = nc.tensor.transpose(pun[:, k * P:(k + 1) * P], un[:, k * P:(k + 1) * P], g.ident[:])
                    last.then_inc(un_turned, 1)
                if b.on:
                    wait(pe, qT2_ready, s, back=3)
                    wait(pe, oT_ready, b)
                    wait(pe, u_ready, b, back=1)
                    for k in range(C):
                        last = nc.tensor.transpose(pon[:, k * P:(k + 1) * P], oT[:, k, :], g.ident[:])
                    last.then_inc(o_turned, 1)
                if a.on:
                    wait(pe, unT_ready, a)
                    if s.on:
                        wait(pe, v_ready, s)
                    for k in range(C):
                        last = nc.tensor.matmul(pout, unT[:, k, :], g.la_wo[:, k, :], start=(k == 0), stop=(k == C - 1))
                    last.then_inc(out_done, 1)
            steps(pe, step, 0, 3)


def gated_convolution(nc, g):
    H, HD = 16, 8
    HB = B // 2
    ROW = P - 1 + 2 * P
    with ExitStack() as ctx:
        m = Names(nc, ctx, "cv")
        qT = g.cv_qT
        oT = g.late[:, 4096:8192].rearrange("p (c b t) -> p c b t", c=C, b=B)
        filt = m.sb("filt", [P, 2, 2 * P])
        kv = m.sb("kv", [P, 2, C, 512])
        z = m.sb("z", [P, 2, C, 512])
        y = m.ps("y", [P, 4, 512])
        kv_ready, y_done, z_ready, o_ready, o_turned, x_added = map(m.sem, (
            "kv_ready", "y_done", "z_ready", "o_ready", "o_turned", "x_added"))
        filt_loaded = [m.sem(f"filt_loaded{i}") for i in range(2)]
        ctxr = g.ctxT[:].rearrange("p c (b t) -> p c b t", b=B)
        block = ctx.enter_context(nc.Block())

        @block.sync
        def _(sp):
            def head(s):
                if s.on:
                    wait(sp, y_done, s, back=2, per=4)
                    window = bass.AP(g.cv_rows.tensor, s.i * ROW, [[1, P], [1, 2 * P]])
                    sp.dma_start(filt[:, s.par, :], window).then_inc(filt_loaded[s.par], 16)
            steps(sp, head, 0, 0, first=2)

        @block.scalar
        def _(act):
            act.dma_start(g.ga_wq, g.h["ga_wq"]).then_inc(g.ga_loaded, 16)
            act.dma_start(g.ga_wk, g.h["ga_wk"]).then_inc(g.ga_loaded, 16)
            act.dma_start(g.ga_wv, g.h["ga_wv"]).then_inc(g.ga_loaded, 16)
            act.dma_start(g.ga_wo, g.h["ga_wo"]).then_inc(g.ga_loaded, 16)
            act.dma_start(g.ga_norm[:], g.h["ga_norm"]).then_inc(g.ga_loaded, 16)
            act.dma_start(g.mo_norm[:], g.h["mo_norm"]).then_inc(g.ga_loaded, 16)
            act.dma_start(g.ga_cosT[:], g.h["ga_cosT"]).then_inc(g.ga_loaded, 16)
            act.dma_start(g.ga_sinT[:], g.h["ga_sinT"]).then_inc(g.ga_loaded, 16)
            act.dma_start(g.ga_hidden[:], g.h["hidden"]).then_inc(g.ga_loaded, 16)


        @block.gpsimd
        def _(pool):
            pool.wait_ge(g.ctx_loaded, 16)

            def products(s):
                for half in range(2):
                    wait(pool, y_done, s, back=2, per=4, more=2 * half + 2)
                    for c in range(C):
                        v = ctxr[:, c, HB * half:HB * (half + 1), bass.ts(s.i, HD)]
                        nc.gpsimd.tensor_tensor(kv[:, half, c, :].rearrange("p (b i j) -> p b i j", b=HB, i=HD),
                                                spread(v, 3, HD), spread(v, 2, HD), ALU.mult).then_inc(kv_ready, 1)

            products(At(None, 0))
            products(At(None, 1))
            with pool.Fori(1, H // 2) as k:
                products(At(2 * k, 0))
                products(At(2 * k, 1))

        @block.vector
        def _(dve):
            def gate(s):
                for half in range(2):
                    bs = slice(HB * half, HB * (half + 1))
                    for c in range(C):
                        wait(dve, y_done, s, back=1, per=4, more=2 * half + c + 1)
                        nc.vector.tensor_tensor(z[:, half, c, :].rearrange("p (b i j) -> p b i j", b=HB, i=HD),
                                                y[:, 2 * half + c, :].rearrange("p (b i j) -> p b i j", b=HB, i=HD),
                                                spread(qT[:, c, bs, bass.ts(s.i, HD)], 3, HD), ALU.mult).then_inc(z_ready, 1)
                    dve.drain()
                    for c in range(C):
                        last = nc.vector.tensor_reduce(oT[:, c, bs, bass.ts(s.i, HD)],
                                                       z[:, half, c, :].rearrange("p (b i j) -> p b j i", b=HB, i=HD),
                                                       AX.X, ALU.add)
                last.then_inc(o_ready, 1)
            with dve.Fori(0, H // 2) as k:
                gate(At(2 * k, 0))
                gate(At(2 * k, 1))
            for b in range(B):
                dve.wait_ge(o_turned, b + 1)
                nc.vector.tensor_tensor(g.x[:, b, :], y[:, b % 4, 0:D], g.x[:, b, :], ALU.add).then_inc(x_added, 1)

        @block.tensor
        def _(pe):
            def convolve(s):
                wait_half(pe, filt_loaded[s.par], s)
                for half in range(2):
                    wait(pe, kv_ready, s, back=1, per=4, more=2 * half + 2)
                    wait(pe, z_ready, s, back=2, per=4, more=2 * half + 1)
                    nc.tensor.matmul(y[:, 2 * half, :], filt[:, s.par, 0:P], kv[:, half, 0, :],
                                     start=True, stop=True).then_inc(y_done, 1)
                    wait(pe, z_ready, s, back=2, per=4, more=2 * half + 2)
                    nc.tensor.matmul(y[:, 2 * half + 1, :], filt[:, s.par, P:], kv[:, half, 0, :], start=True, stop=False)
                    nc.tensor.matmul(y[:, 2 * half + 1, :], filt[:, s.par, 0:P], kv[:, half, 1, :],
                                     start=False, stop=True).then_inc(y_done, 1)
            convolve(At(None, 0))
            convolve(At(None, 1))
            with pe.Fori(1, H // 2) as k:
                convolve(At(2 * k, 0))
                convolve(At(2 * k, 1))
            pe.wait_ge(o_ready, H)
            for b in range(B):
                s = At(None, b)
                wait(pe, x_added, s, back=4)
                for c in range(C):
                    last = nc.tensor.transpose(y[:, b % 4, c * P:(c + 1) * P], oT[:, c, b, :], g.ident[:])
                last.then_inc(o_turned, 1)


E, F = 8, 512
REGION = B * P + P
TILES = 2 * B * P // P + E - 1
SPARE = E - 1
ROW = D + 2


def allocate_moe(nc, g):
    m = g.m
    g.rows = nc.dram_tensor("mo_rows", [E * REGION + SPARE * P, ROW], F32, kind="Internal").ap()
    g.acc = nc.dram_tensor("mo_acc", [B * P + P, D], F32, kind="Internal").ap()
    g.tile_expert, g.tile_row = m.sb("tile_expert", [P, TILES], I32), m.sb("tile_row", [P, TILES], I32)


class Router:

    def __init__(self, nc, g, m, bank, space):
        U32 = mybir.dt.uint32
        self.nc, self.g = nc, g
        self.gate = m.sb("gate", [P, C, E])
        self.before, self.before_bf, self.ones = m.sb("before", [P, P]), m.sb("before_bf", [P, P], BF16), m.sb("ones", [P, P], BF16)
        self.expert_no, self.region_at = m.sb("expert_no", [P, E]), m.sb("region_at", [P, E])
        self.token_no, self.tile_no = m.sb("token_no", [P, B + 1]), m.sb("tile_no", [P, TILES])
        self.ss, self.rms = m.sb("ss", [P, 2, 1]), m.sb("root", [P, 2, 1])
        self.row = m.sb("row", [P, 2, 2 * ROW])
        self.xnT = m.sb("hnT", [P, 2, C, P])
        self.logits, self.top = m.sb("logits", [P, E]), m.sb("top", [P, E])
        self.which, self.which_f = m.sb("which", [P, E], U32), m.sb("which_f", [P, 2])
        self.margin, self.share = m.sb("margin", [P, 2, 1]), m.sb("share", [P, 2, 3])
        self.chosen = m.sb("chosen", [P, 2, 2, E])
        self.both = m.sb("both", [P, 2, E], BF16)
        self.earlier = m.sb("earlier", [P, E], BF16)
        self.place, self.at = m.sb("place", [P, E]), m.sb("at", [P, 2, E])
        self.slot_f, self.slot_d = m.sb("slot_f", [P, 2]), m.sb("slot_d", [P, 2, 2], U32)
        self.slot, self.zero = m.sb("slot", [P, 2, 2], U32), m.sb("zero", [P, 2], U32)
        self.pad = m.sb("pad", [P, ROW])
        self.pad_f, self.pad_at = m.sb("pad_f", [1, E]), m.sb("pad_at", [1, E], I32)
        self.tiles, self.ends, self.ends2 = m.sb("tiles", [P, E]), m.sb("ends", [P, E]), m.sb("ends2", [P, E])
        self.past = space[:, 0:TILES * E].rearrange("p (t e) -> p t e", e=E)
        self.expert_f, self.start_f = m.sb("expert_f", [P, TILES]), m.sb("start_f", [P, TILES])
        self.turn, self.plog, self.prank = bank[:, 0:D], bank[:, D:D + E], bank[:, D + E:D + 2 * E]
        (self.loaded, self.filled, self.ss_ready, self.ms_ready, self.rms_ready, self.row_ready, self.turned,
         self.xnT_ready, self.log_done, self.margin_ready, self.exp_ready, self.chosen_ready, self.rank_done,
         self.slot_ready, self.pad_ready, self.spare_stored, self.sum_ready, self.acc_stored, self.pads_sent) = map(m.sem, (
            "loaded", "filled", "ss_ready", "ms_ready", "root_ready", "row_ready", "r_turned", "hnT_ready",
            "log_done", "margin_ready", "exp_ready", "chosen_ready", "rank_done", "slot_ready", "pad_ready",
            "spare_stored", "sum_ready", "acc_stored", "pads_sent"))
        self.sent = [m.sem(f"sent{i}") for i in range(2)]
        self.constants = ((self.gate[:], "mo_gate"), (self.before[:], "before"), (self.expert_no[:], "expert_no"),
                          (self.region_at[:], "region_at"), (self.token_no[:], "token_no"), (self.tile_no[:], "tile_no"))

    def wait_sent(self, eng, s):
        if s.base is not None or s.n >= 2:
            eng.wait_ge(self.sent[s.par], (s.i - s.par) * 16)

    def load(self, sp):
        for to, name in self.constants:
            sp.dma_start(to, self.g.h[name]).then_inc(self.loaded, 16)

    def store_padding(self, sp):
        g = self.g
        sp.wait_ge(self.pad_ready, 1)
        sp.dma_start(g.rows[E * REGION:, :].rearrange("(t p) c -> p t c", p=P), spread(self.pad[:], 1, SPARE)).then_inc(self.spare_stored, 16)
        sp.dma_start(g.acc[B * P:, :], self.pad[:, 0:D]).then_inc(self.spare_stored, 16)

    def store_sum(self, sp, s):
        g = self.g
        wait(sp, self.sum_ready, s)
        sp.dma_start(g.acc[bass.ts(s.i, P), :], g.x[:, s.i, :]).then_inc(self.acc_stored, 16)

    def pad_regions(self, eng, experts):
        eng.wait_ge(self.pad_ready, 2)
        for e in experts:
            first = eng.value_load(self.pad_at[0:1, e:e + 1], min_val=0, max_val=e * REGION + B * P)
            eng.dma_start(self.g.rows[bass.ds(first, P), :], self.pad[:]).then_inc(self.pads_sent, 16)

    def fill(self, pool):
        nc = self.nc
        nc.gpsimd.memset(self.ones[:], 1.0).then_inc(self.filled, 1)
        nc.gpsimd.memset(self.earlier[:], 0.0).then_inc(self.filled, 1)
        nc.gpsimd.memset(self.pad[:, 0:D + 1], 0.0).then_inc(self.filled, 1)
        nc.gpsimd.memset(self.zero[:], 0)
        pool.drain()

    def root(self, pool, s):
        wait(pool, self.ms_ready, s)
        self.nc.gpsimd.tensor_tensor(self.rms[:, s.par, :], self.ss[:, s.par, :], self.g.minus_half[:],
                                     ALU.pow).then_inc(self.rms_ready, 1)

    def send(self, pool, s):
        nc, g = self.nc, self.g
        wait(pool, self.slot_ready, s)
        nc.gpsimd.tensor_tensor(self.slot[:, s.par, :], self.slot_d[:, s.par, :], self.zero[:], ALU.add)
        pool.drain()
        for k in range(2):
            nc.gpsimd.indirect_dma_start(g.rows, bass.IndirectOffsetOnAxis(ap=self.slot[:, s.par, k:k + 1], axis=0),
                                         self.row[:, s.par, k * ROW:(k + 1) * ROW], None).then_inc(self.sent[s.par], 16)

    def end_sends(self, pool):
        for k in range(2):
            pool.wait_ge(self.sent[k], 16 * B)

    def prepare(self, dve):
        nc = self.nc
        dve.wait_ge(self.filled, 3)
        dve.wait_ge(self.loaded, 16 * len(self.constants))
        nc.vector.tensor_copy(self.pad[:, D + 1:], self.token_no[:, B:]).then_inc(self.pad_ready, 1)
        nc.vector.tensor_copy(self.before_bf[:], self.before[:]).then_inc(self.filled, 1)

    def mean_square(self, dve, s):
        wait(dve, self.ss_ready, s)
        self.nc.vector.tensor_scalar(self.ss[:, s.par, :], self.ss[:, s.par, :], 1.0 / D, 1e-5, ALU.mult,
                                     ALU.add).then_inc(self.ms_ready, 1)

    def rows(self, dve, s):
        nc, g = self.nc, self.g
        wait(dve, self.rms_ready, s)
        self.wait_sent(dve, s)
        for k in range(2):
            nc.vector.tensor_scalar(self.row[:, s.par, k * ROW:k * ROW + D], g.hid[:, s.i, :], self.rms[:, s.par, :], None, ALU.mult)
        nc.vector.tensor_copy(self.row[:, s.par, :].rearrange("p (k c) -> p k c", k=2)[:, :, D + 1],
                              self.token_no[:, bass.ds(s.i, 1)].broadcast_to([P, 2])).then_inc(self.row_ready, 1)
        nc.vector.tensor_tensor(g.x[:, s.i, :], g.x[:, s.i, :], g.hid[:, s.i, :], ALU.add).then_inc(self.sum_ready, 1)

    def choose(self, dve, s):
        nc = self.nc
        wait(dve, self.log_done, s)
        nc.vector.tensor_copy(self.logits[:], self.plog)
        dve.drain()
        nc.vector.max(self.top[:], self.logits[:])
        dve.drain()
        nc.vector.max_index(self.which[:], self.top[:], self.logits[:])
        nc.vector.tensor_tensor(self.margin[:, s.par, :], self.top[:, 1:2], self.top[:, 0:1], ALU.subtract).then_inc(self.margin_ready, 1)
        dve.drain()
        nc.vector.tensor_copy(self.which_f[:], self.which[:, 0:2])
        dve.drain()
        nc.vector.tensor_tensor(self.chosen[:, s.par, :, :], spread(self.which_f[:], 2, E), spread(self.expert_no[:], 1, 2), ALU.is_equal)
        dve.drain()
        nc.vector.tensor_tensor(self.both[:, s.par, :], self.chosen[:, s.par, 0, :], self.chosen[:, s.par, 1, :],
                                ALU.add).then_inc(self.chosen_ready, 1)

    def slots(self, dve, s):
        nc = self.nc
        wait(dve, self.exp_ready, s)
        share = self.share[:, s.par, :]
        nc.vector.tensor_scalar(share[:, 1:2], share[:, 0:1], 1.0, None, ALU.add)
        wait(dve, self.rank_done, s)
        nc.vector.tensor_tensor(self.earlier[:], self.earlier[:], self.both[:, s.par, :], ALU.add)
        nc.vector.tensor_tensor(self.place[:], self.prank, self.region_at[:], ALU.add)
        dve.drain()
        nc.vector.reciprocal(share[:, 2:3], share[:, 1:2])
        nc.vector.tensor_tensor(self.at[:], self.chosen[:, s.par, :, :], spread(self.place[:], 1, 2), ALU.mult)
        dve.drain()
        nc.vector.tensor_copy(self.row[:, s.par, D:D + 1], share[:, 2:3])
        nc.vector.tensor_tensor(self.row[:, s.par, ROW + D:ROW + D + 1], share[:, 0:1], share[:, 2:3], ALU.mult)
        nc.vector.tensor_reduce(self.slot_f[:], self.at[:], AX.X, ALU.add)
        dve.drain()
        nc.vector.tensor_copy(self.slot_d[:, s.par, :], self.slot_f[:]).then_inc(self.slot_ready, 1)

    def tables(self, dve):
        nc, g = self.nc, self.g
        tiles, past, expert_f, start_f = self.tiles, self.past, self.expert_f, self.start_f
        dve.wait_ge(self.rank_done, B + 1)
        nc.vector.tensor_tensor(self.pad_f[:], self.prank[0:1, :], self.region_at[0:1, :], ALU.add)
        nc.vector.tensor_scalar(tiles[:], self.prank, 1.0 / P, 63.5 / P, ALU.mult, ALU.add)
        dve.drain()
        nc.vector.tensor_scalar(tiles[:], tiles[:], MAGIC, None, ALU.add)
        dve.drain()
        nc.vector.tensor_copy(self.pad_at[:], self.pad_f[:]).then_inc(self.pad_ready, 1)
        nc.vector.tensor_scalar(tiles[:], tiles[:], -MAGIC, None, ALU.add)
        dve.drain()
        src, dst = tiles, self.ends
        for shift in (1, 2, 4):
            nc.vector.tensor_copy(dst[:, 0:shift], src[:, 0:shift])
            nc.vector.tensor_tensor(dst[:, shift:], src[:, shift:], src[:, 0:E - shift], ALU.add)
            dve.drain()
            src, dst = dst, (self.ends2 if dst is self.ends else self.ends)
        nc.vector.tensor_tensor(past, spread(self.tile_no[:], 2, E), spread(src[:], 1, TILES), ALU.is_ge)
        dve.drain()
        nc.vector.tensor_reduce(expert_f[:], past, AX.X, ALU.add)
        dve.drain()
        nc.vector.tensor_tensor(past, past, spread(tiles[:], 1, TILES), ALU.mult)
        dve.drain()
        nc.vector.tensor_reduce(start_f[:], past, AX.X, ALU.add)
        dve.drain()
        nc.vector.tensor_tensor(start_f[:], self.tile_no[:], start_f[:], ALU.subtract)
        dve.drain()
        nc.vector.tensor_scalar(start_f[:], start_f[:], float(P), None, ALU.mult)
        dve.drain()
        nc.vector.scalar_tensor_tensor(out=start_f[:], in0=expert_f[:], scalar=float(REGION), in1=start_f[:],
                                       op0=ALU.mult, op1=ALU.add)
        nc.vector.tensor_scalar(expert_f[:], expert_f[:], float(E - 1), None, ALU.min)
        dve.drain()
        nc.vector.tensor_copy(g.tile_row[:], start_f[:])
        nc.vector.tensor_copy(g.tile_expert[:], expert_f[:])

    def squares(self, act, s):
        wait(act, self.row_ready, s, back=2)
        wait(act, self.log_done, s, back=2)
        self.nc.scalar.activation(self.xnT[:, s.par, :, :].rearrange("p c t -> p (c t)"), self.g.hid[:, s.i, :], ACT.Square,
                                  accum_out=self.ss[:, s.par, :]).then_inc(self.ss_ready, 1)

    def copy_xnT(self, act, s):
        wait(act, self.turned, s)
        wait(act, self.log_done, s, back=2)
        for c in range(C):
            last = self.nc.scalar.activation(self.xnT[:, s.par, c, :], self.turn[:, c * P:(c + 1) * P], ACT.Copy,
                                             scale=self.g.mo_norm[:, c:c + 1])
        last.then_inc(self.xnT_ready, 1)

    def exp_margin(self, act, s):
        wait(act, self.margin_ready, s)
        self.nc.scalar.activation(self.share[:, s.par, 0:1], self.margin[:, s.par, :], ACT.Exp).then_inc(self.exp_ready, 1)

    def turn_row(self, pe, s):
        nc = self.nc
        wait(pe, self.row_ready, s)
        wait(pe, self.slot_ready, s, back=1)
        for c in range(C):
            last = nc.tensor.transpose(self.turn[:, c * P:(c + 1) * P], self.row[:, s.par, c * P:(c + 1) * P], self.g.ident[:])
        last.then_inc(self.turned, 1)

    def project(self, pe, s):
        wait(pe, self.xnT_ready, s)
        for c in range(C):
            last = self.nc.tensor.matmul(self.plog, self.xnT[:, s.par, c, :], self.gate[:, c, :], start=(c == 0), stop=(c == C - 1))
        last.then_inc(self.log_done, 1)

    def rank(self, pe, s):
        nc = self.nc
        wait(pe, self.chosen_ready, s)
        nc.tensor.matmul(self.prank, self.before_bf[:], self.both[:, s.par, :], start=True, stop=False)
        nc.tensor.matmul(self.prank, self.ones[:], self.earlier[:], start=False, stop=True).then_inc(self.rank_done, 1)

    def count(self, pe):
        pe.wait_ge(self.slot_ready, B)
        self.nc.tensor.matmul(self.prank, self.ones[:], self.earlier[:], start=True, stop=True).then_inc(self.rank_done, 1)


def grouped_attention(nc, g):
    H, KV, HD = 16, 4, 128
    REP = H // KV
    NB = KV + 1
    scale = HD ** -0.5
    with ExitStack() as ctx:
        m = Names(nc, ctx, "ga")
        xn = m.sb("xn", [P, 2, D])
        m.stats, m.mv = m.sb("stats", [P, 2, 6]), m.sb("mv", [P, 2, 3])
        m.rstd, rms, t = m.sb("rstd", [P, 2, 1]), m.sb("rms", [P, 2, 1]), m.sb("t", [P, 1])
        xnT = m.sb("xnT", [P, C, P])
        v = m.sb("v", [P, 2, 512])
        halves = m.sb("halves", [P, 2, 512])
        by_cos, by_sin = m.sb("by_cos", [P, 2, 512]), halves
        kqT = m.sb("kqT", [P, 2, NB, 512])
        negmax, inv = m.sb("negmax", [P, 2, REP]), m.sb("inv", [P, 2, REP])
        e = m.sb("e", [P, 2, 512])
        probs = e
        pT = m.sb("pT", [P, 2, 512])
        aT = m.sb("aT", [P, KV, 512])
        turn_out = m.ps("turn_out", [P, 512])
        turn, pout = turn_out[:, 0:D], turn_out[:, D:2 * D]
        pkq = m.ps("pkq", [P, 2, 512])
        router = Router(nc, g, m, m.ps("router", [P, 512]), by_cos[:].rearrange("p a n -> p (a n)"))
        psc = m.ps("psc", [P, 2, 512])
        ppT = m.ps("ppT", [P, 512])
        pv = ppT
        paT = m.ps("paT", [P, 512])
        (var_ready, rms_ready, xn_ready, turned, xnT_ready, v_done, v_ready, kq_done, halves_ready, cos_ready,
         sin_ready, kqT_ready, scores_done, max_ready, e_ready, p_ready, p_turned, pT_ready, pv_done, aT_ready,
         out_done, h_ready) = map(m.sem, (
            "var_ready", "rms_ready", "xn_ready", "turned", "xnT_ready", "v_done", "v_ready", "kq_done", "halves_ready",
            "cos_ready", "sin_ready", "kqT_ready", "scores_done", "max_ready", "e_ready", "p_ready", "p_turned",
            "pT_ready", "pv_done", "aT_ready", "out_done", "h_ready"))
        block = ctx.enter_context(nc.Block())

        def bank(eng, sem, s, r, back=0):
            wait_part(eng, sem, s, NB, r - back)

        def group(eng, sem, s, r, back=0):
            wait_part(eng, sem, s, KV, r - back)

        @block.sync
        def _(sp):
            router.load(sp)
            sp.dma_start(g.mo_w1, g.h["mo_w1"]).then_inc(g.mo_loaded, 16)
            sp.dma_start(g.mo_w2, g.h["mo_w2"]).then_inc(g.mo_loaded, 16)
            router.store_padding(sp)

            def step(s):
                if s.on:
                    router.store_sum(sp, s)
            steps(sp, step, 0, 0, count=B - 2, first=2)
            sp.wait_ge(kq_done, NB * B)
            sp.dma_start(g.mo_w3, g.h["mo_w3"]).then_inc(g.mo_loaded, 16)
            for b in range(B - 2, B):
                step(At(None, b))
            sp.wait_ge(router.spare_stored, 32)
            sp.wait_ge(router.acc_stored, 16 * B)
            router.pad_regions(sp, range(0, E, 2))
            sp.wait_ge(router.pads_sent, 16 * E)

        @block.gpsimd
        def _(pool):
            def rope(s, r):
                par = (s.n * NB + r) % 2
                bank(pool, halves_ready, s, r)
                nc.gpsimd.tensor_tensor(by_sin[:, par, :].rearrange("p (h t) -> p h t", h=REP),
                                        halves[:, par, :].rearrange("p (h t) -> p h t", h=REP),
                                        spread(g.ga_sinT[:], 1, REP), ALU.mult).then_inc(sin_ready, 1)
                pool.drain()
                bank(pool, cos_ready, s, r)
                if r == 0:
                    group(pool, scores_done, s, 3, back=2 * KV)
                nc.gpsimd.tensor_tensor(kqT[:, s.par, r, :], by_cos[:, par, :], by_sin[:, par, :], ALU.add).then_inc(kqT_ready, 1)

            router.fill(pool)

            def step(s):
                c = s.back(3)
                if c.back(1).on:
                    router.send(pool, c.back(1))
                if c.on:
                    router.root(pool, c)
                if s.on:
                    rope(s, 0)
                    rope(s, 1)
                n = s.back(-2)
                if n.on:
                    mv, rstd, rr = m.mv[:, n.par, :], m.rstd[:, n.par, :], rms[:, n.par, :]
                    wait(pool, var_ready, n)
                    wait(pool, xn_ready, n, back=2)
                    nc.gpsimd.tensor_tensor(rstd, mv[:, 2:3], g.minus_half[:], ALU.pow)
                    pool.drain()
                    nc.gpsimd.tensor_tensor(t[:], rstd, rstd, ALU.mult)
                    pool.drain()
                    nc.gpsimd.tensor_tensor(t[:], t[:], mv[:, 1:2], ALU.mult)
                    pool.drain()
                    nc.gpsimd.tensor_scalar(t[:], t[:], 1.0, 1e-5, ALU.mult, ALU.add)
                    pool.drain()
                    nc.gpsimd.tensor_tensor(t[:], t[:], g.minus_half[:], ALU.pow)
                    pool.drain()
                    nc.gpsimd.tensor_tensor(rr, t[:], rstd, ALU.mult).then_inc(rms_ready, 1)
                if s.on:
                    for r in range(2, NB):
                        rope(s, r)
            steps(pool, step, 2, 4)
            router.end_sends(pool)

        @block.vector
        def _(dve):
            def cos(s, r):
                par = (s.n * NB + r) % 2
                bank(dve, kq_done, s, r)
                bank(dve, kqT_ready, s, r, back=2)
                nc.vector.tensor_tensor(by_cos[:, par, :].rearrange("p (h t) -> p h t", h=REP),
                                        pkq[:, par, :].rearrange("p (h t) -> p h t", h=REP),
                                        spread(g.ga_cosT[:], 1, REP), ALU.mult).then_inc(cos_ready, 1)

            def maxima(b, r):
                group(dve, scores_done, b, r)
                group(dve, e_ready, b, r, back=2)
                heads = psc[:, r % 2, :].rearrange("p (h k) -> p h k", h=REP)
                nc.vector.tensor_tensor(heads, heads, spread(g.ga_hidden[:], 1, REP), ALU.add)
                dve.drain()
                nc.vector.tensor_reduce(negmax[:, r % 2, :], heads, AX.X, ALU.max)
                dve.drain()
                nc.vector.tensor_scalar(negmax[:, r % 2, :], negmax[:, r % 2, :], -scale, None, ALU.mult).then_inc(max_ready, 1)

            def normalise(b, r):
                group(dve, e_ready, b, r)
                nc.vector.reciprocal(inv[:, r % 2, :], inv[:, r % 2, :])
                dve.drain()
                nc.vector.tensor_tensor(probs[:, r % 2, :].rearrange("p (h k) -> p h k", h=REP),
                                        e[:, r % 2, :].rearrange("p (h k) -> p h k", h=REP),
                                        spread(inv[:, r % 2, :], 2, P), ALU.mult).then_inc(p_ready, 1)

            def step(s):
                if s.base is None and s.n == 1:
                    router.prepare(dve)
                a, b, c = s.back(2), s.back(1), s.back(3)
                if b.on:
                    maxima(b, 0)
                    maxima(b, 1)
                if c.on:
                    router.mean_square(dve, c)
                if b.on:
                    normalise(b, 0)
                    normalise(b, 1)
                if c.on:
                    router.rows(dve, c)
                n = s.back(-2)
                if n.on:
                    wait(dve, xn_ready, n, back=2)
                    layer_norm_stats(nc, m, g.x[:, n.i, :], n.par, var_ready)
                n = s.back(-1)
                if n.on:
                    wait(dve, rms_ready, n)
                    wait(dve, turned, n, back=2)
                    nc.vector.tensor_scalar(g.hid[:, n.i, :], g.x[:, n.i, :], m.mv[:, n.par, 0:1], m.rstd[:, n.par, :],
                                            ALU.subtract, ALU.mult)
                    nc.vector.tensor_scalar(xn[:, n.par, :], g.x[:, n.i, :], m.mv[:, n.par, 0:1], rms[:, n.par, :],
                                            ALU.subtract, ALU.mult).then_inc(xn_ready, 1)
                if a.on:
                    wait(dve, out_done, a)
                    nc.vector.tensor_tensor(g.hid[:, a.i, :], pout, g.hid[:, a.i, :], ALU.add).then_inc(h_ready, 1)
                if s.on:
                    cos(s, 0)
                if b.on:
                    maxima(b, 2)
                if s.on:
                    cos(s, 1)
                if b.on:
                    normalise(b, 2)
                    maxima(b, 3)
                if s.on:
                    cos(s, 2)
                if b.on:
                    normalise(b, 3)
                if s.on:
                    cos(s, 3)
                if c.on:
                    router.choose(dve, c)
                if s.on:
                    cos(s, 4)
                if c.on:
                    router.slots(dve, c)
            steps(dve, step, 2, 4)
            router.tables(dve)

        @block.scalar
        def _(act):
            def swap(s, r):
                par = (s.n * NB + r) % 2
                bank(act, cos_ready, s, r)
                bank(act, kqT_ready, s, r, back=2)
                nc.scalar.activation(halves[0:64, par, :], pkq[64:128, par, :], ACT.Copy)
                nc.scalar.activation(halves[64:128, par, :], pkq[0:64, par, :], ACT.Copy).then_inc(halves_ready, 1)

            def exps(b, r):
                group(act, max_ready, b, r)
                group(act, p_turned, b, r, back=2)
                for j in range(REP):
                    last = nc.scalar.activation(e[:, r % 2, j * P:(j + 1) * P], psc[:, r % 2, j * P:(j + 1) * P], ACT.Exp,
                                                bias=negmax[:, r % 2, j:j + 1], scale=scale, accum_out=inv[:, r % 2, j:j + 1])
                last.then_inc(e_ready, 1)

            def copy_pT(b, r):
                group(act, p_turned, b, r)
                group(act, pv_done, b, r, back=2)
                nc.scalar.activation(pT[:, r % 2, :], ppT[:], ACT.Copy).then_inc(pT_ready, 1)

            def copy_aT(b, r):
                group(act, pv_done, b, r)
                if r == 0:
                    wait(act, out_done, b, back=1)
                nc.scalar.activation(aT[:, r, :], paT[:], ACT.Copy).then_inc(aT_ready, 1)

            def step(s):
                b, c = s.back(1), s.back(3)
                if s.on:
                    wait(act, turned, s)
                    bank(act, kq_done, s, NB - 1, back=NB)
                    for q in range(C):
                        last = nc.scalar.activation(xnT[:, q, :], turn[:, q * P:(q + 1) * P], ACT.Copy, scale=g.ga_norm[:, q:q + 1])
                    last.then_inc(xnT_ready, 1)
                if c.on:
                    router.squares(act, c)
                if b.on:
                    exps(b, 0)
                    exps(b, 1)
                if c.on:
                    router.copy_xnT(act, c)
                if s.on:
                    wait(act, v_done, s)
                    group(act, pv_done, s, KV - 1, back=2 * KV)
                    nc.scalar.activation(v[:, s.par, :], pv[:], ACT.Copy).then_inc(v_ready, 1)
                    swap(s, 0)
                if b.on:
                    copy_pT(b, 0)
                    exps(b, 2)
                if s.on:
                    swap(s, 1)
                if b.on:
                    copy_aT(b, 0)
                    copy_pT(b, 1)
                    exps(b, 3)
                if s.on:
                    swap(s, 2)
                if b.on:
                    copy_aT(b, 1)
                    copy_pT(b, 2)
                if s.on:
                    swap(s, 3)
                if b.on:
                    copy_aT(b, 2)
                    copy_pT(b, 3)
                if c.on:
                    router.exp_margin(act, c)
                if s.on:
                    swap(s, 4)
                if b.on:
                    copy_aT(b, 3)
            steps(act, step, 0, 4)
            router.pad_regions(act, range(1, E, 2))

        @block.tensor
        def _(pe):
            pe.wait_ge(g.ga_loaded, 16 * g.ga_loads)

            def kq(s, r):
                par = (s.n * NB + r) % 2
                bank(pe, halves_ready, s, r, back=2)
                for j in range(REP):
                    w, at = (g.ga_wk, j) if r == 0 else (g.ga_wq, REP * (r - 1) + j)
                    for q in range(C):
                        last = nc.tensor.matmul(pkq[:, par, j * P:(j + 1) * P], w[:, q, at * P:(at + 1) * P], xnT[:, q, :],
                                                start=(q == 0), stop=(q == C - 1))
                last.then_inc(kq_done, 1)

            def scores(b, r):
                wait_part(pe, kqT_ready, b, NB, r + 1)
                group(pe, e_ready, b, r, back=2)
                for j in range(REP):
                    last = nc.tensor.matmul(psc[:, r % 2, j * P:(j + 1) * P], kqT[:, b.par, r + 1, j * P:(j + 1) * P],
                                            kqT[:, b.par, 0, r * P:(r + 1) * P], start=True, stop=True)
                last.then_inc(scores_done, 1)

            def turn_probs(b, r):
                group(pe, p_ready, b, r)
                group(pe, pT_ready, b, r, back=1)
                for j in range(REP):
                    last = nc.tensor.transpose(ppT[:, j * P:(j + 1) * P], probs[:, r % 2, j * P:(j + 1) * P], g.ident[:])
                last.then_inc(p_turned, 1)

            def values(b, r):
                group(pe, pT_ready, b, r)
                group(pe, aT_ready, b, r, back=1)
                nc.tensor.matmul(paT[:], v[:, b.par, r * P:(r + 1) * P], pT[:, r % 2, :], start=True, stop=True).then_inc(pv_done, 1)

            def step(s):
                if s.base is None and s.n == 2:
                    pe.wait_ge(router.filled, 4)
                    pe.wait_ge(router.loaded, 16 * len(router.constants))
                a, b, c = s.back(2), s.back(1), s.back(3)
                if s.on:
                    wait(pe, xn_ready, s)
                    wait(pe, h_ready, s, back=3)
                    for q in range(C):
                        last = nc.tensor.transpose(turn[:, q * P:(q + 1) * P], xn[:, s.par, q * P:(q + 1) * P], g.ident[:])
                    last.then_inc(turned, 1)
                if b.on:
                    scores(b, 0)
                    scores(b, 1)
                if s.on:
                    wait(pe, xnT_ready, s)
                if a.on:
                    group(pe, aT_ready, a, KV - 1)
                    for h in range(H):
                        last = nc.tensor.matmul(pout, aT[:, h // REP, (h % REP) * P:(h % REP + 1) * P], g.ga_wo[:, h, :],
                                                start=(h == 0), stop=(h == H - 1))
                    last.then_inc(out_done, 1)
                if c.on:
                    router.turn_row(pe, c)
                if s.on:
                    group(pe, pT_ready, s, KV - 1, back=2 * KV)
                    for q in range(C):
                        last = nc.tensor.matmul(pv[:], xnT[:, q, :], g.ga_wv[:, q, :], start=(q == 0), stop=(q == C - 1))
                    last.then_inc(v_done, 1)
                    kq(s, 0)
                if c.on:
                    router.project(pe, c)
                if s.on:
                    wait(pe, v_ready, s)
                for r in range(KV):
                    if b.on:
                        turn_probs(b, r)
                        if r < 2:
                            scores(b, r + 2)
                    if s.on:
                        kq(s, r + 1)
                    if b.on:
                        if r == 0:
                            wait(pe, v_ready, b)
                        values(b, r)
                if c.on:
                    router.rank(pe, c)
            steps(pe, step, 0, 4)
            router.count(pe)


def experts(nc, g):
    with ExitStack() as ctx:
        m = Names(nc, ctx, "ex")
        row = m.sb("row", [P, 2, ROW])
        weight, token_d = m.sb("weight", [P, 2, 1]), m.sb("token_d", [P, 2, 1], mybir.dt.uint32)
        token, zero = m.sb("token", [P, 2, 1], mybir.dt.uint32), m.sb("zero", [P, 1], mybir.dt.uint32)
        xnT = m.sb("xnT", [P, 2, C, P])
        silu, hidden = m.sb("silu", [P, F]), m.sb("hidden", [P, F])
        hT = m.sb("hT", [P, F])
        y = m.sb("y", [P, 2, D])
        turn, p1, p3, phT, py = m.ps("turn", [P, 512]), m.ps("p1", [P, F]), m.ps("p3", [P, F]), m.ps("phT", [P, F]), m.ps("py", [P, 512])
        (meta_ready, turned, xnT_ready, h1_done, h3_done, silu_ready, hidden_ready, h_turned, hT_ready, y_done, y_ready,
         added, out_stored) = map(m.sem, (
            "meta_ready", "turned", "xnT_ready", "h1_done", "h3_done", "silu_ready", "hidden_ready", "h_turned", "hT_ready",
            "y_done", "y_ready", "added", "out_stored"))
        row_loaded = [m.sem(f"row_loaded{i}") for i in range(2)]
        block = ctx.enter_context(nc.Block())

        @block.sync
        def _(sp):
            def load(t):
                if t.on:
                    first = sp.value_load(g.tile_row[0:1, bass.ds(t.i, 1)], min_val=0, max_val=E * REGION + (SPARE - 1) * P)
                    wait(sp, turned, t, back=2)
                    wait(sp, meta_ready, t, back=2)
                    sp.dma_start(row[:, t.par, :], g.rows[bass.ds(first, P), :]).then_inc(row_loaded[t.par], 16)
            steps(sp, load, 0, 0, count=TILES, first=2)
            sp.wait_ge(added, 16 * TILES)
            sp.dma_start(g.out.rearrange("b t d -> (b t) d"), g.acc[0:B * P, :]).then_inc(out_stored, 16)
            sp.wait_ge(out_stored, 16)

        @block.gpsimd
        def _(pool):
            nc.gpsimd.memset(zero[:], 0)
            pool.drain()

            def step(t):
                b = t.back(1)
                if b.on:
                    wait(pool, added, b, back=1, per=16)
                    wait(pool, y_ready, b)
                    nc.gpsimd.tensor_tensor(token[:, b.par, :], token_d[:, b.par, :], zero[:], ALU.add)
                    pool.drain()
                    nc.gpsimd.indirect_dma_start(g.acc, bass.IndirectOffsetOnAxis(ap=token[:, b.par, :], axis=0), y[:, b.par, :],
                                                 None, compute_op=ALU.add).then_inc(added, 16)
            steps(pool, step, 0, 1, count=TILES)

        @block.vector
        def _(dve):
            def step(t):
                if t.on:
                    wait_half(dve, row_loaded[t.par], t)
                    wait(dve, added, t, back=2, per=16)
                    nc.vector.tensor_copy(weight[:, t.par, :], row[:, t.par, D:D + 1])
                    nc.vector.tensor_copy(token_d[:, t.par, :], row[:, t.par, D + 1:]).then_inc(meta_ready, 1)
                    wait(dve, silu_ready, t)
                    wait(dve, h3_done, t)
                    wait(dve, h_turned, t, back=1)
                    nc.vector.tensor_tensor(hidden[:], silu[:], p3[:], ALU.mult).then_inc(hidden_ready, 1)
                b = t.back(1)
                if b.on:
                    wait(dve, y_done, b)
                    nc.vector.tensor_scalar(y[:, b.par, :], py[:, 0:D], weight[:, b.par, :], None, ALU.mult).then_inc(y_ready, 1)
            steps(dve, step, 0, 1, count=TILES)

        @block.scalar
        def _(act):
            def step(t):
                if t.on:
                    wait(act, h1_done, t)
                    wait(act, hidden_ready, t, back=1)
                    nc.scalar.activation(silu[:], p1[:], ACT.Silu).then_inc(silu_ready, 1)
                n = t.back(-1)
                if n.on:
                    wait(act, turned, n)
                    wait(act, h3_done, n, back=2)
                    for c in range(C):
                        last = nc.scalar.activation(xnT[:, n.par, c, :], turn[:, c * P:(c + 1) * P], ACT.Copy, scale=g.mo_norm[:, c:c + 1])
                    last.then_inc(xnT_ready, 1)
                if t.on:
                    wait(act, h_turned, t)
                    wait(act, y_done, t, back=1)
                    nc.scalar.activation(hT[:], phT[:], ACT.Copy).then_inc(hT_ready, 1)
            steps(act, step, 1, 1, count=TILES)

        @block.tensor
        def _(pe):
            pe.wait_ge(g.mo_loaded, 16 * g.mo_loads)

            def step(t):
                if t.on:
                    expert = pe.value_load(g.tile_expert[0:1, bass.ds(t.i, 1)], min_val=0, max_val=E - 1)
                    wait(pe, xnT_ready, t)
                    wait(pe, silu_ready, t, back=1)
                    for c in range(C):
                        last = nc.tensor.matmul(p1[:], xnT[:, t.par, c, :], g.mo_w1[:, bass.ds(expert, 1), c, :].rearrange("p e f -> p (e f)"), start=(c == 0), stop=(c == C - 1))
                    last.then_inc(h1_done, 1)
                    wait(pe, hidden_ready, t, back=1)
                    for c in range(C):
                        last = nc.tensor.matmul(p3[:], xnT[:, t.par, c, :], g.mo_w3[:, bass.ds(expert, 1), c, :].rearrange("p e f -> p (e f)"), start=(c == 0), stop=(c == C - 1))
                    last.then_inc(h3_done, 1)
                n = t.back(-1)
                if n.on:
                    wait_half(pe, row_loaded[n.par], n)
                    wait(pe, xnT_ready, n, back=1)
                    for c in range(C):
                        last = nc.tensor.transpose(turn[:, c * P:(c + 1) * P], row[:, n.par, c * P:(c + 1) * P], g.ident[:])
                    last.then_inc(turned, 1)
                b = t.back(1)
                if b.on:
                    expert = pe.value_load(g.tile_expert[0:1, bass.ds(b.i, 1)], min_val=0, max_val=E - 1)
                    wait(pe, hT_ready, b)
                    wait(pe, y_ready, b, back=1)
                    for f in range(4):
                        last = nc.tensor.matmul(py[:, 0:D], hT[:, f * P:(f + 1) * P], g.mo_w2[:, bass.ds(expert, 1), f, :].rearrange("p e d -> p (e d)"), start=(f == 0), stop=(f == 3))
                    last.then_inc(y_done, 1)
                if t.on:
                    wait(pe, hidden_ready, t)
                    wait(pe, hT_ready, t, back=1)
                    for f in range(4):
                        last = nc.tensor.transpose(phT[:, f * P:(f + 1) * P], hidden[:, f * P:(f + 1) * P], g.ident[:])
                    last.then_inc(h_turned, 1)
            steps(pe, step, 1, 1, count=TILES)


def constants():
    f = np.float32
    ident = np.eye(P, dtype=f)
    part = np.arange(P)
    quad = ((part[:, None] % 32) // 8 == np.arange(4)).astype(f)
    pair = ((part[:, None] % 32) // 16 == np.arange(2)).astype(f)
    pos = np.arange(P, dtype=f)

    def rope(base, d):
        half = d // 2
        if base == 10000.0:
            theta = f(base) ** (f(-2.0) * np.arange(half, dtype=f) / f(d))
        else:
            theta = f(1.0) / f(base) ** (np.arange(0, d, 2, dtype=f) / f(d))
        ang = (pos[:, None] * theta[None, :].astype(f)).astype(np.float64)
        cos, sin = np.cos(ang).astype(f), np.sin(ang).astype(f)
        return cos, np.stack([-sin, sin], axis=1)

    la_cos, la_sin = rope(10000.0, 16)
    ga_cos, ga_sin = rope(1000000.0, 128)
    lam = -(2.0 ** (-8.0 * (np.arange(16, dtype=f) + 1.0) / 16)).astype(f)
    diff = pos[None, :] - pos[:, None]
    decay = np.where(diff[:, None, :] >= 0, np.exp(np.minimum(lam[None, :, None] * diff[:, None, :], 0.0)), 0.0).astype(f)
    before = (part[:, None] < part[None, :]).astype(f)
    hidden = np.where(part[None, :] <= part[:, None], 0.0, -3e38).astype(f)
    return dict(ident=ident, quad=quad, pair=pair, la_cos=la_cos, la_sin=la_sin, la_decay=decay,
                ga_cosT=np.concatenate([ga_cos.T, ga_cos.T]), ga_sinT=ga_sin.reshape(P, P).T, before=before, hidden=hidden)


def chunked(w):
    return np.ascontiguousarray(w.reshape(-1, P, w.shape[-1]).transpose(1, 0, 2))


def layouts(i):
    k = constants()
    i = {n: np.asarray(a) for n, a in i.items()}
    kv = np.concatenate([i["L0_xattn_Wk"], i["L0_xattn_Wv"]], axis=0)
    ctx = i["ctx_2048"].reshape(B * P, D).T
    h = dict(
        x=i["x"].transpose(1, 0, 2), ctxT=chunked(ctx), ctxR=chunked(ctx)[::-1],
        ca_wq=chunked(i["L0_attn_Wq"]), ca_wk=chunked(i["L0_attn_Wk"]), ca_wv=chunked(i["L0_attn_Wv"]),
        ca_wo=chunked(i["L0_attn_Wo"]),
        xa_wq=chunked(i["L0_xattn_Wq"].T), xa_wk=chunked(kv[0::2].T), xa_wv=chunked(kv[1::2].T),
        ql_w=chunked(i["L0_ffn_weight"].T),
        la_wqk=chunked(np.concatenate([i["L1_attn_Wq"], i["L1_attn_Wk"]], axis=1)), la_wv=chunked(i["L1_attn_Wv"]),
        la_wo=chunked(i["L1_attn_Wo"]), la_wg1=chunked(i["L1_attn_Wg1"]), la_wg2=i["L1_attn_Wg2"],
        la_norm=i["L1_attn_norm_weight"].reshape(C, P).T,
        cv_taps=i["L1_xattn_ssm_kernel"], cv_skip=i["L1_xattn_D"][:, None],
        ga_norm=i["L1_ffn_norm1_w"].reshape(C, P).T, ga_wq=chunked(i["L1_ffn_wq"]), ga_wk=chunked(i["L1_ffn_wk"]),
        ga_wv=chunked(i["L1_ffn_wv"]), ga_wo=chunked(i["L1_ffn_wo"]),
        mo_norm=i["L1_ffn_norm2_w"].reshape(C, P).T, mo_gate=chunked(i["L1_ffn_gate_w"]),
        mo_w1=i["L1_ffn_w1"].reshape(8, C, P, 512).transpose(2, 0, 1, 3),
        mo_w3=i["L1_ffn_w3"].reshape(8, C, P, 512).transpose(2, 0, 1, 3),
        mo_w2=i["L1_ffn_w2"].reshape(8, 4, P, D).transpose(2, 0, 1, 3),
        expert_no=np.tile(np.arange(8, dtype=np.float32), (P, 1)),
        region_at=np.tile(np.arange(8, dtype=np.float32) * REGION, (P, 1)),
        tile_no=np.tile(np.arange(TILES, dtype=np.float32), (P, 1)),
        token_no=(np.arange(P)[:, None] + P * np.arange(B + 1)[None, :]).astype(np.float32), **k)
    return {n: np.ascontiguousarray(a) for n, a in h.items()}




def decoder(nc, h, out):
    with ExitStack() as ctx:
        g = allocate(nc, ctx, h)
        g.h, g.out = h, out
        allocate_moe(nc, g)
        load_first(nc, g, h)
        channel_attention(nc, g)
        cross_attention_and_quantised_linear(nc, g)
        linear_attention(nc, g)
        gated_convolution(nc, g)
        grouped_attention(nc, g)
        experts(nc, g)


def kernel(**inputs):
    from concourse import bacc
    from concourse.bass_utils import run_bass_kernel_spmd as run

    nc = bacc.Bacc("TRN2", target_bir_lowering=False, num_devices=1)
    arrays = {f"in_{name}": a for name, a in layouts(inputs).items()}
    h = {name[3:]: nc.dram_tensor(name, a.shape, mybir.dt.from_np(a.dtype), kind="ExternalInput").ap() for name, a in arrays.items()}
    out = nc.dram_tensor("out_0", (B, P, D), F32, kind="ExternalOutput").ap()
    decoder(nc, h, out)
    r = run(nc, [arrays], core_ids=[0])
    return r.results[0]["out_0"]
```
